# Optimizing a Trainium2 kernel written in Bass

```python
import numpy as np
import jax
import jax.numpy as jnp

def _softmax(x, axis=-1):
    return jax.nn.softmax(x, axis=axis)

def _gelu(x):
    return jax.nn.gelu(x, approximate=True)

def _silu(x):
    return jax.nn.silu(x)

def _sigmoid(x):
    return jax.nn.sigmoid(x)

def _layernorm(x, axis=-1, eps=1e-05):
    m = jnp.mean(x, axis=axis, keepdims=True)
    v = jnp.var(x, axis=axis, keepdims=True)
    return (x - m) / jnp.sqrt(v + eps)

def _scatter_add(tgt, idx, src, axis=0):
    return tgt.at[idx].add(src)

def _segment_sum(src, seg, n):
    return jax.ops.segment_sum(src, seg, n)
kernel_name = 'mk_gnn_preln_d2_gnn_r64_813fa7'

def setup_inputs(seed: int=0):
    np.random.seed(seed)
    _w = jnp.asarray

    def _rec_inputs():
        import jax
        import jax.numpy as jnp
        _gk = jax.random.key(seed)
        x = -0.0003713 + 1 * jax.random.normal(jax.random.fold_in(_gk, 1), (100000, 128), jnp.float32)
        src = jax.random.randint(jax.random.fold_in(_gk, 2), (50000,), 0, 100000, jnp.int32)
        dst = jax.random.randint(jax.random.fold_in(_gk, 3), (50000,), 0, 100000, jnp.int32)
        _o = jnp.argsort(dst, stable=True)
        src = src[_o]
        dst = dst[_o]
        edge_attr_16 = 0.000254156 + 0.999948 * jax.random.normal(jax.random.fold_in(_gk, 11), (50000, 16), jnp.float32)
        return (x, src, dst, edge_attr_16)
    x, src, dst, edge_attr_16 = _rec_inputs()

    def _L0_gnn_setup():
        import jax, jax.numpy as jnp
        import numpy as np
        NEG_SLOPE = 0.2
        EPS = 1e-16
        N_NODES = 100000
        N_EDGES = 25000
        CHANNELS = 128
        M_LAYERS = 3

        def _gat_conv(x, src, dst, W, a_src, a_dst, b, n_nodes):
            h = x @ W
            s = h @ a_src
            d = h @ a_dst
            e = s[src] + d[dst]
            e = jnp.where(e > 0, e, NEG_SLOPE * e)
            e_max = jax.ops.segment_max(e, dst, num_segments=n_nodes)
            e_max = jnp.where(jnp.isfinite(e_max), e_max, 0.0)
            w = jnp.exp(e - e_max[dst])
            denom = jax.ops.segment_sum(w, dst, num_segments=n_nodes)
            alpha = w / (denom[dst] + EPS)
            out = jax.ops.segment_sum(alpha[:, None] * h[src], dst, num_segments=n_nodes)
            return out + b
        key = jax.random.key(seed)
        k1, k2, k3, k4, k5 = jax.random.split(key, 5)
        x = jax.random.normal(k1, (N_NODES, CHANNELS), dtype=jnp.float32)
        edge_index = jax.random.randint(k2, (2, N_EDGES), 0, N_NODES, dtype=jnp.int64)
        Ws = jax.random.normal(k3, (M_LAYERS, CHANNELS, CHANNELS), dtype=jnp.float32) / np.sqrt(CHANNELS)
        att_src = jax.random.normal(k4, (M_LAYERS, CHANNELS), dtype=jnp.float32) / np.sqrt(CHANNELS)
        att_dst = jax.random.normal(k5, (M_LAYERS, CHANNELS), dtype=jnp.float32) / np.sqrt(CHANNELS)
        bias = jnp.zeros((M_LAYERS, CHANNELS), dtype=jnp.float32)
        return {'x': x, 'edge_index': edge_index, 'Ws': Ws, 'att_src': att_src, 'att_dst': att_dst, 'bias': bias}
    _L0_gnn_all = _L0_gnn_setup()
    _L0_gnn_in = {k: v for k, v in _L0_gnn_all.items() if k in ('Ws', 'att_src', 'att_dst', 'bias')}
    del _L0_gnn_all

    def _L1_gnn_setup():
        import jax, jax.numpy as jnp
        import numpy as np
        N, E, H, DE = (50000, 12500, 128, 16)
        BN_EPS = 1e-05

        def _bn_eval(h, g, b, rm, rv):
            return g * (h - rm) * jax.lax.rsqrt(rv + BN_EPS) + b

        def _gin_layer(x, ei, ea, p, concat):
            enc_w, enc_b, w1, b1, g, be, rm, rv, w2, b2 = p
            ee = ea @ enc_w + enc_b
            src = x[ei[1]]
            h = jnp.concatenate([src, ee], axis=1) if concat else src + ee
            agg = jax.ops.segment_sum(h, ei[0], num_segments=x.shape[0])
            h = agg @ w1 + b1
            h = jax.nn.relu(_bn_eval(h, g, be, rm, rv))
            return h @ w2 + b2
        key = jax.random.key(seed)
        ks = jax.random.split(key, 32)
        d = {'x': jax.random.normal(ks[0], (N, H), jnp.float32), 'edge_index': jax.random.randint(ks[1], (2, E), 0, N, jnp.int64 if jax.config.jax_enable_x64 else jnp.int32), 'edge_attr': jax.random.normal(ks[2], (E, DE), jnp.float32), 'self_loop_index': 0, 'self_loop_type': 1, 'enc_w0': jax.random.normal(ks[3], (DE, H), jnp.float32) * 0.1, 'enc_b0': jax.random.normal(ks[4], (H,), jnp.float32) * 0.1, 'w1_0': jax.random.normal(ks[5], (H, 2 * H), jnp.float32) * 0.05, 'b1_0': jax.random.normal(ks[6], (2 * H,), jnp.float32) * 0.05, 'g0': jax.random.normal(ks[7], (2 * H,), jnp.float32), 'be0': jax.random.normal(ks[8], (2 * H,), jnp.float32) * 0.1, 'rm0': jax.random.normal(ks[9], (2 * H,), jnp.float32) * 0.1, 'rv0': jax.random.uniform(ks[10], (2 * H,), jnp.float32, 0.5, 1.5), 'w2_0': jax.random.normal(ks[11], (2 * H, H), jnp.float32) * 0.05, 'b2_0': jax.random.normal(ks[12], (H,), jnp.float32) * 0.05, 'enc_w': jax.random.normal(ks[13], (2, DE, H), jnp.float32) * 0.1, 'enc_b': jax.random.normal(ks[14], (2, H), jnp.float32) * 0.1, 'w1': jax.random.normal(ks[15], (2, 2 * H, 2 * H), jnp.float32) * 0.05, 'b1': jax.random.normal(ks[16], (2, 2 * H), jnp.float32) * 0.05, 'g': jax.random.normal(ks[17], (2, 2 * H), jnp.float32), 'be': jax.random.normal(ks[18], (2, 2 * H), jnp.float32) * 0.1, 'rm': jax.random.normal(ks[19], (2, 2 * H), jnp.float32) * 0.1, 'rv': jax.random.uniform(ks[20], (2, 2 * H), jnp.float32, 0.5, 1.5), 'w2': jax.random.normal(ks[21], (2, 2 * H, H), jnp.float32) * 0.05, 'b2': jax.random.normal(ks[22], (2, H), jnp.float32) * 0.05}
        return d
    _L1_gnn_all = _L1_gnn_setup()
    _L1_gnn_in = {k: v for k, v in _L1_gnn_all.items() if k in ('enc_w0', 'enc_b0', 'w1_0', 'b1_0', 'g0', 'be0', 'rm0', 'rv0', 'w2_0', 'b2_0', 'enc_w', 'enc_b', 'w1', 'b1', 'g', 'be', 'rm', 'rv', 'w2', 'b2')}
    del _L1_gnn_all
    return {'x': x, 'src': src, 'dst': dst, 'edge_attr_16': edge_attr_16, 'L0_gnn_Ws': _L0_gnn_in['Ws'], 'L0_gnn_att_src': _L0_gnn_in['att_src'], 'L0_gnn_att_dst': _L0_gnn_in['att_dst'], 'L0_gnn_bias': _L0_gnn_in['bias'], 'L1_gnn_enc_w0': _L1_gnn_in['enc_w0'], 'L1_gnn_enc_b0': _L1_gnn_in['enc_b0'], 'L1_gnn_w1_0': _L1_gnn_in['w1_0'], 'L1_gnn_b1_0': _L1_gnn_in['b1_0'], 'L1_gnn_g0': _L1_gnn_in['g0'], 'L1_gnn_be0': _L1_gnn_in['be0'], 'L1_gnn_rm0': _L1_gnn_in['rm0'], 'L1_gnn_rv0': _L1_gnn_in['rv0'], 'L1_gnn_w2_0': _L1_gnn_in['w2_0'], 'L1_gnn_b2_0': _L1_gnn_in['b2_0'], 'L1_gnn_enc_w': _L1_gnn_in['enc_w'], 'L1_gnn_enc_b': _L1_gnn_in['enc_b'], 'L1_gnn_w1': _L1_gnn_in['w1'], 'L1_gnn_b1': _L1_gnn_in['b1'], 'L1_gnn_g': _L1_gnn_in['g'], 'L1_gnn_be': _L1_gnn_in['be'], 'L1_gnn_rm': _L1_gnn_in['rm'], 'L1_gnn_rv': _L1_gnn_in['rv'], 'L1_gnn_w2': _L1_gnn_in['w2'], 'L1_gnn_b2': _L1_gnn_in['b2']}

def reference(x, src, dst, edge_attr_16, L0_gnn_Ws, L0_gnn_att_src, L0_gnn_att_dst, L0_gnn_bias, L1_gnn_enc_w0, L1_gnn_enc_b0, L1_gnn_w1_0, L1_gnn_b1_0, L1_gnn_g0, L1_gnn_be0, L1_gnn_rm0, L1_gnn_rv0, L1_gnn_w2_0, L1_gnn_b2_0, L1_gnn_enc_w, L1_gnn_enc_b, L1_gnn_w1, L1_gnn_b1, L1_gnn_g, L1_gnn_be, L1_gnn_rm, L1_gnn_rv, L1_gnn_w2, L1_gnn_b2):
    import jax
    import jax.numpy as jnp

    def _L0_gnn_ref(x, edge_index, Ws, att_src, att_dst, bias):
        import jax, jax.numpy as jnp
        import numpy as np
        NEG_SLOPE = 0.2
        EPS = 1e-16
        N_NODES = 100000
        N_EDGES = 25000
        CHANNELS = 128
        M_LAYERS = 3

        def _gat_conv(x, src, dst, W, a_src, a_dst, b, n_nodes):
            h = x @ W
            s = h @ a_src
            d = h @ a_dst
            e = s[src] + d[dst]
            e = jnp.where(e > 0, e, NEG_SLOPE * e)
            e_max = jax.ops.segment_max(e, dst, num_segments=n_nodes)
            e_max = jnp.where(jnp.isfinite(e_max), e_max, 0.0)
            w = jnp.exp(e - e_max[dst])
            denom = jax.ops.segment_sum(w, dst, num_segments=n_nodes)
            alpha = w / (denom[dst] + EPS)
            out = jax.ops.segment_sum(alpha[:, None] * h[src], dst, num_segments=n_nodes)
            return out + b
        n = x.shape[0]
        loop = jnp.arange(n, dtype=edge_index.dtype)
        src = jnp.concatenate([edge_index[0], loop])
        dst = jnp.concatenate([edge_index[1], loop])
        for m in range(Ws.shape[0]):
            x = x + jax.nn.sigmoid(_gat_conv(x, src, dst, Ws[m], att_src[m], att_dst[m], bias[m], n))
        return x

    def _L1_gnn_ref(x, edge_index, edge_attr, self_loop_index, self_loop_type, enc_w0, enc_b0, w1_0, b1_0, g0, be0, rm0, rv0, w2_0, b2_0, enc_w, enc_b, w1, b1, g, be, rm, rv, w2, b2):
        import jax, jax.numpy as jnp
        import numpy as np
        N, E, H, DE = (50000, 12500, 128, 16)
        BN_EPS = 1e-05

        def _bn_eval(h, g, b, rm, rv):
            return g * (h - rm) * jax.lax.rsqrt(rv + BN_EPS) + b

        def _gin_layer(x, ei, ea, p, concat):
            enc_w, enc_b, w1, b1, g, be, rm, rv, w2, b2 = p
            ee = ea @ enc_w + enc_b
            src = x[ei[1]]
            h = jnp.concatenate([src, ee], axis=1) if concat else src + ee
            agg = jax.ops.segment_sum(h, ei[0], num_segments=x.shape[0])
            h = agg @ w1 + b1
            h = jax.nn.relu(_bn_eval(h, g, be, rm, rv))
            return h @ w2 + b2
        n = x.shape[0]
        loops = jnp.arange(n, dtype=edge_index.dtype)
        ei = jnp.concatenate([edge_index, jnp.stack([loops, loops])], axis=1)
        sl_attr = jnp.zeros((n, edge_attr.shape[1]), edge_attr.dtype)
        sl_attr = sl_attr.at[:, self_loop_index].set(jnp.asarray(self_loop_type, edge_attr.dtype))
        ea = jnp.concatenate([edge_attr, sl_attr], axis=0)
        p0 = (enc_w0, enc_b0, w1_0, b1_0, g0, be0, rm0, rv0, w2_0, b2_0)
        h = jax.nn.relu(_gin_layer(x, ei, ea, p0, concat=False))
        for i in range(2):
            pi = tuple((a[i] for a in (enc_w, enc_b, w1, b1, g, be, rm, rv, w2, b2)))
            h = _gin_layer(h, ei, ea, pi, concat=True)
            if i < 1:
                h = jax.nn.relu(h)
        return h
    edge_index = jnp.stack([src, dst])
    h = jnp.maximum(_layernorm(x, axis=-1), 0.0)
    x = x + _L0_gnn_ref(h, edge_index, L0_gnn_Ws, L0_gnn_att_src, L0_gnn_att_dst, L0_gnn_bias)
    h = jnp.maximum(_layernorm(x, axis=-1), 0.0)
    x = x + _L1_gnn_ref(h, edge_index, edge_attr_16, 0, 1, L1_gnn_enc_w0, L1_gnn_enc_b0, L1_gnn_w1_0, L1_gnn_b1_0, L1_gnn_g0, L1_gnn_be0, L1_gnn_rm0, L1_gnn_rv0, L1_gnn_w2_0, L1_gnn_b2_0, L1_gnn_enc_w, L1_gnn_enc_b, L1_gnn_w1, L1_gnn_b1, L1_gnn_g, L1_gnn_be, L1_gnn_rm, L1_gnn_rv, L1_gnn_w2, L1_gnn_b2)
    return x

_drawn_inputs = setup_inputs


def setup_inputs(seed=0):
    import zlib

    import numpy as np

    out = dict(_drawn_inputs(seed))
    spreads = {'L0_gnn_bias': (0.0, 0.536)}
    factors = {'L0_gnn_att_src': 16.738,
     'L0_gnn_att_dst': 200.0,
     'L1_gnn_enc_w0': 8.0,
     'L1_gnn_enc_b0': 8.0,
     'L1_gnn_w1_0': 5.524,
     'L1_gnn_b1_0': 44.921,
     'L1_gnn_g0': 5.715,
     'L1_gnn_be0': 43.669,
     'L1_gnn_rm0': 21.404,
     'L1_gnn_rv0': 8.0,
     'L1_gnn_w2_0': 5.063,
     'L1_gnn_b2_0': 200.0,
     'L1_gnn_enc_b': 9.778,
     'L1_gnn_b1': 13.559,
     'L1_gnn_rm': 9.057,
     'L1_gnn_rv': 7.385,
     'L1_gnn_b2': 2.9,
     'L1_gnn_enc_w': 4.408,
     'L1_gnn_be': 2.677}
    for name, (base, spread) in spreads.items():
        noise = np.random.default_rng([zlib.crc32(name.encode()), seed]).standard_normal(out[name].shape)
        drawn = base * np.exp(spread * noise) if base else spread * noise
        out[name] = jnp.asarray(drawn.astype(out[name].dtype))
    for name, factor in factors.items():
        out[name] = (out[name] * factor).astype(out[name].dtype)
    return out
```

```python
from contextlib import ExitStack

import concourse.bass as bass
from concourse import mybir

ALU = mybir.AluOpType
ACT = mybir.ActivationFunctionType
F32 = mybir.dt.float32
I32 = mybir.dt.int32

P = 128
J = 4
TN = P * J
U = 8
M = 3
BIG = 1e30
EPS_LN = 1e-5
EPS_BN = 1e-5
EPS_SM = 1e-16
SLOPE = 0.2
C = 128
H = 256
DE = 16
EA = DE + 1
CP = 132


def gnn_program(nc, x, src, dst, attr, Ws, a_src, a_dst, gat_b, enc_w0, enc_b0, w1_0, b1_0, g_0, be_0, rm_0,
                rv_0, w2_0, b2_0, enc_w, enc_b, w1, b1, g, be, rm, rv, w2, b2, out):
    N = x.shape[0]
    E = src.shape[0]
    NT = -(-N // TN)
    NT += -NT % 4
    LAST = N - TN
    R = -(-E // (P * U))
    ET = R * U
    ETP = ET + U
    NB_ = 4
    EB = ET // NB_
    NR = (NT + 1) * TN
    TRASH = NR - P
    SKIP = 2 * N
    assert EB * NB_ == ET and EB <= P and R >= 3 and NT >= 12

    def dram(name, shape):
        return nc.dram_tensor(name, shape, F32, kind="Internal").ap()

    h0_d = dram("h0_d", (N, C))
    x1_d = dram("x1_d", (N, C))
    x2_d = dram("x2_d", (N, C))
    yg_d = dram("yg_d", (N, 2 * C))
    g1_d = dram("g1_d", (N, C))
    g2_d = dram("g2_d", (N, C))
    AW = [C + EA, C, C]
    agg_d = [[dram(f"agg{m}{b}_d", (NR, AW[m])) for b in range(2)] for m in range(M)]
    eaT_d = dram("eaT_d", (NT, EA, TN))
    gat_in = [h0_d, x1_d, x2_d]
    gin_in = [yg_d.rearrange("n (t c) -> (n t) c", t=2), g1_d, g2_d]

    with ExitStack() as ctx:
        def sb(name, shape, dt=F32):
            return ctx.enter_context(nc.sbuf_tensor(name, shape, dt))

        def sem(name):
            return ctx.enter_context(nc.semaphore(name))

        def sems(name, n):
            return [sem(f"{name}{k}") for k in range(n)]

        ps = [ctx.enter_context(nc.psum_tensor(f"ps{k}", [P, 512], F32)) for k in range(8)]

        ident = sb("ident", [P, P])
        last_row = sb("last_row", [P, P])
        later = sb("later", [P, P])
        ones_row = sb("ones_row", [1, P])
        zeros = sb("zeros", [P, J * (C + EA)])
        mhalf = sb("mhalf", [P, U])
        eps_ln = sb("eps_ln", [P, 1])
        trash_id = sb("trash_id", [P, 1])
        self_ea = sb("self_ea", [P, J, EA])
        W = sb("W", [P, M, C])
        W1X = sb("W1X", [P, M, H])
        W1B = sb("W1B", [P, M, H])
        W2 = sb("W2", [P, M, 2, C])
        ENC = sb("ENC", [EA, M, C])
        ENCT = sb("ENCT", [P, M, EA])
        EP = sb("EP", [EA, M, H])
        BN = sb("BN", [P, 5, M, 2])
        BNS = sb("BNS", [P, M, 2])
        BNT = sb("BNT", [P, M, 2])
        B2 = sb("B2", [P, M, C])
        GBC = sb("GBC", [P, M])
        GBR = sb("GBR", [1, M, C])
        AR = sb("AR", [P, 2, M, C])
        VC = sb("VC", [P, 2 * M])
        VR = sb("VR", [P, 2 * M, C])

        rowI = sb("rowI", [EB, 3, NB_, P], I32)
        rowF = sb("rowF", [EB, 3, NB_, P])
        keys = sb("keys", [P, 3, ET])
        META = sb("META", [P, 3, ET])
        cnt = sb("cnt", [P, ET])
        tmp = sb("tmp", [P, 2, ET])
        IDX = sb("IDX", [P, 5, ETP], I32)

        s_w = sem("s_w")
        s_idx = sem("s_idx")
        s_pool = sem("s_pool")
        s_rowf, s_keys, s_enct, s_vc, s_setup, s_pe, s_dclr = [
            sem(n) for n in ["s_rowf", "s_keys", "s_enct", "s_vc", "s_setup", "s_pe", "s_dclr"]]
        s_v = sem("s_v")
        s_gate = sem("s_gate")
        s_cid = sem("s_cid")
        s_cnt = sem("s_cnt")
        n_idx = [0]

        weight_loads = [
            (W[:, :, :], Ws.rearrange("m k c -> k m c")),
            (W1X[:, 0, :], w1_0), (W1B[:, 0, :], w1_0),
            (W2[:, 0, :, :], w2_0.rearrange("(h k) c -> k h c", h=2)),
            (ENC[0:DE, 0, :], enc_w0), (ENC[DE:EA, 0, :], enc_b0.rearrange("(o c) -> o c", o=1)),
            (GBC[:, :], gat_b.rearrange("m c -> c m")), (GBR[:, :, :], gat_b.rearrange("(o m) c -> o m c", o=1)),
            (B2[:, 0, :], b2_0.rearrange("(o c) -> o c", o=1).to_broadcast([P, C])),
        ]
        for m in range(1, M):
            weight_loads += [
                (W1X[:, m, :], w1[m - 1, 0:C, :]), (W1B[:, m, :], w1[m - 1, C:2 * C, :]),
                (W2[:, m, :, :], w2[m - 1].rearrange("(h k) c -> k h c", h=2)),
                (ENC[0:DE, m, :], enc_w[m - 1]), (ENC[DE:EA, m, :], enc_b[m - 1:m, :]),
                (B2[:, m, :], b2[m - 1:m, :].to_broadcast([P, C])),
            ]
        for m in range(M):
            weight_loads += [(AR[:, 0, m, :], a_src[m:m + 1, :].to_broadcast([P, C])),
                             (AR[:, 1, m, :], a_dst[m:m + 1, :].to_broadcast([P, C]))]
            for q, (v0, v) in enumerate(((g_0, g), (be_0, be), (rm_0, rm), (rv_0, rv), (b1_0, b1))):
                vec = v0 if m == 0 else v[m - 1]
                weight_loads.append((BN[:, q, m, :], vec.rearrange("(h p) -> p h", p=P)))
        NW = len(weight_loads)

        block = ctx.enter_context(nc.Block())

        aX = sb("aX", [P, 4, J, C])
        aH = sb("aH", [P, 2, J, C])
        aT = sb("aT", [P, 2, 4, TN])
        aS = sb("aS", [P, 2, TN])
        aO = sb("aO", [P, 2, 2, J, C])
        aYG = sb("aYG", [P, 2, J, 2 * C])
        aBS = sb("aBS", [P, 2, 2, J, 6])
        aMV = sb("aMV", [P, 2, 2, J, 2])
        aRS = sb("aRS", [P, 2, 2, J])
        aNM = sb("aNM", [P, 2, 2, J])
        aVE = sb("aVE", [P, 2, 2, J])
        a_x = sems("a_x", 4)
        a_mv, a_rs, a_nm, a_h, a_tp, a_tc, a_mm, a_sg, a_xT, a_bk, a_o, a_y, a_g, a_pv, a_bs = [
            sem(n) for n in ["a_mv", "a_rs", "a_nm", "a_h", "a_tp", "a_tc", "a_mm", "a_sg", "a_xT", "a_bk", "a_o",
                             "a_y", "a_g", "a_pv", "a_bs"]]
        a_sh = sems("a_sh", 2)
        a_s1 = sems("a_s1", 2)
        a_s2 = sems("a_s2", 2)
        a_sy = sems("a_sy", 2)
        NA = NT // 2
        NQ = NT // 4

        bXs = sb("bXs", [P, U, CP])
        bXd = sb("bXd", [P, U, CP])
        bXx = sb("bXx", [P, U, C])
        bNE = sb("bNE", [P, U, P])
        bSW = sb("bSW", [P, U, P])
        bT0 = sb("bT0", [P, U, CP])
        bTL = sb("bTL", [P, U, CP])
        bT1 = sb("bT1", [P, U, CP])
        bTOT = sb("bTOT", [P, U, CP])
        bA = sb("bA", [P, U, C])
        bAT = sb("bAT", [P, U, C])
        bXP = sb("bXP", [P, U, C])
        bTH = sb("bTH", [P, U, C])
        bO = sb("bO", [P, U, 2 * C])
        bFM = sb("bFM", [P, 3, U])
        bGI = sb("bGI", [P, 2, U], I32)
        bOI = sb("bOI", [P, U], I32)
        bDT = sb("bDT", [P, 3, U])
        bNX = sb("bNX", [P, 2, U])
        bQ = sb("bQ", [P, 2, U])
        bNM = sb("bNM", [P, U])
        bPR = sb("bPR", [P, U, 2])
        bARG = sb("bARG", [P, 2, U])
        bWX = sb("bWX", [P, 2, U])
        bWS = sb("bWS", [P, U])
        bF = sb("bF", [P, U, 2])
        bRL = sb("bRL", [P, 2, U])
        bBS = sb("bBS", [P, U, 6])
        bMV = sb("bMV", [P, U, 2])
        bRS = sb("bRS", [P, 2, U])
        bNR = sb("bNR", [P, U])
        b_gs = sems("b_gs", U)
        b_gd = sems("b_gd", U)
        b_gx = sems("b_gx", U)
        b_sc = sems("b_sc", U)
        b_names = ["b_fm", "b_gi", "b_d", "b_ne", "b_q", "b_e", "b_eu", "b_arg", "b_wx", "b_ws", "b_sw", "b_t0",
                   "b_acc", "b_tl", "b_bc", "b_nm", "b_ft", "b_tot", "b_rl", "b_a", "b_at", "b_atc", "b_h",
                   "b_th", "b_out", "b_oi", "b_f", "b_mv", "b_rs", "b_nr"]
        (b_fm, b_gi, b_d, b_ne, b_q, b_e, b_eu, b_arg, b_wx, b_ws, b_sw, b_t0, b_acc, b_tl, b_bc, b_nm, b_ft,
         b_tot, b_rl, b_a, b_at, b_atc, b_h, b_th, b_out, b_oi, b_f, b_mv, b_rs, b_nr) = [sem(n) for n in b_names]
        s_zero = sem("s_zero")
        b_v = sem("b_v")
        b_per = [3 + U, 3 + U, 7 + U]
        b_base = [0, R * b_per[0], 2 * R * b_per[0]]
        s_cg = sem("s_cg")
        s_cw = sem("s_cw")
        e_a = sem("e_a")

        dG = bO
        dS = bNE
        dO = sb("dO", [P, U, C + EA])
        dK = sb("dK", [P, U])
        dGI = sb("dGI", [P, U], I32)
        dOI = sb("dOI", [P, U], I32)
        d_g = sems("d_g", U)
        d_a = sems("d_a", 2)
        d_at, d_k, d_gi, d_oi, d_t, d_s, d_acc, d_o = [
            sem(n) for n in ["d_at", "d_k", "d_gi", "d_oi", "d_t", "d_s", "d_acc", "d_o"]]

        eG = aX[:, 0:2, :, :]
        eY = aX[:, 2:4, :, :]
        eA = sb("eA", [P, 2, 2, J, C + EA])
        eS = aO[:, 0, :, :, :]
        eE = sb("eE", [P, 2, J, EA])
        eHT = aS
        eET = sb("eET", [EA, 2, TN])
        eZ = aT[:, 0, :, :].rearrange("p (k h) n -> p k h n", k=2)
        eO = aH
        e_in = sems("e_in", 2)
        e_et = sems("e_et", 2)
        e_st = sems("e_st", 2)
        e_se = sems("e_se", 2)
        e_yi = sems("e_yi", 2)
        e_s, e_tp, e_tc, e_z, e_zr, e_y, e_o, e_v = [
            sem(n) for n in ["e_s", "e_tp", "e_tc", "e_z", "e_zr", "e_y", "e_o", "e_v"]]

        def node_tile(t, buf):
            return buf[bass.ds(t * TN, TN), :].rearrange("(p j) c -> p j c", j=J)

        def last_tile(buf):
            return buf[LAST:N, :].rearrange("(p j) c -> p j c", j=J)

        @block.sync
        def _(sp):
            sp.wait_ge(s_pool, 1)
            full = E // P
            for k, (vec, off) in enumerate(((src, 0), (dst, 0), (dst, 1))):
                for b in range(NB_):
                    lo = b * EB
                    n = max(0, min(EB, (E - off) // P - lo))
                    if n:
                        sp.dma_start(rowI[0:n, k, b, :], vec[off + lo * P:off + (lo + n) * P]
                                     .rearrange("(t p) -> t p", p=P)).then_inc(s_idx, 16)
                        n_idx[0] += 1
                    rest = E - off - (lo + n) * P
                    if 0 <= n < EB and 0 < rest < P:
                        sp.dma_start(rowI[n:n + 1, k, b, 0:rest],
                                     vec[off + (lo + n) * P:E].rearrange("(t p) -> t p", t=1)).then_inc(s_idx, 16)
                        n_idx[0] += 1

            def tile_of(t):
                if isinstance(t, int) and (t + 1) * TN > N:
                    return last_tile
                return lambda buf: node_tile(t, buf)

            def stores_before(stores, p, k):
                if isinstance(p, int) and 2 * p + k >= N // TN:
                    for s in stores:
                        for kk in range(2):
                            sp.wait_ge(s[kk], 16 * (p + 1 + (kk < k)))

            def a_pair(p, q, more):
                for k in range(2):
                    stores_before((a_sh, a_s1, a_s2), p, k)
                    pick = tile_of(2 * p + k)
                    sp.wait_ge(a_h, 2 * J * p + J * (k + 1))
                    sp.dma_start(pick(h0_d), aH[:, k, :, :]).then_inc(a_sh[k], 16)
                    for m, (o, s) in enumerate(((x1_d, a_s1), (x2_d, a_s2))):
                        sp.wait_ge(a_o, 4 * p + 2 * m + k + 1)
                        sp.dma_start(pick(o), aO[:, k, m, :, :]).then_inc(s[k], 16)
                for k in range(2):
                    pick = tile_of(2 * p + k)
                    sp.wait_ge(a_y, 2 * p + k + 1)
                    if more:
                        sp.dma_start(aX[:, 2 * q + k, :, :], tile_of(2 * p + 4 + k)(x)).then_inc(a_x[2 * q + k], 16)
                    sp.wait_ge(a_g, 2 * J * p + J * (k + 1))
                    stores_before((a_sy,), p, k)
                    sp.dma_start(pick(yg_d), aYG[:, k, :, :]).then_inc(a_sy[k], 16)

            for t in range(4):
                sp.dma_start(aX[:, t, :, :], node_tile(t, x)).then_inc(a_x[t], 16)
            with sp.Fori(0, NQ - 2) as i:
                for q in range(2):
                    a_pair(2 * i + q, q, True)
            for p in range(NA - 4, NA):
                a_pair(p, p % 2, p < NA - 2)

            for m in range(M):
                for b in range(2):
                    agg = agg_d[m][b]
                    n = J * AW[m]
                    sp.wait_ge(b_fm, m * R + 1)
                    with sp.Fori(0, NT + 1) as i:
                        sp.dma_start(agg[bass.ds(i * TN, TN), :].rearrange("(p j) c -> p (j c)", j=J),
                                     zeros[:, 0:n]).then_inc(s_zero, 16)

            def attrs(r, t0):
                for u in range(U):
                    left = E - (t0 + u) * P
                    if left > 0:
                        k = min(P, left)
                        sp.dma_start(dG[0:k, u, C:C + DE], attr[(t0 + u) * P:(t0 + u) * P + k, :]).then_inc(d_at, 16)
                    else:
                        sp.sem_inc(d_at, 16)

            def attr_round(r):
                sp.dma_start(dG[:, :, C:C + DE],
                             attr[bass.ds(r * (U * P), U * P), :].rearrange("(u p) c -> p u c", p=P)
                             ).then_inc(d_at, 16 * U)

            sp.wait_ge(s_dclr, 1)
            attr_round(0)
            with sp.Fori(1, R - 1) as i:
                sp.wait_ge(d_acc, U * i)
                attr_round(i)
            sp.wait_ge(d_acc, U * (R - 1))
            sp.wait_ge(d_at, 16 * U * (R - 1))
            attrs(R - 1, (R - 1) * U)

            for m in range(M):
                n0 = m * NT
                into = [g1_d, g2_d, out][m]

                def load_rows(k, t, m=m):
                    pick = tile_of(t)
                    own = pick(yg_d)[:, :, C:2 * C] if m == 0 else pick([None, g1_d, g2_d][m])
                    sp.dma_start(eG[:, k, :, :], own).then_inc(e_in[k], 16)
                    for b in range(2):
                        sp.dma_start(eA[:, k, b, :, 0:AW[m]], pick(agg_d[m][b])).then_inc(e_in[k], 16)

                def load_ea(k, t):
                    sp.dma_start(eET[:, k, :], eaT_d[bass.ds(t, 1), :, :].rearrange("o r n -> (o r) n")
                                 ).then_inc(e_et[k], 16)

                def load_y(k, t):
                    sp.dma_start(eY[:, k, :, :], tile_of(t)(yg_d)[:, :, 0:C]).then_inc(e_yi[k], 16)

                def e_pair(p, more, m=m, n0=n0, into=into):
                    for k in range(2):
                        if m == 0:
                            sp.wait_ge(e_tc, 4 * p + 2 * (k + 1))
                            sp.dma_start(eaT_d[bass.ds(2 * p + k, 1), :, :].rearrange("o r n -> (o r) n"),
                                         eET[:, k, :]).then_inc(e_se[k], 16)
                        if more:
                            sp.wait_ge(e_s, n0 + 2 * p + k + 1)
                            load_rows(k, 2 * p + 2 + k)
                    if more and m:
                        for k in range(2):
                            sp.wait_ge(e_z, 2 * (n0 + 2 * p + k + 1))
                            load_ea(k, 2 * p + 2 + k)
                    for k in range(2):
                        if isinstance(p, int) and 2 * p + k >= N // TN:
                            for kk in range(2):
                                sp.wait_ge(e_st[kk], 16 * (m * NA + p + 1 + (kk < k)))
                        sp.wait_ge(e_o, n0 + 2 * p + k + 1)
                        sp.dma_start(tile_of(2 * p + k)(into), eO[:, k, :, :]).then_inc(e_st[k], 16)
                        if more and m == M - 1:
                            load_y(k, 2 * p + 2 + k)

                for b in range(2):
                    sp.wait_ge(d_a[b], 16 * (U // 2) * R * (m + 1))
                if m == 0:
                    sp.wait_ge(s_zero, 16 * 2 * M * (NT + 1))
                else:
                    for k in range(2):
                        sp.wait_ge(e_st[k], 16 * (NA * m + 1))
                        sp.wait_ge(e_se[k], 16 * (NA + 1))
                for k in range(2):
                    load_rows(k, k)
                    if m:
                        load_ea(k, k)
                    if m == M - 1:
                        load_y(k, k)
                with sp.Fori(0, NA - 4) as i:
                    e_pair(i, True)
                for p in range(NA - 4, NA):
                    e_pair(p, p < NA - 1)
            for k in range(2):
                sp.wait_ge(e_st[k], 16 * (NA * M + 1))

        @block.gpsimd
        def _(pool):
            pool.memset(rowI[:, 0:2, :, :], -1)
            pool.memset(rowI[:, 2, :, :], -2)
            pool.memset(ident[:, :], 0.0)
            pool.memset(last_row[:, :], 0.0)
            pool.memset(later[:, :], 1.0)
            pool.memset(ones_row[:, :], 1.0)
            pool.memset(zeros[:, :], 0.0)
            pool.memset(mhalf[:, :], -0.5)
            pool.memset(eps_ln[:, :], EPS_LN)
            pool.memset(self_ea[:, :, :], 0.0)
            pool.memset(bXs[:, :, C:CP], 1.0)
            pool.memset(bXd[:, :, C:CP], 1.0)
            pool.memset(bTOT[:, :, :], 0.0)
            pool.memset(IDX[:, :, :], 0).then_inc(s_pool, 1)
            for s in a_sh + a_s1 + a_s2 + a_sy + e_se + e_st:
                pool.sem_inc(s, 16)
            pool.wait_ge(s_pool, 1)
            pool.memset(self_ea[:, :, 0:1], 1.0)
            pool.memset(self_ea[:, :, DE:EA], 1.0)
            pool.affine_select(out=ident[:, :], in_=ident[:, :], compare_op=ALU.not_equal, fill=1.0, base=0,
                               pattern=[[-1, P]], channel_multiplier=1)
            pool.affine_select(out=last_row[:, :], in_=last_row[:, :], compare_op=ALU.not_equal, fill=1.0,
                               base=-(P - 1), pattern=[[0, P]], channel_multiplier=1)
            pool.affine_select(out=later[:, :], in_=later[:, :], compare_op=ALU.is_gt, fill=0.0, base=0,
                               pattern=[[1, P]], channel_multiplier=-1)
            pool.iota(trash_id[:, :], pattern=[[0, 1]], base=TRASH, channel_multiplier=1,
                      allow_small_or_imprecise_dtypes=True).then_inc(s_pool, 1)

            pool.wait_ge(s_w, 16 * NW)
            pool.tensor_scalar(BNS[:, :, :], BN[:, 3, :, :], EPS_BN, None, ALU.add).then_inc(s_pool, 1)
            pool.wait_ge(s_pool, 3)
            pool.tensor_tensor(BNT[:, :, :], BNS[:, :, :], mhalf[:, 0:2 * M].rearrange("p (m h) -> p m h", h=2),
                               ALU.pow).then_inc(s_pool, 1)

            def a_rstd(n, k, w):
                pool.wait_ge(a_mv, n)
                pool.sem_inc(s_gate, 1)
                pool.tensor_scalar(aVE[:, k, w, :], aMV[:, k, w, :, 1], EPS_LN, None, ALU.add).then_inc(a_pv, 1)
                pool.wait_ge(a_pv, n)
                pool.tensor_tensor(aRS[:, k, w, :], aVE[:, k, w, :], mhalf[:, 0:J], ALU.pow).then_inc(a_rs, 1)

            def a_pair(p, more):
                if more:
                    for k in range(2):
                        a_rstd(2 + 4 * p + k + 1, k, 0)
                for k in range(2):
                    a_rstd(2 + 4 * p + 2 * more + k + 1, k, 1)

            for k in range(2):
                a_rstd(k + 1, k, 0)
            with pool.Fori(0, NQ - 1) as i:
                for q in range(2):
                    a_pair(2 * i + q, 1)
            a_pair(NA - 2, 1)
            a_pair(NA - 1, 0)

            n_last = pool.to_reg(N - 1)
            for s in (a_sh, a_s1, a_s2, a_sy):
                for k in range(2):
                    pool.wait_ge(s[k], 16 * (NA + 1))
            for m in range(M):
                r0 = m * R

                def b_gather(r, m=m):
                    pool.wait_ge(b_gi, r + m + 1)
                    for u in range(U):
                        if not isinstance(r, int) or r > 0:
                            pool.wait_ge(b_acc, U * (r - 1) + u + 1)
                        pool.sem_inc(s_gate, 1)
                        pool.indirect_dma_start(bXs[:, u, 0:C], None, gat_in[m],
                                                bass.IndirectOffsetOnAxis(ap=bGI[:, 0, u:u + 1], axis=0),
                                                bounds_check=n_last, oob_is_err=False).then_inc(b_gs[u], 16)
                        if not isinstance(r, int) or r > 0:
                            pool.wait_ge(b_t0, U * (r - 1) + u + 1)
                        pool.sem_inc(s_gate, 1)
                        pool.indirect_dma_start(bXd[:, u, 0:C], None, gat_in[m],
                                                bass.IndirectOffsetOnAxis(ap=bGI[:, 1, u:u + 1], axis=0),
                                                bounds_check=n_last, oob_is_err=False).then_inc(b_gd[u], 16)
                        if m == M - 1:
                            if not isinstance(r, int) or r > r0:
                                pool.wait_ge(b_mv, U * (r - r0 - 1) + u + 1)
                            pool.sem_inc(s_gate, 1)
                            pool.indirect_dma_start(bXx[:, u, :], None, x,
                                                    bass.IndirectOffsetOnAxis(ap=bGI[:, 1, u:u + 1], axis=0),
                                                    bounds_check=n_last, oob_is_err=False).then_inc(b_gx[u], 16)

                def b_scatter(r, m=m):
                    for u in range(U):
                        pool.wait_ge(b_out, U * r + u + 1)
                        pool.wait_ge(b_oi, r + 1)
                        pool.sem_inc(s_gate, 1)
                        dest, wid = [(x1_d, C), (x2_d, C), (yg_d, 2 * C)][m]
                        pool.indirect_dma_start(dest, bass.IndirectOffsetOnAxis(ap=bOI[:, u:u + 1], axis=0),
                                                bO[:, u, 0:wid], None, bounds_check=n_last,
                                                oob_is_err=False).then_inc(b_sc[u], 16)

                b_gather(r0)
                with pool.Fori(1, R) as i:
                    b_gather(r0 + i)
                    b_scatter(r0 + i - 1)
                b_scatter(r0 + R - 1)
                for u in range(U):
                    pool.wait_ge(b_sc[u], 16 * (r0 + R))

            lim2 = pool.to_reg(2 * N - 1)
            agg_last = pool.to_reg(NR - 1)
            pool.wait_ge(s_zero, 16 * 2 * M * (NT + 1))
            for m in range(M):
                r0 = m * R
                if m:
                    for k in range(2):
                        pool.wait_ge(e_st[k], 16 * (NA * m + 1))

                def d_gather(r, m=m):
                    pool.wait_ge(d_gi, r + m + 1)
                    for u in range(U):
                        if not isinstance(r, int) or r > 0:
                            pool.wait_ge(d_acc, U * (r - 1) + u + 1)
                        pool.sem_inc(s_gate, 1)
                        pool.indirect_dma_start(dG[:, u, 0:C], None, gin_in[m],
                                                bass.IndirectOffsetOnAxis(ap=dGI[:, u:u + 1], axis=0),
                                                bounds_check=lim2 if m == 0 else n_last,
                                                oob_is_err=False).then_inc(d_g[u], 16)

                def d_add(r, m=m):
                    pool.wait_ge(d_oi, r + 1)
                    for u in range(U):
                        pool.wait_ge(d_o, U * r + u + 1)
                        if not isinstance(r, int) or U * r + u >= 2:
                            pool.wait_ge(d_a[u % 2], 16 * ((U // 2) * r + u // 2))
                        pool.sem_inc(s_gate, 1)
                        pool.indirect_dma_start(agg_d[m][u % 2],
                                                bass.IndirectOffsetOnAxis(ap=dOI[:, u:u + 1], axis=0),
                                                dO[:, u, 0:AW[m]], None, bounds_check=agg_last,
                                                oob_is_err=True, compute_op=ALU.add).then_inc(d_a[u % 2], 16)

                d_gather(r0)
                if m == 0:
                    d_gather(1)
                    d_add(0)
                with pool.Fori(2 if m == 0 else 1, R) as i:
                    d_gather(r0 + i)
                    d_add(r0 + i - 1)
                d_add(r0 + R - 1)

        @block.scalar
        def _(act):
            with nc.allow_non_contiguous_dma(reason="a few short vectors as columns"):
                for to, of in weight_loads:
                    act.dma_start(to, of).then_inc(s_w, 16)

            act.wait_ge(s_setup, 1)
            def a_before(p, q, c):
                for k in range(2):
                    act.wait_ge(a_nm, c + k + 1)
                    act.wait_ge(a_sh[k], 16 * (p + 1))
                    for j in range(J):
                        act.activation(aH[:, k, j, :], aX[:, 2 * q + k, j, :], ACT.Relu, bias=aNM[:, k, 0, j:j + 1],
                                       scale=aRS[:, k, 0, j:j + 1]).then_inc(a_h, 1)
                for k in range(2):
                    act.wait_ge(a_tp, 2 * p + k + 1)
                    act.copy(aT[:, k, 0, :], ps[k][:, :]).then_inc(a_tc, 1)

            def a_pair(p, q, more):
                for m in range(M):
                    for k in range(2):
                        act.wait_ge(a_mm, 2 * M * p + 2 * m + k + 1)
                        act.activation(aS[:, k, :], ps[2 + k][:, :], ACT.Sigmoid,
                                       bias=GBC[:, m:m + 1]).then_inc(a_sg, 1)
                    if m < M - 1:
                        for k in range(2):
                            act.wait_ge(a_bk, 2 * M * p + 2 * m + k + 1)
                            act.wait_ge([a_s1, a_s2][m][k], 16 * (p + 1))
                            act.copy(aO[:, k, m, :, :], ps[4 + k][:, :].rearrange("p (j c) -> p j c", j=J)
                                     ).then_inc(a_o, 1)
                if more:
                    a_before(p + 1, 1 - q, 2 + 4 * p)
                for k in range(2):
                    act.wait_ge(a_nm, 2 + 4 * p + 2 * more + k + 1)
                    for j in range(J):
                        act.activation(aYG[:, k, j, C:2 * C], aYG[:, k, j, 0:C], ACT.Relu,
                                       bias=aNM[:, k, 1, j:j + 1], scale=aRS[:, k, 1, j:j + 1]).then_inc(a_g, 1)

            a_before(0, 0, 0)
            with act.Fori(0, NQ - 1) as i:
                for q in range(2):
                    a_pair(2 * i + q, q, 1)
            a_pair(NA - 2, 0, 1)
            a_pair(NA - 1, 1, 0)

            for m in range(M):
                with act.Fori(0, R) as i:
                    r = m * R + i
                    act.wait_ge(b_arg, r + 1)
                    act.activation(bWX[:, :, :], bARG[:, :, :], ACT.Exp).then_inc(b_wx, 1)
                    act.wait_ge(b_ws, r + 1)
                    for u in range(U):
                        act.activation(bXP[:, u, :], bXd[:, u, 0:C], ACT.Copy, bias=0.5)
                        act.activation(bT0[:, u, 0:C + 1], bXd[:, u, 0:C + 1], ACT.Copy,
                                       scale=bWS[:, u:u + 1]).then_inc(b_t0, 1)
                    for u in range(U):
                        n = U * r + u + 1
                        act.wait_ge(b_nm, n)
                        act.activation(bF[:, u, :], bPR[:, u, :], ACT.Exp, bias=bTOT[:, u, C + 1:C + 2],
                                       scale=-1.0).then_inc(b_f, 1)
                        act.wait_ge(b_tl, n)
                        act.wait_ge(b_f, n)
                        act.activation(bT1[:, u, 0:C + 1], bTL[:, u, 0:C + 1], ACT.Copy,
                                       scale=bF[:, u, 0:1]).then_inc(b_ft, 1)
                    act.wait_ge(b_rl, r + 1)
                    for u in range(U):
                        act.activation(bA[:, u, :], bTOT[:, u, 0:C], ACT.Copy,
                                       scale=bRL[:, 1, u:u + 1]).then_inc(b_a, 1)
                    for u in range(U):
                        if u % 4 == 0:
                            act.wait_ge(b_at, U * r + u + 4)
                        act.copy(bAT[:, u, :], ps[u // 4][:, (u % 4) * P:(u % 4 + 1) * P]).then_inc(b_atc, 1)
                    for u in range(U):
                        if u % 4 == 0:
                            act.wait_ge(b_h, U * r + u + 4)
                        act.activation(bTH[:, u, :], ps[2 + u // 4][:, (u % 4) * P:(u % 4 + 1) * P], ACT.Tanh,
                                       scale=0.5).then_inc(b_th, 1)
                    if m == M - 1:
                        act.wait_ge(b_mv, U * (i + 1))
                        act.activation(bRS[:, 0, :], bMV[:, :, 1], ACT.Sqrt, bias=eps_ln[:, :]).then_inc(b_rs, 1)
                        act.wait_ge(b_nr, i + 1)
                        for u in range(U):
                            act.activation(bO[:, u, C:2 * C], bO[:, u, 0:C], ACT.Relu, bias=bNR[:, u:u + 1],
                                           scale=bRS[:, 1, u:u + 1]).then_inc(b_out, 1)

            for m in range(M):
                def d_round(r, m=m):
                    for u in range(U):
                        act.wait_ge(d_acc, U * r + u + 1)
                        if not isinstance(r, int) or r > 0:
                            act.wait_ge(d_a[u % 2], 16 * ((U // 2) * (r - 1) + u // 2 + 1))
                        act.copy(dO[:, u, 0:AW[m]], ps[2 + u % 4][:, 0:AW[m]]).then_inc(d_o, 1)

                if m == 0:
                    d_round(0)
                with act.Fori(1 if m == 0 else 0, R) as i:
                    d_round(m * R + i)

                n0 = m * NT

                def turned(p, m=m, n0=n0):
                    for k in range(2):
                        act.wait_ge(e_tp, n0 + 2 * p + k + 1)
                        if m == 0:
                            act.wait_ge(e_se[k], 16 * (p + 1))
                            act.copy(eET[:, k, :], ps[6 + k][0:EA, :]).then_inc(e_tc, 1)
                        act.copy(eHT[:, k, :], ps[k][:, :]).then_inc(e_tc, 1)

                def e_pair(p, more, m=m, n0=n0):
                    for k in range(2):
                        for h in range(2):
                            act.wait_ge(e_z, 2 * (n0 + 2 * p + k) + h + 1)
                            act.activation(eZ[:, k, h, :], ps[2 + 2 * k + h][:, :], ACT.Relu,
                                           bias=BNT[:, m, h:h + 1], scale=BNS[:, m, h:h + 1]).then_inc(e_zr, 1)
                    if more:
                        turned(p + 1)
                    if m < M - 1:
                        for k in range(2):
                            act.wait_ge(e_v, n0 + 2 * p + k + 1)
                            act.activation(eO[:, k, :, :], eO[:, k, :, :], ACT.Relu).then_inc(e_o, 1)

                turned(0)
                with act.Fori(0, NA - 1) as i:
                    e_pair(i, True)
                e_pair(NA - 1, False)

        @block.tensor
        def _(pe):
            def cols(b, u):
                return ps[b][:, u * P:(u + 1) * P]

            pe.wait_ge(s_pool, 2)
            pe.wait_ge(s_rowf, 1)
            for k in range(3):
                for b in range(NB_):
                    mm = pe.transpose(ps[k][:, b * EB:(b + 1) * EB], rowF[:, k, b, :], ident[0:EB, 0:EB])
                mm.then_inc(s_pe, 1)
            pe.wait_ge(s_keys, 1)
            pe.matmul(ps[3][:, 0:ET], last_row[:, :], keys[:, 1, :], start=True, stop=True).then_inc(s_pe, 1)
            pe.wait_ge(s_w, 16 * NW)
            for m in range(M):
                mm = pe.transpose(ps[4][:, m * EA:(m + 1) * EA], ENC[:, m, :], ident[0:EA, 0:EA])
            mm.then_inc(s_pe, 1)
            pe.wait_ge(s_enct, 1)
            for m in range(M):
                mm = pe.matmul(ps[5 + m][0:EA, 0:H], ENCT[:, m, :], W1B[:, m, :], start=True, stop=True)
            mm.then_inc(s_pe, 1)
            pe.wait_ge(s_vc, 1)
            for q in range(2 * M):
                mm = pe.transpose(ps[q // 4][:, (q % 4) * P:(q % 4 + 1) * P], VC[:, q:q + 1].to_broadcast([P, P]),
                                  ident[:, :])
            mm.then_inc(s_pe, 1)
            with pe.Fori(0, R) as i:
                pe.wait_ge(s_cid, i + 1)
                for u in range(U):
                    b = 2 + u // 4
                    pe.transpose(cols(b, u % 4), dK[:, u:u + 1].to_broadcast([P, P]), ident[:, :]).then_inc(s_cnt, 1)

            pe.wait_ge(s_setup, 1)
            def a_turn(p):
                for k in range(2):
                    pe.wait_ge(a_h, J * (2 * p + k + 1))
                    for j in range(J):
                        mm = pe.transpose(ps[k][:, j * P:(j + 1) * P], aH[:, k, j, :], ident[:, :])
                    mm.then_inc(a_tp, 1)

            def a_pair(p, more):
                for m in range(M):
                    for k in range(2):
                        if m == 0:
                            pe.wait_ge(a_tc, 2 * p + k + 1)
                        else:
                            pe.wait_ge(a_xT, 2 * M * p + 2 * (m - 1) + k + 1)
                        pe.matmul(ps[2 + k][:, :], W[:, m, :], aT[:, k, m, :], start=True, stop=True
                                  ).then_inc(a_mm, 1)
                    for k in range(2):
                        pe.wait_ge(a_xT, 2 * M * p + 2 * m + k + 1)
                        if m:
                            pe.wait_ge(a_o, 4 * p + 2 * (m - 1) + k + 1)
                        for j in range(J):
                            mm = pe.transpose(ps[4 + k][:, j * P:(j + 1) * P],
                                              aT[:, k, m + 1, j * P:(j + 1) * P], ident[:, :])
                        mm.then_inc(a_bk, 1)
                if more:
                    a_turn(p + 1)

            a_turn(0)
            with pe.Fori(0, NA - 1) as i:
                a_pair(i, 1)
            a_pair(NA - 1, 0)

            for m in range(M):
                with pe.Fori(0, R) as i:
                    r = m * R + i
                    pe.wait_ge(b_fm, r + 1)
                    for u in range(U):
                        pe.transpose(cols(u // 4, u % 4), bFM[:, 0, u:u + 1].to_broadcast([P, P]), ident[:, :]
                                     ).then_inc(b_d, 1)
                    pe.wait_ge(b_q, r + 1)
                    for u in range(U):
                        pe.transpose(cols(2 + u // 4, u % 4), bQ[:, 0, u:u + 1].to_broadcast([P, P]), ident[:, :]
                                     ).then_inc(b_e, 1)
                    for u in range(U):
                        pe.wait_ge(b_sw, U * r + u + 1)
                        if u >= 3:
                            pe.wait_ge(b_tl, U * r + u - 2)
                        pe.matmul(ps[4 + u % 3][:, 0:C + 1], bSW[:, u, :], bXs[:, u, 0:C + 1],
                                  start=True, stop=True).then_inc(b_acc, 1)
                    for u in range(U):
                        pe.wait_ge(b_tot, U * r + u + 1)
                        pe.matmul(ps[7][:, 0:C + 2], last_row[:, :],
                                  bTOT[:, (u - 1) % U, 0:C + 2], start=True, stop=True).then_inc(b_bc, 1)
                    for u in range(U):
                        pe.wait_ge(b_a, U * r + u + 1)
                        pe.transpose(cols(u // 4, u % 4), bA[:, u, :], ident[:, :]).then_inc(b_at, 1)
                    for u in range(U):
                        pe.wait_ge(b_atc, U * r + u + 1)
                        pe.matmul(cols(2 + u // 4, u % 4), ones_row[:, :], GBR[:, m, :], start=True, stop=False)
                        pe.matmul(cols(2 + u // 4, u % 4), bAT[:, u, :], W[:, m, :], start=False, stop=True
                                  ).then_inc(b_h, 1)

            for m in range(M):
                def d_round(i, m=m):
                    r = m * R + i
                    pe.wait_ge(d_k, r + 1)
                    for u in range(U):
                        pe.transpose(cols(u // 4, u % 4), dK[:, u:u + 1].to_broadcast([P, P]), ident[:, :]
                                     ).then_inc(d_t, 1)
                    for u in range(U):
                        pe.wait_ge(d_g[u], 16 * (r + 1))
                        if m == 0 and u == 0:
                            pe.wait_ge(d_at, 16 * U * (i + 1))
                        pe.wait_ge(d_s, U * r + u + 1)
                        if not isinstance(r, int) or U * r + u >= 4:
                            pe.wait_ge(d_o, U * r + u - 3)
                        pe.matmul(ps[2 + u % 4][:, 0:AW[m]], dS[:, u, :], dG[:, u, 0:AW[m]], start=True, stop=True
                                  ).then_inc(d_acc, 1)

                if m == 0:
                    d_round(0)
                with pe.Fori(1 if m == 0 else 0, R) as i:
                    d_round(i)
                n0 = m * NT
                tc = 2 if m == 0 else 1
                tc0 = 0 if m == 0 else NT

                def turn(p, m=m, n0=n0):
                    for k in range(2):
                        pe.wait_ge(e_s, n0 + 2 * p + k + 1)
                        if m == 0:
                            for j in range(J):
                                pe.transpose(ps[6 + k][0:EA, j * P:(j + 1) * P], eE[:, k, j, :], ident[:, :])
                        for j in range(J):
                            mm = pe.transpose(ps[k][:, j * P:(j + 1) * P], eS[:, k, j, :], ident[:, :])
                        mm.then_inc(e_tp, 1)

                def e_pair(p, more, m=m, n0=n0, tc=tc, tc0=tc0):
                    for k in range(2):
                        pe.wait_ge(e_tc, tc0 + tc * (n0 + 2 * p + k + 1))
                        if m:
                            pe.wait_ge(e_et[k], 16 * ((m - 1) * NA + p + 1))
                        for h in range(2):
                            z = ps[2 + 2 * k + h][:, :]
                            pe.matmul(z, W1X[:, m, h * P:(h + 1) * P], eHT[:, k, :], start=True, stop=False)
                            pe.matmul(z, EP[:, m, h * P:(h + 1) * P], eET[:, k, :], start=False, stop=True
                                      ).then_inc(e_z, 1)
                    if more:
                        turn(p + 1)
                    for k in range(2):
                        pe.wait_ge(e_zr, 2 * (n0 + 2 * p + k + 1))
                        if not more:
                            pe.wait_ge(e_v, n0 + 2 * p + k - 1)
                        if m == 0 and more:
                            pe.wait_ge(e_tc, 2 * (2 * p + 2 + k + 1))
                        for j in range(J):
                            for h in range(2):
                                mm = pe.matmul(ps[6 + k][:, j * P:(j + 1) * P], eZ[:, k, h, j * P:(j + 1) * P],
                                               W2[:, m, h, :], start=(h == 0), stop=(h == 1))
                        mm.then_inc(e_y, 1)

                turn(0)
                with pe.Fori(0, NA - 1) as i:
                    e_pair(i, 1)
                e_pair(NA - 1, 0)

        @block.vector
        def _(v):
            done = [0]

            def link(ins):
                done[0] += 1
                ins.then_inc(s_v, 1)
                v.wait_ge(s_v, done[0])

            v.wait_ge(s_idx, 16 * n_idx[0])
            v.tensor_copy(rowF[:, :, :, :], rowI[:, :, :, :]).then_inc(s_rowf, 1)
            v.wait_ge(s_pe, 3)
            for k in range(3):
                ins = v.tensor_copy(keys[:, k, :], ps[k][:, 0:ET])
            ins.then_inc(s_keys, 1)
            v.wait_ge(s_keys, 1)
            v.wait_ge(s_pool, 2)
            v.tensor_copy(META[:, 0, :], keys[:, 1, :])
            v.memset(META[:, 2, 0:1], 1.0)
            v.tensor_scalar(IDX[:, 0, 0:ET], keys[:, 0, :], 0.0, None, ALU.max)
            v.tensor_scalar(IDX[:, 1, 0:ET], keys[:, 1, :], 0.0, None, ALU.max)
            v.tensor_scalar(tmp[:, 0, :], keys[:, 1, :], 0.0, 2.0, ALU.max, ALU.mult)
            link(v.tensor_tensor(tmp[:, 1, :], keys[:, 1, :], keys[:, 2, :], ALU.not_equal))
            v.tensor_scalar(IDX[:, 2, 0:ET], tmp[:, 0, :], 1.0, None, ALU.add)
            link(v.scalar_tensor_tensor(out=cnt[:, :], in0=keys[:, 1, :], scalar=0.0, in1=tmp[:, 1, :],
                                        op0=ALU.is_ge, op1=ALU.mult))
            link(v.scalar_tensor_tensor(out=tmp[:, 0, :], in0=keys[:, 1, :], scalar=-float(SKIP), in1=cnt[:, :],
                                        op0=ALU.add, op1=ALU.mult))
            v.tensor_scalar(IDX[:, 3, 0:ET], tmp[:, 0, :], float(SKIP), None, ALU.add)
            v.wait_ge(s_pe, 4)
            link(v.tensor_tensor(META[:, 2, 1:ET], keys[:, 1, 1:ET], ps[3][:, 0:ET - 1], ALU.not_equal))
            v.tensor_scalar(META[:, 1, :], META[:, 2, :], BIG, None, ALU.mult)

            v.wait_ge(s_w, 16 * NW)
            v.wait_ge(s_pe, 5)
            v.tensor_copy(ENCT[:, :, :], ps[4][:, 0:M * EA].rearrange("p (m a) -> p m a", m=M)).then_inc(s_enct, 1)
            for m in range(M):
                for w in range(2):
                    ins = v.tensor_tensor_reduce(bTL[:, 2 * m + w, 0:C], W[:, m, :], AR[:, w, m, :], 1.0, 0.0, ALU.mult, ALU.add,
                                                 VC[:, 2 * m + w:2 * m + w + 1])
            ins.then_inc(s_vc, 1)
            v.wait_ge(s_pe, 6)
            for m in range(M):
                v.tensor_copy(EP[:, m, :], ps[5 + m][0:EA, 0:H])
            v.wait_ge(s_pool, 4)
            link(v.tensor_tensor(BNS[:, :, :], BN[:, 0, :, :], BNT[:, :, :], ALU.mult))
            link(v.tensor_tensor(BN[:, 4, :, :], BN[:, 4, :, :], BN[:, 2, :, :], ALU.subtract))
            link(v.tensor_tensor(BN[:, 4, :, :], BN[:, 4, :, :], BNS[:, :, :], ALU.mult))
            v.tensor_tensor(BNT[:, :, :], BN[:, 4, :, :], BN[:, 1, :, :], ALU.add)
            v.wait_ge(s_pe, 7)
            for b in range(2):
                n = min(4, 2 * M - 4 * b)
                v.tensor_copy(VR[:, 4 * b:4 * b + n, :], ps[b][:, 0:n * P].rearrange("p (q c) -> p q c", q=n))

            with v.Fori(0, R) as i:
                v.tensor_copy(dK[:, :], keys[:, 0, bass.ds(i * U, U)]).then_inc(s_cid, 1)
                for u in range(U):
                    if u % 4 == 0:
                        v.wait_ge(s_cnt, U * i + u + 4)
                    ins = v.scalar_tensor_tensor(out=bTL[:, u, 0:C], in0=ps[2 + u // 4][:, (u % 4) * P:(u % 4 + 1) * P],
                                                 scalar=dK[:, u:u + 1], in1=later[:, :], op0=ALU.is_equal,
                                                 op1=ALU.mult, accum_out=bNM[:, u:u + 1])
                ins.then_inc(s_cg, 1)
                v.wait_ge(s_cg, i + 1)
                v.tensor_copy(cnt[:, bass.ds(i * U, U)], bNM[:, :]).then_inc(s_cw, 1)
            v.wait_ge(s_cw, R)
            link(v.tensor_scalar(tmp[:, 0, :], cnt[:, :], 0.0, None, ALU.is_equal))
            link(v.scalar_tensor_tensor(out=tmp[:, 1, :], in0=keys[:, 0, :], scalar=0.0, in1=tmp[:, 0, :],
                                        op0=ALU.is_ge, op1=ALU.mult))
            link(v.scalar_tensor_tensor(out=tmp[:, 0, :], in0=keys[:, 0, :], scalar=trash_id[:, 0:1],
                                        in1=tmp[:, 1, :], op0=ALU.subtract, op1=ALU.mult))
            link(v.tensor_scalar(IDX[:, 4, 0:ET], tmp[:, 0, :], trash_id[:, 0:1], None, ALU.add))
            v.tensor_copy(bGI[:, :, :], IDX[:, 0:2, 0:U]).then_inc(b_gi, 1)
            v.sem_inc(b_tot, 1)
            v.wait_ge(b_gi, 1)
            v.sem_inc(s_setup, 1)

            def stats(buf, k, w, slot):
                for j in range(J):
                    ins = v.bn_stats(aBS[:, k, w, j, :], buf[:, slot, j, 0:C])
                return ins

            def aggr(k, w):
                for j in range(J):
                    ins = v.bn_aggr(aMV[:, k, w, j, :], aBS[:, k, w, j, :])
                ins.then_inc(a_mv, 1)

            def shift(k, w, n):
                v.wait_ge(a_rs, n)
                v.scalar_tensor_tensor(out=aNM[:, k, w, :], in0=aMV[:, k, w, :, 0], scalar=-1.0, in1=aRS[:, k, w, :],
                                       op0=ALU.mult, op1=ALU.mult).then_inc(a_nm, 1)

            def a_x_stats(p2, q, c):
                for k in range(2):
                    v.wait_ge(a_x[2 * q + k], 16 * (p2 + 1))
                    ins = stats(aX, k, 0, 2 * q + k)
                ins.then_inc(a_bs, 1)
                v.wait_ge(a_bs, c + 1)
                v.sem_inc(s_gate, 1)
                for k in range(2):
                    aggr(k, 0)

            def a_pair(p, i, q, more):
                for m in range(M):
                    for k in range(2):
                        v.wait_ge(a_sg, 2 * M * p + 2 * m + k + 1)
                        if m:
                            v.wait_ge(a_xT, 2 * M * p + 2 * (m - 1) + k + 1)
                        else:
                            v.wait_ge(a_tc, 2 * p + k + 1)
                        v.tensor_tensor(aT[:, k, m + 1, :], aT[:, k, m, :], aS[:, k, :], ALU.add).then_inc(a_xT, 1)
                if more:
                    a_x_stats(i + q, 1 - q, 2 * p + 1)
                for k in range(2):
                    v.wait_ge(a_bk, 2 * M * p + 2 * (M - 1) + k + 1)
                    v.wait_ge(a_sy[k], 16 * (p + 1))
                    v.tensor_tensor(aYG[:, k, :, 0:C], ps[4 + k][:, :].rearrange("p (j c) -> p j c", j=J),
                                    aX[:, 2 * q + k, :, :], ALU.add).then_inc(a_y, 1)
                v.wait_ge(a_y, 2 * p + 2)
                for k in range(2):
                    ins = stats(aYG, k, 1, k)
                ins.then_inc(a_bs, 1)
                v.wait_ge(a_bs, 2 * p + 2 + more)
                v.sem_inc(s_gate, 1)
                for k in range(2):
                    aggr(k, 1)
                c = 2 + 4 * p
                if more:
                    for k in range(2):
                        shift(k, 0, c + k + 1)
                for k in range(2):
                    shift(k, 1, c + 2 * more + k + 1)

            a_x_stats(0, 0, 0)
            for k in range(2):
                shift(k, 0, k + 1)
            with v.Fori(0, NQ - 1) as i:
                for q in range(2):
                    a_pair(2 * i + q, i, q, 1)
            a_pair(NA - 2, NQ - 1, 0, 1)
            a_pair(NA - 1, NQ - 1, 1, 0)

            def steps(s, base, per):
                n = [0]

                def step(ins, wait=True):
                    n[0] += 1
                    ins.then_inc(s, 1)
                    if wait:
                        v.wait_ge(s, base + n[0])
                    return n[0] == per
                return step

            for m in range(M):
                vs, vd = VR[:, 2 * m, :], VR[:, 2 * m + 1, :]

                def b_round(i, m=m, vs=vs, vd=vd):
                    r = m * R + i
                    step = steps(b_v, b_base[m] + i * b_per[m], b_per[m])
                    v.tensor_copy(bFM[:, :, :], META[:, :, bass.ds(i * U, U)]).then_inc(b_fm, 1)
                    v.wait_ge(b_fm, r + 1)
                    for u in range(U):
                        v.wait_ge(b_gs[u], 16 * (r + 1))
                        v.tensor_tensor_reduce(bTL[:, u, 0:C], bXs[:, u, 0:C], vs, 1.0, 0.0, ALU.mult, ALU.add,
                                               bDT[:, 0, u:u + 1])
                        v.wait_ge(b_gd[u], 16 * (r + 1))
                        v.tensor_tensor_reduce(bT1[:, u, 0:C], bXd[:, u, 0:C], vd, 1.0, 0.0, ALU.mult, ALU.add,
                                               bDT[:, 1, u:u + 1])
                        v.tensor_tensor_reduce(bSW[:, u, :], bXd[:, u, 0:C], vs, 1.0, 0.0, ALU.mult, ALU.add,
                                               bDT[:, 2, u:u + 1])
                        if u % 4 == 0:
                            v.wait_ge(b_d, U * r + u + 4)
                        v.tensor_scalar(bNE[:, u, :], ps[u // 4][:, (u % 4) * P:(u % 4 + 1) * P], bFM[:, 0, u:u + 1], BIG,
                                        ALU.not_equal, ALU.mult).then_inc(b_ne, 1)
                    if m == M - 1:
                        for u in range(U):
                            v.wait_ge(b_gx[u], 16 * (i + 1))
                    v.tensor_copy(bGI[:, :, :], IDX[:, 0:2, bass.ds(i * U + U, U)]).then_inc(b_gi, 1)
                    v.wait_ge(b_ne, U * (r + 1))
                    v.scalar_tensor_tensor(out=bNX[:, 0, :], in0=bDT[:, 0, :], scalar=-1.0, in1=bDT[:, 1, :],
                                           op0=ALU.mult, op1=ALU.subtract)
                    step(v.scalar_tensor_tensor(out=bNX[:, 1, :], in0=bDT[:, 2, :], scalar=-1.0, in1=bDT[:, 1, :],
                                                op0=ALU.mult, op1=ALU.subtract))
                    v.scalar_tensor_tensor(out=bQ[:, :, :], in0=bNX[:, :, :], scalar=SLOPE, in1=bNX[:, :, :],
                                           op0=ALU.mult, op1=ALU.min).then_inc(b_q, 1)
                    for u in range(U):
                        if u % 4 == 0:
                            v.wait_ge(b_e, U * r + u + 4)
                            v.sem_inc(s_gate, 1)
                        v.tensor_tensor_reduce(bTL[:, u, 0:P], bNE[:, u, :], ps[2 + u // 4][:, (u % 4) * P:(u % 4 + 1) * P], 1.0,
                                               BIG, ALU.add, ALU.min, bNM[:, u:u + 1]).then_inc(b_eu, 1)
                    v.wait_ge(b_eu, U * (r + 1))
                    step(v.tensor_tensor(bPR[:, :, 0], bNM[:, :], bQ[:, 1, :], ALU.min))
                    v.tensor_tensor(bARG[:, 0, :], bPR[:, :, 0], bQ[:, 0, :], ALU.subtract)
                    v.tensor_tensor(bARG[:, 1, :], bPR[:, :, 0], bQ[:, 1, :], ALU.subtract).then_inc(b_arg, 1)
                    v.wait_ge(b_wx, r + 1)
                    v.tensor_tensor(bWS[:, :], bWX[:, 1, :], bFM[:, 2, :], ALU.mult).then_inc(b_ws, 1)
                    for u in range(U):
                        v.tensor_scalar(bSW[:, u, :], bNE[:, u, :], 0.0, bWX[:, 0, u:u + 1], ALU.is_equal,
                                        ALU.mult).then_inc(b_sw, 1)
                    for u in range(U):
                        v.wait_ge(b_acc, U * r + u + 1)
                        v.wait_ge(b_t0, U * r + u + 1)
                        v.tensor_tensor(bTL[:, u, 0:C + 1], ps[4 + u % 3][:, 0:C + 1],
                                        bT0[:, u, 0:C + 1], ALU.add).then_inc(b_tl, 1)
                    for u in range(U):
                        bc = ps[7][:, 0:CP]
                        v.wait_ge(b_bc, U * r + u + 1)
                        step(v.tensor_scalar(bPR[:, u, 1:2], bc[:, C + 1:C + 2], bFM[:, 1, u:u + 1], None, ALU.add))
                        v.tensor_tensor(bTOT[:, u, C + 1:C + 2], bPR[:, u, 0:1], bPR[:, u, 1:2], ALU.min
                                        ).then_inc(b_nm, 1)
                        v.wait_ge(b_ft, U * r + u + 1)
                        v.scalar_tensor_tensor(out=bTOT[:, u, 0:C + 1], in0=bc[:, 0:C + 1], scalar=bF[:, u, 1:2],
                                               in1=bT1[:, u, 0:C + 1], op0=ALU.mult, op1=ALU.add).then_inc(b_tot, 1)
                    v.wait_ge(b_tot, U * (r + 1) + 1)
                    step(v.tensor_scalar(bRL[:, 0, :], bTOT[:, :, C], EPS_SM, None, ALU.add))
                    v.reciprocal(bRL[:, 1, :], bRL[:, 0, :]).then_inc(b_rl, 1)
                    if not isinstance(r, int) or r > 0:
                        for u in range(U):
                            v.wait_ge(b_sc[u], 16 * r)
                    v.tensor_copy(bOI[:, :], IDX[:, 3, bass.ds(i * U, U)]).then_inc(b_oi, 1)
                    for u in range(U):
                        v.wait_ge(b_th, U * r + u + 1)
                        ins = v.scalar_tensor_tensor(out=bO[:, u, 0:C], in0=bTH[:, u, :], scalar=0.5,
                                                     in1=bXP[:, u, :], op0=ALU.mult, op1=ALU.add)
                        if m < M - 1:
                            ins.then_inc(b_out, 1)
                    if m == M - 1:
                        step(ins)
                        for u in range(U):
                            ins = v.tensor_tensor(bO[:, u, 0:C], bO[:, u, 0:C], bXx[:, u, :], ALU.add)
                        step(ins)
                        for u in range(U):
                            ins = v.bn_stats(bBS[:, u, :], bO[:, u, 0:C])
                        step(ins)
                        v.sem_inc(s_gate, 1)
                        for u in range(U):
                            v.bn_aggr(bMV[:, u, :], bBS[:, u, :]).then_inc(b_mv, 1)
                        v.wait_ge(b_rs, i + 1)
                        step(v.reciprocal(bRS[:, 1, :], bRS[:, 0, :]))
                        v.scalar_tensor_tensor(out=bNR[:, :], in0=bMV[:, :, 0], scalar=-1.0, in1=bRS[:, 1, :],
                                               op0=ALU.mult, op1=ALU.mult).then_inc(b_nr, 1)
                if m == 0:
                    b_round(0)
                with v.Fori(1 if m == 0 else 0, R) as i:
                    b_round(i)
                if m < M - 1:
                    v.tensor_copy(bGI[:, :, :], IDX[:, 0:2, 0:U]).then_inc(b_gi, 1)

            for u in range(U):
                v.wait_ge(b_sc[u], 16 * M * R)
            v.wait_ge(b_out, U * M * R)
            v.memset(dG[:, :, C + DE:C + EA], 1.0)
            link(v.memset(dG[:, :, C:C + DE], 0.0))
            v.sem_inc(s_dclr, 1)
            for m in range(M):
                gi = 2 if m == 0 else 1
                v.tensor_copy(dGI[:, :], IDX[:, gi, 0:U]).then_inc(d_gi, 1)

                def d_round(i, m=m, gi=gi):
                    r = m * R + i
                    v.tensor_copy(dK[:, :], keys[:, 0, bass.ds(i * U, U)]).then_inc(d_k, 1)
                    v.wait_ge(d_k, r + 1)
                    for u in range(U):
                        if u % 4 == 0:
                            v.wait_ge(d_t, U * r + u + 4)
                        v.tensor_scalar(dS[:, u, :], ps[u // 4][:, (u % 4) * P:(u % 4 + 1) * P], dK[:, u:u + 1], None,
                                        ALU.is_equal).then_inc(d_s, 1)
                    v.wait_ge(d_s, U * (r + 1))
                    for u in range(U):
                        v.wait_ge(d_g[u], 16 * (r + 1))
                    v.tensor_copy(dGI[:, :], IDX[:, gi, bass.ds(i * U + U, U)]).then_inc(d_gi, 1)
                    if not isinstance(r, int) or r > 0:
                        for b in range(2):
                            v.wait_ge(d_a[b], 16 * (U // 2) * r)
                    v.tensor_copy(dOI[:, :], IDX[:, 4, bass.ds(i * U, U)]).then_inc(d_oi, 1)

                if m == 0:
                    d_round(0)
                with v.Fori(1 if m == 0 else 0, R) as i:
                    d_round(i)

                n0 = m * NT

                def add_up(p, m=m, n0=n0):
                    for k in range(2):
                        v.wait_ge(e_in[k], 48 * (m * NA + p + 1))
                        v.tensor_tensor(eA[:, k, 0, :, 0:AW[m]], eA[:, k, 0, :, 0:AW[m]], eA[:, k, 1, :, 0:AW[m]],
                                        ALU.add).then_inc(e_a, 1)
                    for k in range(2):
                        v.wait_ge(e_a, n0 + 2 * p + k + 1)
                        if not isinstance(p, int):
                            v.wait_ge(e_tp, n0 + 2 * p + k - 1)
                        if m == 0:
                            v.tensor_tensor(eE[:, k, :, :], eA[:, k, 0, :, C:C + EA], self_ea[:, :, :], ALU.add)
                        v.tensor_tensor(eS[:, k, :, :], eA[:, k, 0, :, 0:C], eG[:, k, :, :], ALU.add
                                        ).then_inc(e_s, 1)

                def finish(p, m=m, n0=n0):
                    bias = B2[:, m, :].unsqueeze(1).to_broadcast([P, J, C])
                    for k in range(2):
                        v.wait_ge(e_y, n0 + 2 * p + k + 1)
                        v.wait_ge(e_st[k], 16 * (m * NA + p + 1))
                        v.tensor_tensor(eO[:, k, :, :], ps[6 + k][:, :].rearrange("p (j c) -> p j c", j=J), bias,
                                        ALU.add).then_inc(e_v, 1)
                    if m == M - 1:
                        for k in range(2):
                            v.wait_ge(e_v, n0 + 2 * p + k + 1)
                            v.wait_ge(e_yi[k], 16 * (p + 1))
                            v.tensor_tensor(eO[:, k, :, :], eO[:, k, :, :], eY[:, k, :, :], ALU.add).then_inc(e_o, 1)

                add_up(0)
                with v.Fori(0, NA - 1) as i:
                    add_up(i + 1)
                    finish(i)
                finish(NA - 1)


_INS = ["x", "src", "dst", "edge_attr_16", "L0_gnn_Ws", "L0_gnn_att_src", "L0_gnn_att_dst", "L0_gnn_bias",
        "L1_gnn_enc_w0", "L1_gnn_enc_b0", "L1_gnn_w1_0", "L1_gnn_b1_0", "L1_gnn_g0", "L1_gnn_be0", "L1_gnn_rm0",
        "L1_gnn_rv0", "L1_gnn_w2_0", "L1_gnn_b2_0", "L1_gnn_enc_w", "L1_gnn_enc_b", "L1_gnn_w1", "L1_gnn_b1",
        "L1_gnn_g", "L1_gnn_be", "L1_gnn_rm", "L1_gnn_rv", "L1_gnn_w2", "L1_gnn_b2"]


def kernel(**inputs):
    import numpy as _np
    import concourse.bacc as _bacc
    from concourse import mybir as _mybir
    from concourse.bass_utils import run_bass_kernel_spmd as _run

    nc = _bacc.Bacc("TRN2", target_bir_lowering=False, num_devices=1)
    arrays, args = {}, []
    for name in _INS:
        a = _np.ascontiguousarray(inputs[name])
        arrays[f"in_{name}_dram"] = a
        args.append(nc.dram_tensor(f"in_{name}_dram", a.shape, _mybir.dt.from_np(a.dtype), kind="ExternalInput").ap())
    shape = inputs["x"].shape
    args.append(nc.dram_tensor("out_0_dram", shape, _mybir.dt.float32, kind="ExternalOutput").ap())
    gnn_program(nc, *args)
    r = _run(nc, [arrays], core_ids=[0])
    return r.results[0]["out_0_dram"]
```

```python
from contextlib import ExitStack

import concourse.bass as bass
from concourse import mybir

ALU = mybir.AluOpType
ACT = mybir.ActivationFunctionType
F32 = mybir.dt.float32
I32 = mybir.dt.int32

P = 128
J = 4
TN = P * J
U = 8
M = 3
BIG = 1e30
EPS_LN = 1e-5
EPS_BN = 1e-5
EPS_SM = 1e-16
SLOPE = 0.2
C = 128
H = 256
DE = 16
EA = DE + 1
CP = 132


def gnn_program(nc, x, src, dst, attr, Ws, a_src, a_dst, gat_b, enc_w0, enc_b0, w1_0, b1_0, g_0, be_0, rm_0,
                rv_0, w2_0, b2_0, enc_w, enc_b, w1, b1, g, be, rm, rv, w2, b2, out):
    N = x.shape[0]
    E = src.shape[0]
    NT = -(-N // TN)
    NT += -NT % 4
    LAST = N - TN
    R = -(-E // (P * U))
    R += 1 - R % 2
    ET = R * U
    ETP = ET + U
    NB_ = 4
    EB = ET // NB_
    NR = (NT + 1) * TN
    TRASH = NR - P
    SKIP = 2 * N
    assert EB * NB_ == ET and EB <= P and R >= 5 and NT >= 12

    def dram(name, shape):
        return nc.dram_tensor(name, shape, F32, kind="Internal").ap()

    h0_d = dram("h0_d", (N, C))
    x1_d = dram("x1_d", (N, C))
    x2_d = dram("x2_d", (N, C))
    yg_d = dram("yg_d", (N, 2 * C))
    g1_d = dram("g1_d", (N, C))
    g2_d = dram("g2_d", (N, C))
    AW = [C + EA, C, C]
    agg_d = [[dram(f"agg{m}{b}_d", (NR, AW[m])) for b in range(2)] for m in range(M)]
    eaT_d = dram("eaT_d", (NT, EA, TN))
    gat_in = [h0_d, x1_d, x2_d]
    gin_in = [yg_d.rearrange("n (t c) -> (n t) c", t=2), g1_d, g2_d]

    with ExitStack() as ctx:
        def sb(name, shape, dt=F32):
            return ctx.enter_context(nc.sbuf_tensor(name, shape, dt))

        def sem(name):
            return ctx.enter_context(nc.semaphore(name))

        def sems(name, n):
            return [sem(f"{name}{k}") for k in range(n)]

        ps = [ctx.enter_context(nc.psum_tensor(f"ps{k}", [P, 512], F32)) for k in range(8)]

        ident = sb("ident", [P, P])
        last_row = sb("last_row", [P, P])
        later = sb("later", [P, P])
        ones_row = sb("ones_row", [1, P])
        zeros = sb("zeros", [P, J * (C + EA)])
        mhalf = sb("mhalf", [P, U])
        trash_id = sb("trash_id", [P, 1])
        self_ea = sb("self_ea", [P, J, EA])
        W = sb("W", [P, M, C])
        W1X = sb("W1X", [P, M, H])
        W1B = sb("W1B", [P, M, H])
        W2 = sb("W2", [P, M, 2, C])
        ENC = sb("ENC", [EA, M, C])
        ENCT = sb("ENCT", [P, M, EA])
        EP = sb("EP", [EA, M, H])
        BN = sb("BN", [P, 5, M, 2])
        BNS = sb("BNS", [P, M, 2])
        BNT = sb("BNT", [P, M, 2])
        B2 = sb("B2", [P, M, C])
        GBC = sb("GBC", [P, M])
        GBR = sb("GBR", [1, M, C])
        AR = sb("AR", [P, 2, M, C])
        VC = sb("VC", [P, 2 * M])
        VR = sb("VR", [P, 2 * M, C])

        rowI = sb("rowI", [EB, 3, NB_, P], I32)
        rowF = sb("rowF", [EB, 3, NB_, P])
        keys = sb("keys", [P, 3, ET])
        META = sb("META", [P, 4, ET])
        cnt = sb("cnt", [P, ET])
        tmp = sb("tmp", [P, 2, ET])
        IDX = sb("IDX", [P, 5, ETP], I32)

        s_w = sem("s_w")
        s_idx = sem("s_idx")
        s_pool = sem("s_pool")
        s_rowf, s_keys, s_meta, s_enct, s_vc, s_setup, s_pe, s_dclr = [
            sem(n) for n in ["s_rowf", "s_keys", "s_meta", "s_enct", "s_vc", "s_setup", "s_pe", "s_dclr"]]
        s_v = sem("s_v")
        s_gate = sem("s_gate")
        s_cid = sem("s_cid")
        s_cnt = sem("s_cnt")
        n_idx = [0]

        weight_loads = [
            (W[:, :, :], Ws.rearrange("m k c -> k m c")),
            (W1X[:, 0, :], w1_0), (W1B[:, 0, :], w1_0),
            (W2[:, 0, :, :], w2_0.rearrange("(h k) c -> k h c", h=2)),
            (ENC[0:DE, 0, :], enc_w0), (ENC[DE:EA, 0, :], enc_b0.rearrange("(o c) -> o c", o=1)),
            (GBC[:, :], gat_b.rearrange("m c -> c m")), (GBR[:, :, :], gat_b.rearrange("(o m) c -> o m c", o=1)),
            (B2[:, 0, :], b2_0.rearrange("(o c) -> o c", o=1).to_broadcast([P, C])),
        ]
        for m in range(1, M):
            weight_loads += [
                (W1X[:, m, :], w1[m - 1, 0:C, :]), (W1B[:, m, :], w1[m - 1, C:2 * C, :]),
                (W2[:, m, :, :], w2[m - 1].rearrange("(h k) c -> k h c", h=2)),
                (ENC[0:DE, m, :], enc_w[m - 1]), (ENC[DE:EA, m, :], enc_b[m - 1:m, :]),
                (B2[:, m, :], b2[m - 1:m, :].to_broadcast([P, C])),
            ]
        for m in range(M):
            weight_loads += [(AR[:, 0, m, :], a_src[m:m + 1, :].to_broadcast([P, C])),
                             (AR[:, 1, m, :], a_dst[m:m + 1, :].to_broadcast([P, C]))]
            for q, (v0, v) in enumerate(((g_0, g), (be_0, be), (rm_0, rm), (rv_0, rv), (b1_0, b1))):
                vec = v0 if m == 0 else v[m - 1]
                weight_loads.append((BN[:, q, m, :], vec.rearrange("(h p) -> p h", p=P)))
        NW = len(weight_loads)

        block = ctx.enter_context(nc.Block())

        aX = sb("aX", [P, 4, J, C])
        aH = sb("aH", [P, 2, J, C])
        aT = sb("aT", [P, 2, 4, TN])
        aS = sb("aS", [P, 2, TN])
        aO = sb("aO", [P, 2, 2, J, C])
        aYG = sb("aYG", [P, 4, J, 2 * C])
        aBS = sb("aBS", [P, 2, 3, J, 6])
        aMV = sb("aMV", [P, 2, 3, J, 2])
        aRS = sb("aRS", [P, 2, 3, J])
        aNM = sb("aNM", [P, 2, 3, J])
        aVE = sb("aVE", [P, 2, 3, J])
        a_x = sems("a_x", 4)
        a_mv, a_rs, a_nm, a_h, a_tp, a_tc, a_mm, a_sg, a_xT, a_bk, a_o, a_y, a_g, a_pv, a_bs = [
            sem(n) for n in ["a_mv", "a_rs", "a_nm", "a_h", "a_tp", "a_tc", "a_mm", "a_sg", "a_xT", "a_bk", "a_o",
                             "a_y", "a_g", "a_pv", "a_bs"]]
        a_sh = sems("a_sh", 2)
        a_s1 = sems("a_s1", 2)
        a_s2 = sems("a_s2", 2)
        a_sy = sems("a_sy", 4)
        NA = NT // 2

        def a_rounds(engine, a_pair, end):
            a_pair(0, 0, 0, True, False)
            with engine.Fori(0, end // 2) as i:
                a_pair(2 * i + 1, 1, i, False, False)
                a_pair(2 * i + 2, 0, i + 1, False, False)
            for p in range(2 * (end // 2) + 1, NA):
                a_pair(p, p % 2, p // 2, False, p == NA - 1)

        bXs = sb("bXs", [P, 2, U, CP])
        bXd = sb("bXd", [P, 2, U, CP])
        bXx = sb("bXx", [P, U, C])
        bNE = sb("bNE", [P, U, P])
        bSW = sb("bSW", [P, U, P])
        bTL = sb("bTL", [P, U, CP])
        bTOT = sb("bTOT", [P, U, CP])
        bCB = sb("bCB", [P, U, CP])
        bA = sb("bA", [P, U, C])
        bAT = sb("bAT", [P, U, C])
        bXP = sb("bXP", [P, U, C])
        bTH = sb("bTH", [P, U, C])
        bO = sb("bO", [P, U, 2 * C])
        bFM = sb("bFM", [P, 4, U])
        bGI = sb("bGI", [P, 2, 2, U], I32)
        bOI = sb("bOI", [P, U], I32)
        bDT = sb("bDT", [P, 3, U])
        bNX = sb("bNX", [P, 2, U])
        bSB = sb("bSB", [P, 4, U])
        bNM = sb("bNM", [P, U])
        bPR = sb("bPR", [P, U])
        bNC = sb("bNC", [P, U + 1])
        bMX = sb("bMX", [P, U])
        bARG = sb("bARG", [P, 4, U])
        bW4 = sb("bW4", [P, 4, U])
        bWS = sb("bWS", [P, U])
        bRL = sb("bRL", [P, 2, U])
        bBS = sb("bBS", [P, U, 6])
        bMV = sb("bMV", [P, U, 2])
        bRS = sb("bRS", [P, 2, U])
        bNR = sb("bNR", [P, U])
        b_g = [sems(f"b_g{s}", U) for s in range(2)]
        RS = [(R + 1) // 2, R // 2]
        b_gx = sems("b_gx", U)
        b_sc = sems("b_sc", U)
        b_names = ["b_fm", "b_gi", "b_d", "b_ne", "b_q", "b_e", "b_eu", "b_pr", "b_bn", "b_arg", "b_wx", "b_sw",
                   "b_acc", "b_tl", "b_bc", "b_cb", "b_tot", "b_rl", "b_a", "b_at", "b_atc", "b_h",
                   "b_th", "b_out", "b_oi", "b_mv", "b_ve", "b_rs", "b_nr"]
        (b_fm, b_gi, b_d, b_ne, b_q, b_e, b_eu, b_pr, b_bn, b_arg, b_wx, b_sw, b_acc, b_tl, b_bc, b_cb,
         b_tot, b_rl, b_a, b_at, b_atc, b_h, b_th, b_out, b_oi, b_mv, b_ve, b_rs, b_nr) = [sem(n) for n in b_names]
        s_zero = sem("s_zero")
        b_v = sem("b_v")
        b_per = [7, 7, 10]
        b_base = [0, R * b_per[0], 2 * R * b_per[0]]
        s_cg = sem("s_cg")
        s_cw = sem("s_cw")
        e_a = sem("e_a")

        dG = bO
        dS = bNE
        dO = sb("dO", [P, U, C + EA])
        dK = sb("dK", [P, U])
        dGI = sb("dGI", [P, U], I32)
        dOI = sb("dOI", [P, U], I32)
        d_g = sems("d_g", U)
        d_a = sems("d_a", 2)
        d_at, d_k, d_gi, d_oi, d_t, d_s, d_acc, d_o = [
            sem(n) for n in ["d_at", "d_k", "d_gi", "d_oi", "d_t", "d_s", "d_acc", "d_o"]]

        eG = aX[:, 0:2, :, :]
        eY = aX[:, 2:4, :, :]
        eA = sb("eA", [P, 2, 2, J, C + EA])
        eS = aO[:, 0, :, :, :]
        eE = sb("eE", [P, 2, J, EA])
        eHT = aS
        eET = sb("eET", [EA, 2, TN])
        eZ = aT[:, 0, :, :].rearrange("p (k h) n -> p k h n", k=2)
        eO = aH
        e_in = sems("e_in", 2)
        e_et = sems("e_et", 2)
        e_st = sems("e_st", 2)
        e_se = sems("e_se", 2)
        e_yi = sems("e_yi", 2)
        e_s, e_tp, e_tc, e_z, e_zr, e_y, e_o, e_v = [
            sem(n) for n in ["e_s", "e_tp", "e_tc", "e_z", "e_zr", "e_y", "e_o", "e_v"]]

        def node_tile(t, buf):
            return buf[bass.ds(t * TN, TN), :].rearrange("(p j) c -> p j c", j=J)

        def last_tile(buf):
            return buf[LAST:N, :].rearrange("(p j) c -> p j c", j=J)

        def b_rounds(engine, b_round):
            b_round(0, 0, 0)
            with engine.Fori(0, R // 2) as i:
                b_round(2 * i + 1, 1, i)
                b_round(2 * i + 2, 0, i + 1)

        @block.sync
        def _(sp):
            sp.wait_ge(s_pool, 1)
            full = E // P
            for k, (vec, off) in enumerate(((src, 0), (dst, 0), (dst, 1))):
                for b in range(NB_):
                    lo = b * EB
                    n = max(0, min(EB, (E - off) // P - lo))
                    if n:
                        sp.dma_start(rowI[0:n, k, b, :], vec[off + lo * P:off + (lo + n) * P]
                                     .rearrange("(t p) -> t p", p=P)).then_inc(s_idx, 16)
                        n_idx[0] += 1
                    rest = E - off - (lo + n) * P
                    if 0 <= n < EB and 0 < rest < P:
                        sp.dma_start(rowI[n:n + 1, k, b, 0:rest],
                                     vec[off + (lo + n) * P:E].rearrange("(t p) -> t p", t=1)).then_inc(s_idx, 16)
                        n_idx[0] += 1

            def tile_of(t):
                if isinstance(t, int) and (t + 1) * TN > N:
                    return last_tile
                return lambda buf: node_tile(t, buf)

            def stores_before(s, p, k):
                if isinstance(p, int) and 2 * p + k >= N // TN:
                    for kk in range(2):
                        sp.wait_ge(s[kk], 16 * (p + 1 + (kk < k)))

            def h0_out(p):
                for k in range(2):
                    stores_before(a_sh, p, k)
                    sp.wait_ge(a_h, 2 * J * p + J * (k + 1))
                    sp.dma_start(tile_of(2 * p + k)(h0_d), aH[:, k, :, :]).then_inc(a_sh[k], 16)

            def yg_out(p, q):
                for k in range(2):
                    if isinstance(p, int) and 2 * p + k >= N // TN:
                        for st in range(2):
                            for kk in range(2):
                                before = (p + 1 - st) // 2 + (st == q and kk < k)
                                sp.wait_ge(a_sy[2 * st + kk], 16 * (before + 1))
                    sp.wait_ge(a_g, 2 * J * p + J * (k + 1))
                    sp.dma_start(tile_of(2 * p + k)(yg_d), aYG[:, 2 * q + k, :, :]).then_inc(a_sy[2 * q + k], 16)

            def a_pair(p, q, n, first, last):
                if not first and not last:
                    for k in range(2):
                        sp.wait_ge(a_y, 2 * (p - 1) + k + 1)
                        sp.dma_start(aX[:, 2 * (1 - q) + k, :, :], tile_of(2 * p + 2 + k)(x)).then_inc(a_x[2 * (1 - q) + k], 16)
                for m, (o, s) in enumerate(((x1_d, a_s1), (x2_d, a_s2))):
                    for k in range(2):
                        stores_before(s, p, k)
                        sp.wait_ge(a_o, 4 * p + 2 * m + k + 1)
                        sp.dma_start(tile_of(2 * p + k)(o), aO[:, k, m, :, :]).then_inc(s[k], 16)
                if not last:
                    h0_out(p + 1)
                if not first:
                    yg_out(p - 1, 1 - q)

            for t in range(4):
                sp.dma_start(aX[:, t, :, :], node_tile(t, x)).then_inc(a_x[t], 16)
            h0_out(0)
            a_rounds(sp, a_pair, NA - 4)
            yg_out(NA - 1, 1)

            for m in range(M):
                for b in range(2):
                    agg = agg_d[m][b]
                    n = J * AW[m]
                    sp.wait_ge(b_fm, m * R + 1)
                    with sp.Fori(0, NT + 1) as i:
                        sp.dma_start(agg[bass.ds(i * TN, TN), :].rearrange("(p j) c -> p (j c)", j=J),
                                     zeros[:, 0:n]).then_inc(s_zero, 16)

            def attrs(r, t0):
                for u in range(U):
                    left = E - (t0 + u) * P
                    if left > 0:
                        k = min(P, left)
                        sp.dma_start(dG[0:k, u, C:C + DE], attr[(t0 + u) * P:(t0 + u) * P + k, :]).then_inc(d_at, 16)
                    else:
                        sp.sem_inc(d_at, 16)

            def attr_round(r):
                sp.dma_start(dG[:, :, C:C + DE],
                             attr[bass.ds(r * (U * P), U * P), :].rearrange("(u p) c -> p u c", p=P)
                             ).then_inc(d_at, 16 * U)

            sp.wait_ge(s_dclr, 1)
            attr_round(0)
            with sp.Fori(1, R - 1) as i:
                sp.wait_ge(d_acc, U * i)
                attr_round(i)
            sp.wait_ge(d_acc, U * (R - 1))
            sp.wait_ge(d_at, 16 * U * (R - 1))
            attrs(R - 1, (R - 1) * U)

            for m in range(M):
                n0 = m * NT
                into = [g1_d, g2_d, out][m]

                def load_rows(k, t, m=m):
                    pick = tile_of(t)
                    own = pick(yg_d)[:, :, C:2 * C] if m == 0 else pick([None, g1_d, g2_d][m])
                    sp.dma_start(eG[:, k, :, :], own).then_inc(e_in[k], 16)
                    for b in range(2):
                        sp.dma_start(eA[:, k, b, :, 0:AW[m]], pick(agg_d[m][b])).then_inc(e_in[k], 16)

                def load_ea(k, t):
                    sp.dma_start(eET[:, k, :], eaT_d[bass.ds(t, 1), :, :].rearrange("o r n -> (o r) n")
                                 ).then_inc(e_et[k], 16)

                def load_y(k, t):
                    sp.dma_start(eY[:, k, :, :], tile_of(t)(yg_d)[:, :, 0:C]).then_inc(e_yi[k], 16)

                def e_out(p, more, m=m, n0=n0, into=into):
                    for k in range(2):
                        if isinstance(p, int) and 2 * p + k >= N // TN:
                            for kk in range(2):
                                sp.wait_ge(e_st[kk], 16 * (m * NA + p + 1 + (kk < k)))
                        sp.wait_ge(e_o, n0 + 2 * p + k + 1)
                        sp.dma_start(tile_of(2 * p + k)(into), eO[:, k, :, :]).then_inc(e_st[k], 16)
                        if more and m == M - 1:
                            load_y(k, 2 * p + 2 + k)

                def e_pair(p, first, more, m=m, n0=n0):
                    if more:
                        for k in range(2):
                            sp.wait_ge(e_s, n0 + 2 * p + k + 1)
                            load_rows(k, 2 * p + 2 + k)
                    if m == 0:
                        for k in range(2):
                            sp.wait_ge(e_tc, 4 * p + 2 * (k + 1))
                            sp.dma_start(eaT_d[bass.ds(2 * p + k, 1), :, :].rearrange("o r n -> (o r) n"),
                                         eET[:, k, :]).then_inc(e_se[k], 16)
                    if not first:
                        e_out(p - 1, True)
                    if more and m:
                        for k in range(2):
                            sp.wait_ge(e_z, 2 * (n0 + 2 * p + k + 1))
                            load_ea(k, 2 * p + 2 + k)

                for b in range(2):
                    sp.wait_ge(d_a[b], 16 * (U // 2) * R * (m + 1))
                if m == 0:
                    sp.wait_ge(s_zero, 16 * 2 * M * (NT + 1))
                else:
                    for k in range(2):
                        sp.wait_ge(e_st[k], 16 * (NA * m + 1))
                        sp.wait_ge(e_se[k], 16 * (NA + 1))
                for k in range(2):
                    load_rows(k, k)
                    if m:
                        load_ea(k, k)
                    if m == M - 1:
                        load_y(k, k)
                e_pair(0, True, True)
                with sp.Fori(1, NA - 3) as i:
                    e_pair(i, False, True)
                for p in range(NA - 3, NA):
                    e_pair(p, False, p < NA - 1)
                e_out(NA - 1, False)
            for k in range(2):
                sp.wait_ge(e_st[k], 16 * (NA * M + 1))

        @block.gpsimd
        def _(pool):
            pool.memset(rowI[:, 0:2, :, :], -1)
            pool.memset(rowI[:, 2, :, :], -2)
            pool.memset(ident[:, :], 0.0)
            pool.memset(last_row[:, :], 0.0)
            pool.memset(later[:, :], 1.0)
            pool.memset(ones_row[:, :], 1.0)
            pool.memset(zeros[:, :], 0.0)
            pool.memset(mhalf[:, :], -0.5)
            pool.memset(self_ea[:, :, :], 0.0)
            pool.memset(bXs[:, :, :, C:CP], 1.0)
            pool.memset(bXd[:, :, :, C:CP], 1.0)
            pool.memset(bCB[:, :, :], 0.0)
            pool.memset(bNC[:, :], 0.0)
            pool.memset(IDX[:, :, :], 0).then_inc(s_pool, 1)
            for s in a_sh + a_s1 + a_s2 + a_sy + e_se + e_st:
                pool.sem_inc(s, 16)
            pool.wait_ge(s_pool, 1)
            pool.memset(self_ea[:, :, 0:1], 1.0)
            pool.memset(self_ea[:, :, DE:EA], 1.0)
            pool.affine_select(out=ident[:, :], in_=ident[:, :], compare_op=ALU.not_equal, fill=1.0, base=0,
                               pattern=[[-1, P]], channel_multiplier=1)
            pool.affine_select(out=last_row[:, :], in_=last_row[:, :], compare_op=ALU.not_equal, fill=1.0,
                               base=-(P - 1), pattern=[[0, P]], channel_multiplier=1)
            pool.affine_select(out=later[:, :], in_=later[:, :], compare_op=ALU.is_gt, fill=0.0, base=0,
                               pattern=[[1, P]], channel_multiplier=-1)
            pool.iota(trash_id[:, :], pattern=[[0, 1]], base=TRASH, channel_multiplier=1,
                      allow_small_or_imprecise_dtypes=True).then_inc(s_pool, 1)

            pool.wait_ge(s_w, 16 * NW)
            pool.tensor_scalar(BNS[:, :, :], BN[:, 3, :, :], EPS_BN, None, ALU.add).then_inc(s_pool, 1)
            pool.wait_ge(s_pool, 3)
            pool.tensor_tensor(BNT[:, :, :], BNS[:, :, :], mhalf[:, 0:2 * M].rearrange("p (m h) -> p m h", h=2),
                               ALU.pow).then_inc(s_pool, 1)

            def a_rstd(n, k, w):
                pool.wait_ge(a_mv, n)
                pool.sem_inc(s_gate, 1)
                pool.tensor_scalar(aVE[:, k, w, :], aMV[:, k, w, :, 1], EPS_LN, None, ALU.add).then_inc(a_pv, 1)
                pool.wait_ge(a_pv, n)
                pool.tensor_tensor(aRS[:, k, w, :], aVE[:, k, w, :], mhalf[:, 0:J], ALU.pow).then_inc(a_rs, 1)

            def a_pair(p, q, n, first, last):
                c = 2 if first else 4 * p
                if not last:
                    for k in range(2):
                        a_rstd(c + k + 1, k, 0)
                if not first:
                    for k in range(2):
                        a_rstd(c + 2 * (not last) + k + 1, k, 2 - q)

            for k in range(2):
                a_rstd(k + 1, k, 0)
            a_rounds(pool, a_pair, NA - 2)
            for k in range(2):
                a_rstd(4 * (NA - 1) + 2 + k + 1, k, 2)

            n_last = pool.to_reg(N - 1)
            for s in a_sh + a_s1 + a_s2:
                pool.wait_ge(s, 16 * (NA + 1))
            for s in a_sy:
                pool.wait_ge(s, 16 * (NA // 2 + 1))
            for m in range(M):
                r0 = m * R

                def b_rows(to, of, index, signal):
                    pool.indirect_dma_start(to, None, of, bass.IndirectOffsetOnAxis(ap=index, axis=0),
                                            bounds_check=n_last, oob_is_err=False).then_inc(signal, 16)

                def b_gather(i, s, m=m):
                    pool.wait_ge(b_gi, m * R + i + m + 1)
                    pool.sem_inc(s_gate, 1)
                    for u in range(U):
                        b_rows(bXs[:, s, u, 0:C], gat_in[m], bGI[:, s, 0, u:u + 1], b_g[s][u])
                        b_rows(bXd[:, s, u, 0:C], gat_in[m], bGI[:, s, 1, u:u + 1], b_g[s][u])

                def b_gather_x(s):
                    for u in range(U):
                        b_rows(bXx[:, u, :], x, bGI[:, s, 1, u:u + 1], b_gx[u])

                def b_scatter(i, m=m):
                    r = m * R + i
                    if m == M - 1:
                        pool.wait_ge(b_mv, U * (i + 1))
                        pool.sem_inc(s_gate, 1)
                        pool.tensor_scalar(bRS[:, 0, :], bMV[:, :, 1], EPS_LN, None, ALU.add).then_inc(b_ve, 1)
                        pool.wait_ge(b_ve, i + 1)
                        pool.tensor_tensor(bRS[:, 1, :], bRS[:, 0, :], mhalf[:, 0:U], ALU.pow).then_inc(b_rs, 1)
                    pool.wait_ge(b_oi, r + 1)
                    for u in range(U):
                        pool.wait_ge(b_out, U * r + u + 1)
                        pool.sem_inc(s_gate, 1)
                        dest, wid = [(x1_d, C), (x2_d, C), (yg_d, 2 * C)][m]
                        pool.indirect_dma_start(dest, bass.IndirectOffsetOnAxis(ap=bOI[:, u:u + 1], axis=0),
                                                bO[:, u, 0:wid], None, bounds_check=n_last,
                                                oob_is_err=False).then_inc(b_sc[u], 16)

                def b_step(i, s, m=m):
                    if not isinstance(i, int) or i > 0:
                        b_scatter(i - 1)
                    if m == M - 1:
                        b_gather_x(s)
                    if not isinstance(i, int) or i < R - 1:
                        b_gather(i + 1, 1 - s)

                b_gather(0, 0)
                b_step(0, 0)
                with pool.Fori(0, R // 2 - 1) as i:
                    b_step(2 * i + 1, 1)
                    b_step(2 * i + 2, 0)
                b_step(R - 2, 1)
                b_step(R - 1, 0)
                b_scatter(R - 1)
                for u in range(U):
                    pool.wait_ge(b_sc[u], 16 * (r0 + R))

            lim2 = pool.to_reg(2 * N - 1)
            agg_last = pool.to_reg(NR - 1)
            pool.wait_ge(s_zero, 16 * 2 * M * (NT + 1))
            for m in range(M):
                r0 = m * R
                if m:
                    for k in range(2):
                        pool.wait_ge(e_st[k], 16 * (NA * m + 1))

                def d_gather(r, m=m):
                    pool.wait_ge(d_gi, r + m + 1)
                    for u in range(U):
                        if not isinstance(r, int) or r > 0:
                            pool.wait_ge(d_acc, U * (r - 1) + u + 1)
                        pool.sem_inc(s_gate, 1)
                        pool.indirect_dma_start(dG[:, u, 0:C], None, gin_in[m],
                                                bass.IndirectOffsetOnAxis(ap=dGI[:, u:u + 1], axis=0),
                                                bounds_check=lim2 if m == 0 else n_last,
                                                oob_is_err=False).then_inc(d_g[u], 16)

                def d_add(r, m=m):
                    pool.wait_ge(d_oi, r + 1)
                    for u in range(U):
                        pool.wait_ge(d_o, U * r + u + 1)
                        if not isinstance(r, int) or U * r + u >= 2:
                            pool.wait_ge(d_a[u % 2], 16 * ((U // 2) * r + u // 2))
                        pool.sem_inc(s_gate, 1)
                        pool.indirect_dma_start(agg_d[m][u % 2],
                                                bass.IndirectOffsetOnAxis(ap=dOI[:, u:u + 1], axis=0),
                                                dO[:, u, 0:AW[m]], None, bounds_check=agg_last,
                                                oob_is_err=True, compute_op=ALU.add).then_inc(d_a[u % 2], 16)

                d_gather(r0)
                if m == 0:
                    d_gather(1)
                    d_add(0)
                with pool.Fori(2 if m == 0 else 1, R) as i:
                    d_gather(r0 + i)
                    d_add(r0 + i - 1)
                d_add(r0 + R - 1)

        @block.scalar
        def _(act):
            with nc.allow_non_contiguous_dma(reason="a few short vectors as columns"):
                for to, of in weight_loads:
                    act.dma_start(to, of).then_inc(s_w, 16)

            act.wait_ge(s_setup, 1)
            def normed(p, q, c):
                for k in range(2):
                    act.wait_ge(a_nm, c + k + 1)
                    act.wait_ge(a_sh[k], 16 * (p + 1))
                    for j in range(J):
                        act.activation(aH[:, k, j, :], aX[:, 2 * q + k, j, :], ACT.Relu, bias=aNM[:, k, 0, j:j + 1],
                                       scale=aRS[:, k, 0, j:j + 1]).then_inc(a_h, 1)

            def by_channel(p):
                for k in range(2):
                    act.wait_ge(a_tp, 2 * p + k + 1)
                    act.copy(aT[:, k, 0, :], ps[k][:, :]).then_inc(a_tc, 1)

            def normed_y(q, c):
                for k in range(2):
                    act.wait_ge(a_nm, c + k + 1)
                    yg = aYG[:, 2 * q + k, :, :]
                    for j in range(J):
                        act.activation(yg[:, j, C:2 * C], yg[:, j, 0:C], ACT.Relu,
                                       bias=aNM[:, k, 1 + q, j:j + 1], scale=aRS[:, k, 1 + q, j:j + 1]).then_inc(a_g, 1)

            def a_pair(p, q, n, first, last):
                c = 2 if first else 4 * p
                for m in range(M):
                    for k in range(2):
                        act.wait_ge(a_mm, 2 * M * p + 2 * m + k + 1)
                        act.activation(aS[:, k, :], ps[2 + k][:, :], ACT.Sigmoid,
                                       bias=GBC[:, m:m + 1]).then_inc(a_sg, 1)
                        if m:
                            act.wait_ge(a_bk, 2 * M * p + 2 * (m - 1) + k + 1)
                            act.wait_ge([a_s1, a_s2][m - 1][k], 16 * (p + 1))
                            act.copy(aO[:, k, m - 1, :, :], ps[4 + k][:, :].rearrange("p (j c) -> p j c", j=J)
                                     ).then_inc(a_o, 1)
                if not last:
                    normed(p + 1, 1 - q, c)
                    by_channel(p + 1)
                if not first:
                    normed_y(1 - q, c + 2 * (not last))

            normed(0, 0, 0)
            by_channel(0)
            a_rounds(act, a_pair, NA - 2)
            normed_y(1, 4 * (NA - 1) + 2)

            for m in range(M):
                def b_round(i, s, n, m=m):
                    r = m * R + i
                    act.wait_ge(b_arg, r + 1)
                    act.activation(bW4[:, :, :], bARG[:, :, :], ACT.Exp).then_inc(b_wx, 1)
                    for h in range(2):
                        act.activation(bXP[:, 4 * h:4 * h + 4, :], bXd[:, s, 4 * h:4 * h + 4, 0:C], ACT.Copy, bias=0.5)
                    for h in range(2):
                        act.wait_ge(b_rl, 2 * r + h + 1)
                        for u in range(4 * h, 4 * h + 4):
                            act.activation(bA[:, u, :], bTOT[:, u, 0:C], ACT.Copy,
                                           scale=bRL[:, 1, u:u + 1]).then_inc(b_a, 1)
                        act.wait_ge(b_at, 2 * r + h + 1)
                        act.copy(bAT[:, 4 * h:4 * h + 4, :], ps[h][:, :].rearrange("p (u c) -> p u c", u=4)
                                 ).then_inc(b_atc, 1)
                    for h in range(2):
                        act.wait_ge(b_h, 2 * r + h + 1)
                        act.activation(bTH[:, 4 * h:4 * h + 4, :], ps[6 - 2 * h][:, :].rearrange("p (u c) -> p u c", u=4),
                                       ACT.Tanh, scale=0.5).then_inc(b_th, 1)
                    if m == M - 1:
                        act.wait_ge(b_nr, i + 1)
                        for u in range(U):
                            act.activation(bO[:, u, C:2 * C], bO[:, u, 0:C], ACT.Relu, bias=bNR[:, u:u + 1],
                                           scale=bRS[:, 1, u:u + 1]).then_inc(b_out, 1)

                b_rounds(act, b_round)

            for m in range(M):
                def d_round(r, m=m):
                    for u in range(U):
                        act.wait_ge(d_acc, U * r + u + 1)
                        if not isinstance(r, int) or r > 0:
                            act.wait_ge(d_a[u % 2], 16 * ((U // 2) * (r - 1) + u // 2 + 1))
                        act.copy(dO[:, u, 0:AW[m]], ps[2 + u % 4][:, 0:AW[m]]).then_inc(d_o, 1)

                if m == 0:
                    d_round(0)
                with act.Fori(1 if m == 0 else 0, R) as i:
                    d_round(m * R + i)

                n0 = m * NT

                def turned(p, m=m, n0=n0):
                    for k in range(2):
                        act.wait_ge(e_tp, n0 + 2 * p + k + 1)
                        if m == 0:
                            act.wait_ge(e_se[k], 16 * (p + 1))
                            act.copy(eET[:, k, :], ps[6 + k][0:EA, :]).then_inc(e_tc, 1)
                        act.copy(eHT[:, k, :], ps[k][:, :]).then_inc(e_tc, 1)

                def e_pair(p, more, m=m, n0=n0):
                    for k in range(2):
                        for h in range(2):
                            act.wait_ge(e_z, 2 * (n0 + 2 * p + k) + h + 1)
                            act.activation(eZ[:, k, h, :], ps[2 + 2 * k + h][:, :], ACT.Relu,
                                           bias=BNT[:, m, h:h + 1], scale=BNS[:, m, h:h + 1]).then_inc(e_zr, 1)
                    if more:
                        turned(p + 1)
                    if m < M - 1:
                        for k in range(2):
                            act.wait_ge(e_v, n0 + 2 * p + k + 1)
                            act.activation(eO[:, k, :, :], eO[:, k, :, :], ACT.Relu).then_inc(e_o, 1)

                turned(0)
                with act.Fori(0, NA - 1) as i:
                    e_pair(i, True)
                e_pair(NA - 1, False)

        @block.tensor
        def _(pe):
            def cols(b, u):
                return ps[b][:, u * P:(u + 1) * P]

            pe.wait_ge(s_pool, 2)
            pe.wait_ge(s_rowf, 1)
            for k in range(3):
                for b in range(NB_):
                    mm = pe.transpose(ps[k][:, b * EB:(b + 1) * EB], rowF[:, k, b, :], ident[0:EB, 0:EB])
                mm.then_inc(s_pe, 1)
            pe.wait_ge(s_keys, 1)
            pe.matmul(ps[3][:, 0:ET], last_row[:, :], keys[:, 1, :], start=True, stop=True).then_inc(s_pe, 1)
            pe.wait_ge(s_meta, 1)
            pe.matmul(ps[2][:, 0:ET], last_row[:, :], META[:, 2, :], start=True, stop=True).then_inc(s_pe, 1)
            pe.wait_ge(s_w, 16 * NW)
            for m in range(M):
                mm = pe.transpose(ps[4][:, m * EA:(m + 1) * EA], ENC[:, m, :], ident[0:EA, 0:EA])
            mm.then_inc(s_pe, 1)
            pe.wait_ge(s_enct, 1)
            for m in range(M):
                mm = pe.matmul(ps[5 + m][0:EA, 0:H], ENCT[:, m, :], W1B[:, m, :], start=True, stop=True)
            mm.then_inc(s_pe, 1)
            pe.wait_ge(s_vc, 1)
            for q in range(2 * M):
                mm = pe.transpose(ps[q // 4][:, (q % 4) * P:(q % 4 + 1) * P], VC[:, q:q + 1].to_broadcast([P, P]),
                                  ident[:, :])
            mm.then_inc(s_pe, 1)
            with pe.Fori(0, R) as i:
                pe.wait_ge(s_cid, i + 1)
                for u in range(U):
                    b = 2 + u // 4
                    pe.transpose(cols(b, u % 4), dK[:, u:u + 1].to_broadcast([P, P]), ident[:, :]).then_inc(s_cnt, 1)

            pe.wait_ge(s_setup, 1)
            def a_turn(p):
                for k in range(2):
                    pe.wait_ge(a_h, J * (2 * p + k + 1))
                    for j in range(J):
                        mm = pe.transpose(ps[k][:, j * P:(j + 1) * P], aH[:, k, j, :], ident[:, :])
                    mm.then_inc(a_tp, 1)

            def a_mul(p, m, k):
                if m == 0:
                    pe.wait_ge(a_tc, 2 * p + k + 1)
                else:
                    pe.wait_ge(a_xT, 2 * M * p + 2 * (m - 1) + k + 1)
                pe.matmul(ps[2 + k][:, :], W[:, m, :], aT[:, k, m, :], start=True, stop=True).then_inc(a_mm, 1)

            def a_back(p, m, k):
                pe.wait_ge(a_xT, 2 * M * p + 2 * m + k + 1)
                if m:
                    pe.wait_ge(a_o, 4 * p + 2 * (m - 1) + k + 1)
                for j in range(J):
                    mm = pe.transpose(ps[4 + k][:, j * P:(j + 1) * P], aT[:, k, m + 1, j * P:(j + 1) * P], ident[:, :])
                mm.then_inc(a_bk, 1)

            def a_pair(p, q, n, first, last):
                for k in range(2):
                    a_mul(p, 0, k)
                for m in range(M):
                    for k in range(2):
                        if m < M - 1:
                            a_mul(p, m + 1, k)
                        a_back(p, m, k)
                if not last:
                    a_turn(p + 1)

            a_turn(0)
            a_rounds(pe, a_pair, NA - 2)

            bc_bank = [ps[7], ps[2], ps[3]]
            for m in range(M):
                def b_round(i, s, n, m=m):
                    r = m * R + i
                    pe.wait_ge(b_fm, r + 1)
                    for u in range(U):
                        pe.transpose(cols(u // 4, u % 4), bFM[:, 0, u:u + 1].to_broadcast([P, P]), ident[:, :]
                                     ).then_inc(b_d, 1)
                    pe.wait_ge(b_q, r + 1)
                    for u in range(U):
                        pe.transpose(cols(2 + u // 4, u % 4), bSB[:, 0, u:u + 1].to_broadcast([P, P]), ident[:, :]
                                     ).then_inc(b_e, 1)
                    pe.wait_ge(b_pr, r + 1)
                    pe.matmul(ps[7][:, 0:U], last_row[:, :], bPR[:, :], start=True, stop=True).then_inc(b_bn, 1)

                    def spread(u):
                        pe.wait_ge(b_tl, U * r + u + 1)
                        if u >= 3:
                            pe.wait_ge(b_cb, U * r + u - 2)
                        pe.matmul(bc_bank[u % 3][:, 0:C + 1], last_row[:, :], bTL[:, u, 0:C + 1],
                                  start=True, stop=True).then_inc(b_bc, 1)

                    for u in range(U):
                        pe.wait_ge(b_sw, U * r + u + 1)
                        if u >= 3:
                            pe.wait_ge(b_tl, U * r + u - 2)
                        pe.matmul(ps[4 + u % 3][:, 0:C + 1], bSW[:, u, :], bXs[:, s, u, 0:C + 1],
                                  start=True, stop=True).then_inc(b_acc, 1)
                        if u >= 3:
                            spread(u - 3)
                    for u in range(U - 3, U):
                        spread(u)
                    for h in range(2):
                        for u in range(4 * h, 4 * h + 4):
                            pe.wait_ge(b_a, U * r + u + 1)
                            mm = pe.transpose(cols(h, u % 4), bA[:, u, :], ident[:, :])
                        mm.then_inc(b_at, 1)
                        pe.wait_ge(b_atc, 2 * r + h + 1)
                        if h:
                            pe.wait_ge(b_tl, U * r + U - 1)
                        for u in range(4 * h, 4 * h + 4):
                            to = cols(6 - 2 * h, u % 4)
                            pe.matmul(to, ones_row[:, :], GBR[:, m, :], start=True, stop=False)
                            mm = pe.matmul(to, bAT[:, u, :], W[:, m, :], start=False, stop=True)
                        mm.then_inc(b_h, 1)

                b_rounds(pe, b_round)

            for m in range(M):
                def d_round(i, m=m):
                    r = m * R + i
                    pe.wait_ge(d_k, r + 1)
                    for u in range(U):
                        pe.transpose(cols(u // 4, u % 4), dK[:, u:u + 1].to_broadcast([P, P]), ident[:, :]
                                     ).then_inc(d_t, 1)
                    for u in range(U):
                        pe.wait_ge(d_g[u], 16 * (r + 1))
                        if m == 0 and u == 0:
                            pe.wait_ge(d_at, 16 * U * (i + 1))
                        pe.wait_ge(d_s, U * r + u + 1)
                        if not isinstance(r, int) or U * r + u >= 4:
                            pe.wait_ge(d_o, U * r + u - 3)
                        pe.matmul(ps[2 + u % 4][:, 0:AW[m]], dS[:, u, :], dG[:, u, 0:AW[m]], start=True, stop=True
                                  ).then_inc(d_acc, 1)

                if m == 0:
                    d_round(0)
                with pe.Fori(1 if m == 0 else 0, R) as i:
                    d_round(i)
                n0 = m * NT
                tc = 2 if m == 0 else 1
                tc0 = 0 if m == 0 else NT

                def turn(p, m=m, n0=n0):
                    for k in range(2):
                        pe.wait_ge(e_s, n0 + 2 * p + k + 1)
                        if m == 0:
                            for j in range(J):
                                pe.transpose(ps[6 + k][0:EA, j * P:(j + 1) * P], eE[:, k, j, :], ident[:, :])
                        for j in range(J):
                            mm = pe.transpose(ps[k][:, j * P:(j + 1) * P], eS[:, k, j, :], ident[:, :])
                        mm.then_inc(e_tp, 1)

                def e_pair(p, more, m=m, n0=n0, tc=tc, tc0=tc0):
                    for k in range(2):
                        pe.wait_ge(e_tc, tc0 + tc * (n0 + 2 * p + k + 1))
                        if m:
                            pe.wait_ge(e_et[k], 16 * ((m - 1) * NA + p + 1))
                        for h in range(2):
                            z = ps[2 + 2 * k + h][:, :]
                            pe.matmul(z, W1X[:, m, h * P:(h + 1) * P], eHT[:, k, :], start=True, stop=False)
                            pe.matmul(z, EP[:, m, h * P:(h + 1) * P], eET[:, k, :], start=False, stop=True
                                      ).then_inc(e_z, 1)
                    if more:
                        turn(p + 1)
                    for k in range(2):
                        pe.wait_ge(e_zr, 2 * (n0 + 2 * p + k + 1))
                        if not more:
                            pe.wait_ge(e_v, n0 + 2 * p + k - 1)
                        if m == 0 and more:
                            pe.wait_ge(e_tc, 2 * (2 * p + 2 + k + 1))
                        for j in range(J):
                            for h in range(2):
                                mm = pe.matmul(ps[6 + k][:, j * P:(j + 1) * P], eZ[:, k, h, j * P:(j + 1) * P],
                                               W2[:, m, h, :], start=(h == 0), stop=(h == 1))
                        mm.then_inc(e_y, 1)

                turn(0)
                with pe.Fori(0, NA - 1) as i:
                    e_pair(i, 1)
                e_pair(NA - 1, 0)

        @block.vector
        def _(v):
            done = [0]

            def link(ins):
                done[0] += 1
                ins.then_inc(s_v, 1)
                v.wait_ge(s_v, done[0])

            v.wait_ge(s_idx, 16 * n_idx[0])
            v.tensor_copy(rowF[:, :, :, :], rowI[:, :, :, :]).then_inc(s_rowf, 1)
            v.wait_ge(s_pe, 3)
            for k in range(3):
                ins = v.tensor_copy(keys[:, k, :], ps[k][:, 0:ET])
            ins.then_inc(s_keys, 1)
            v.wait_ge(s_keys, 1)
            v.wait_ge(s_pool, 2)
            v.tensor_copy(META[:, 0, :], keys[:, 1, :])
            v.memset(META[:, 1, 0:1], 1.0)
            v.tensor_scalar(IDX[:, 0, 0:ET], keys[:, 0, :], 0.0, None, ALU.max)
            v.tensor_scalar(IDX[:, 1, 0:ET], keys[:, 1, :], 0.0, None, ALU.max)
            v.tensor_scalar(tmp[:, 0, :], keys[:, 1, :], 0.0, 2.0, ALU.max, ALU.mult)
            link(v.tensor_tensor(tmp[:, 1, :], keys[:, 1, :], keys[:, 2, :], ALU.not_equal))
            v.tensor_scalar(IDX[:, 2, 0:ET], tmp[:, 0, :], 1.0, None, ALU.add)
            link(v.scalar_tensor_tensor(out=cnt[:, :], in0=keys[:, 1, :], scalar=0.0, in1=tmp[:, 1, :],
                                        op0=ALU.is_ge, op1=ALU.mult))
            link(v.scalar_tensor_tensor(out=tmp[:, 0, :], in0=keys[:, 1, :], scalar=-float(SKIP), in1=cnt[:, :],
                                        op0=ALU.add, op1=ALU.mult))
            v.tensor_scalar(IDX[:, 3, 0:ET], tmp[:, 0, :], float(SKIP), None, ALU.add)
            v.wait_ge(s_pe, 4)
            link(v.tensor_tensor(META[:, 1, 1:ET], keys[:, 1, 1:ET], ps[3][:, 0:ET - 1], ALU.not_equal))
            v.tensor_scalar(META[:, 2, :], META[:, 1, :], BIG, None, ALU.mult).then_inc(s_meta, 1)
            v.wait_ge(s_pe, 5)
            v.tensor_copy(META[:, 3, :], ps[2][:, 0:ET])

            v.wait_ge(s_w, 16 * NW)
            v.wait_ge(s_pe, 6)
            v.tensor_copy(ENCT[:, :, :], ps[4][:, 0:M * EA].rearrange("p (m a) -> p m a", m=M)).then_inc(s_enct, 1)
            for m in range(M):
                for w in range(2):
                    ins = v.tensor_tensor_reduce(bTL[:, 2 * m + w, 0:C], W[:, m, :], AR[:, w, m, :], 1.0, 0.0, ALU.mult, ALU.add,
                                                 VC[:, 2 * m + w:2 * m + w + 1])
            ins.then_inc(s_vc, 1)
            v.wait_ge(s_pe, 7)
            for m in range(M):
                v.tensor_copy(EP[:, m, :], ps[5 + m][0:EA, 0:H])
            v.wait_ge(s_pool, 4)
            link(v.tensor_tensor(BNS[:, :, :], BN[:, 0, :, :], BNT[:, :, :], ALU.mult))
            link(v.tensor_tensor(BN[:, 4, :, :], BN[:, 4, :, :], BN[:, 2, :, :], ALU.subtract))
            link(v.tensor_tensor(BN[:, 4, :, :], BN[:, 4, :, :], BNS[:, :, :], ALU.mult))
            v.tensor_tensor(BNT[:, :, :], BN[:, 4, :, :], BN[:, 1, :, :], ALU.add)
            v.wait_ge(s_pe, 8)
            for b in range(2):
                n = min(4, 2 * M - 4 * b)
                v.tensor_copy(VR[:, 4 * b:4 * b + n, :], ps[b][:, 0:n * P].rearrange("p (q c) -> p q c", q=n))

            with v.Fori(0, R) as i:
                v.tensor_copy(dK[:, :], keys[:, 0, bass.ds(i * U, U)]).then_inc(s_cid, 1)
                for u in range(U):
                    if u % 4 == 0:
                        v.wait_ge(s_cnt, U * i + u + 4)
                    ins = v.scalar_tensor_tensor(out=bTL[:, u, 0:C], in0=ps[2 + u // 4][:, (u % 4) * P:(u % 4 + 1) * P],
                                                 scalar=dK[:, u:u + 1], in1=later[:, :], op0=ALU.is_equal,
                                                 op1=ALU.mult, accum_out=bNM[:, u:u + 1])
                ins.then_inc(s_cg, 1)
                v.wait_ge(s_cg, i + 1)
                v.tensor_copy(cnt[:, bass.ds(i * U, U)], bNM[:, :]).then_inc(s_cw, 1)
            v.wait_ge(s_cw, R)
            link(v.tensor_scalar(tmp[:, 0, :], cnt[:, :], 0.0, None, ALU.is_equal))
            link(v.scalar_tensor_tensor(out=tmp[:, 1, :], in0=keys[:, 0, :], scalar=0.0, in1=tmp[:, 0, :],
                                        op0=ALU.is_ge, op1=ALU.mult))
            link(v.scalar_tensor_tensor(out=tmp[:, 0, :], in0=keys[:, 0, :], scalar=trash_id[:, 0:1],
                                        in1=tmp[:, 1, :], op0=ALU.subtract, op1=ALU.mult))
            link(v.tensor_scalar(IDX[:, 4, 0:ET], tmp[:, 0, :], trash_id[:, 0:1], None, ALU.add))
            v.tensor_copy(bGI[:, 0, :, :], IDX[:, 0:2, 0:U]).then_inc(b_gi, 1)
            v.wait_ge(b_gi, 1)
            v.sem_inc(s_setup, 1)

            def stats(buf, k, w, slot):
                for j in range(J):
                    ins = v.bn_stats(aBS[:, k, w, j, :], buf[:, slot, j, 0:C])
                return ins

            def aggr(k, w):
                for j in range(J):
                    ins = v.bn_aggr(aMV[:, k, w, j, :], aBS[:, k, w, j, :])
                ins.then_inc(a_mv, 1)

            def shift(k, w, n):
                v.wait_ge(a_rs, n)
                v.scalar_tensor_tensor(out=aNM[:, k, w, :], in0=aMV[:, k, w, :, 0], scalar=-1.0, in1=aRS[:, k, w, :],
                                       op0=ALU.mult, op1=ALU.mult).then_inc(a_nm, 1)

            def a_stats(buf, w, q, c, loads=None):
                for k in range(2):
                    if loads is not None:
                        v.wait_ge(a_x[2 * q + k], 16 * (loads + 1))
                    ins = stats(buf, k, w, 2 * q + k)
                ins.then_inc(a_bs, 1)
                v.wait_ge(a_bs, c + 1)
                v.sem_inc(s_gate, 1)
                for k in range(2):
                    aggr(k, w)

            def add(p, m, k):
                v.wait_ge(a_sg, 2 * M * p + 2 * m + k + 1)
                if m:
                    v.wait_ge(a_xT, 2 * M * p + 2 * (m - 1) + k + 1)
                else:
                    v.wait_ge(a_tc, 2 * p + k + 1)
                v.tensor_tensor(aT[:, k, m + 1, :], aT[:, k, m, :], aS[:, k, :], ALU.add).then_inc(a_xT, 1)

            def a_pair(p, q, n, first, last):
                c = 2 if first else 4 * p
                for k in range(2):
                    add(p, 0, k)
                if not last:
                    a_stats(aX, 0, 1 - q, c // 2 if first else 2 * p, n + q)
                for k in range(2):
                    add(p, 1, k)
                if not first:
                    v.wait_ge(a_y, 2 * p)
                    a_stats(aYG, 2 - q, 1 - q, 2 * p + (not last))
                if not last:
                    for k in range(2):
                        shift(k, 0, c + k + 1)
                for k in range(2):
                    add(p, 2, k)
                if not first:
                    for k in range(2):
                        shift(k, 2 - q, c + 2 * (not last) + k + 1)
                for k in range(2):
                    v.wait_ge(a_bk, 2 * M * p + 2 * (M - 1) + k + 1)
                    v.wait_ge(a_sy[2 * q + k], 16 * (n + 1))
                    v.tensor_tensor(aYG[:, 2 * q + k, :, 0:C], ps[4 + k][:, :].rearrange("p (j c) -> p j c", j=J),
                                    aX[:, 2 * q + k, :, :], ALU.add).then_inc(a_y, 1)

            a_stats(aX, 0, 0, 0, 0)
            for k in range(2):
                shift(k, 0, k + 1)
            a_rounds(v, a_pair, NA - 2)
            v.wait_ge(a_y, 2 * NA)
            a_stats(aYG, 2, 1, 2 * (NA - 1) + 1)
            for k in range(2):
                shift(k, 2, 4 * (NA - 1) + 2 + k + 1)

            def steps(s, base, per):
                n = [0]

                def step(ins, wait=True):
                    n[0] += 1
                    ins.then_inc(s, 1)
                    if wait:
                        v.wait_ge(s, base + n[0])
                    return n[0] == per
                return step

            for m in range(M):
                vs, vd = VR[:, 2 * m, :], VR[:, 2 * m + 1, :]

                def b_round(i, s, n, m=m, vs=vs, vd=vd):
                    r = m * R + i
                    step = steps(b_v, b_base[m] + i * b_per[m], b_per[m])
                    v.tensor_copy(bNC[:, 0:1], bNC[:, U:U + 1])
                    v.tensor_copy(bFM[:, :, :], META[:, :, bass.ds(i * U, U)]).then_inc(b_fm, 1)
                    v.wait_ge(b_fm, r + 1)
                    for u in range(U):
                        v.wait_ge(b_g[s][u], 32 * (m * RS[s] + n + 1))
                        v.tensor_tensor_reduce(bTL[:, u, 0:C], bXs[:, s, u, 0:C], vs, 1.0, 0.0, ALU.mult, ALU.add,
                                               bDT[:, 0, u:u + 1])
                        v.tensor_tensor_reduce(bTOT[:, u, 0:C], bXd[:, s, u, 0:C], vd, 1.0, 0.0, ALU.mult, ALU.add,
                                               bDT[:, 1, u:u + 1])
                        v.tensor_tensor_reduce(bSW[:, u, :], bXd[:, s, u, 0:C], vs, 1.0, 0.0, ALU.mult, ALU.add,
                                               bDT[:, 2, u:u + 1])
                        if u == 0:
                            v.tensor_copy(bGI[:, 1 - s, :, :], IDX[:, 0:2, bass.ds(i * U + U, U)]).then_inc(b_gi, 1)
                    for u in range(U):
                        if u % 4 == 0:
                            v.wait_ge(b_d, U * r + u + 4)
                        v.tensor_scalar(bNE[:, u, :], ps[u // 4][:, (u % 4) * P:(u % 4 + 1) * P], bFM[:, 0, u:u + 1], BIG,
                                        ALU.not_equal, ALU.mult).then_inc(b_ne, 1)
                    v.wait_ge(b_ne, U * (r + 1))
                    v.scalar_tensor_tensor(out=bNX[:, 0, :], in0=bDT[:, 0, :], scalar=-1.0, in1=bDT[:, 1, :],
                                           op0=ALU.mult, op1=ALU.subtract)
                    step(v.scalar_tensor_tensor(out=bNX[:, 1, :], in0=bDT[:, 2, :], scalar=-1.0, in1=bDT[:, 1, :],
                                                op0=ALU.mult, op1=ALU.subtract))
                    v.scalar_tensor_tensor(out=bSB[:, 0:2, :], in0=bNX[:, :, :], scalar=SLOPE, in1=bNX[:, :, :],
                                           op0=ALU.mult, op1=ALU.min).then_inc(b_q, 1)
                    for u in range(U):
                        if u % 4 == 0:
                            v.wait_ge(b_e, U * r + u + 4)
                            v.sem_inc(s_gate, 1)
                        v.tensor_tensor_reduce(bTL[:, u, 0:P], bNE[:, u, :], ps[2 + u // 4][:, (u % 4) * P:(u % 4 + 1) * P], 1.0,
                                               BIG, ALU.add, ALU.min, bNM[:, u:u + 1]).then_inc(b_eu, 1)
                    v.wait_ge(b_eu, U * (r + 1))
                    v.tensor_tensor(bPR[:, :], bNM[:, :], bSB[:, 1, :], ALU.min).then_inc(b_pr, 1)
                    v.wait_ge(b_bn, r + 1)
                    step(v.tensor_tensor_scan(out=bNC[:, 1:U + 1], data0=bFM[:, 3, :], data1=ps[7][:, 0:U],
                                              initial=bNC[:, 0:1], op0=ALU.add, op1=ALU.min))
                    step(v.tensor_tensor(bSB[:, 2:4, :], bFM[:, 2:4, :],
                                         bNC[:, 0:U].unsqueeze(1).to_broadcast([P, 2, U]), ALU.add))
                    step(v.tensor_tensor(bMX[:, :], bPR[:, :], bSB[:, 2, :], ALU.min))
                    v.tensor_tensor(bARG[:, 0:3, :], bMX[:, :].unsqueeze(1).to_broadcast([P, 3, U]), bSB[:, 0:3, :],
                                    ALU.subtract)
                    v.tensor_tensor(bARG[:, 3, :], bNC[:, 1:U + 1], bSB[:, 3, :], ALU.subtract).then_inc(b_arg, 1)
                    v.wait_ge(b_wx, r + 1)
                    step(v.tensor_tensor(bWS[:, :], bW4[:, 1, :], bFM[:, 1, :], ALU.mult))

                    def within(u):
                        v.wait_ge(b_acc, U * r + u + 1)
                        v.scalar_tensor_tensor(out=bTL[:, u, 0:C + 1], in0=bXd[:, s, u, 0:C + 1], scalar=bWS[:, u:u + 1],
                                               in1=ps[4 + u % 3][:, 0:C + 1], op0=ALU.mult, op1=ALU.add).then_inc(b_tl, 1)

                    def join(u):
                        v.wait_ge(b_bc, U * r + u + 1)
                        v.wait_ge(b_cb, U * r + u)
                        v.scalar_tensor_tensor(out=bTOT[:, u, 0:C + 1], in0=bCB[:, u, 0:C + 1], scalar=bW4[:, 2, u:u + 1],
                                               in1=bTL[:, u, 0:C + 1], op0=ALU.mult, op1=ALU.add).then_inc(b_tot, 1)
                        v.scalar_tensor_tensor(out=bCB[:, (u + 1) % U, 0:C + 1], in0=bCB[:, u, 0:C + 1],
                                               scalar=bW4[:, 3, u:u + 1], in1=[ps[7], ps[2], ps[3]][u % 3][:, 0:C + 1],
                                               op0=ALU.mult, op1=ALU.add).then_inc(b_cb, 1)
                        if u % 4 == 3:
                            v.wait_ge(b_tot, U * r + u + 1)
                            step(v.tensor_scalar(bRL[:, 0, u - 3:u + 1], bTOT[:, u - 3:u + 1, C], EPS_SM, None, ALU.add))
                            v.reciprocal(bRL[:, 1, u - 3:u + 1], bRL[:, 0, u - 3:u + 1]).then_inc(b_rl, 1)

                    for u in range(U + 4):
                        if u < U:
                            v.tensor_scalar(bSW[:, u, :], bNE[:, u, :], 0.0, bW4[:, 0, u:u + 1], ALU.is_equal,
                                            ALU.mult).then_inc(b_sw, 1)
                        if 2 <= u < U + 2:
                            within(u - 2)
                        if u >= 4:
                            join(u - 4)
                    if not isinstance(r, int) or r > 0:
                        for u in range(U):
                            v.wait_ge(b_sc[u], 16 * r)
                    v.tensor_copy(bOI[:, :], IDX[:, 3, bass.ds(i * U, U)]).then_inc(b_oi, 1)
                    for h in range(2):
                        v.wait_ge(b_th, 2 * r + h + 1)
                        ins = v.scalar_tensor_tensor(out=bO[:, 4 * h:4 * h + 4, 0:C], in0=bTH[:, 4 * h:4 * h + 4, :],
                                                     scalar=0.5, in1=bXP[:, 4 * h:4 * h + 4, :], op0=ALU.mult, op1=ALU.add)
                        if m < M - 1:
                            ins.then_inc(b_out, 4)
                    if m < M - 1:
                        v.wait_ge(b_out, U * (r + 1))
                    else:
                        step(ins)
                        for u in range(U):
                            v.wait_ge(b_gx[u], 16 * (i + 1))
                        step(v.tensor_tensor(bO[:, :, 0:C], bO[:, :, 0:C], bXx[:, :, :], ALU.add))
                        for u in range(U):
                            ins = v.bn_stats(bBS[:, u, :], bO[:, u, 0:C])
                        step(ins)
                        v.sem_inc(s_gate, 1)
                        for u in range(U):
                            v.bn_aggr(bMV[:, u, :], bBS[:, u, :]).then_inc(b_mv, 1)
                        v.wait_ge(b_rs, i + 1)
                        v.scalar_tensor_tensor(out=bNR[:, :], in0=bMV[:, :, 0], scalar=-1.0, in1=bRS[:, 1, :],
                                               op0=ALU.mult, op1=ALU.mult).then_inc(b_nr, 1)

                b_rounds(v, b_round)
                if m < M - 1:
                    v.tensor_copy(bGI[:, 0, :, :], IDX[:, 0:2, 0:U]).then_inc(b_gi, 1)

            for u in range(U):
                v.wait_ge(b_sc[u], 16 * M * R)
            v.wait_ge(b_out, U * M * R)
            v.memset(dG[:, :, C + DE:C + EA], 1.0)
            link(v.memset(dG[:, :, C:C + DE], 0.0))
            v.sem_inc(s_dclr, 1)
            for m in range(M):
                gi = 2 if m == 0 else 1
                v.tensor_copy(dGI[:, :], IDX[:, gi, 0:U]).then_inc(d_gi, 1)

                def d_round(i, m=m, gi=gi):
                    r = m * R + i
                    v.tensor_copy(dK[:, :], keys[:, 0, bass.ds(i * U, U)]).then_inc(d_k, 1)
                    v.wait_ge(d_k, r + 1)
                    for u in range(U):
                        if u % 4 == 0:
                            v.wait_ge(d_t, U * r + u + 4)
                        v.tensor_scalar(dS[:, u, :], ps[u // 4][:, (u % 4) * P:(u % 4 + 1) * P], dK[:, u:u + 1], None,
                                        ALU.is_equal).then_inc(d_s, 1)
                    v.wait_ge(d_s, U * (r + 1))
                    for u in range(U):
                        v.wait_ge(d_g[u], 16 * (r + 1))
                    v.tensor_copy(dGI[:, :], IDX[:, gi, bass.ds(i * U + U, U)]).then_inc(d_gi, 1)
                    if not isinstance(r, int) or r > 0:
                        for b in range(2):
                            v.wait_ge(d_a[b], 16 * (U // 2) * r)
                    v.tensor_copy(dOI[:, :], IDX[:, 4, bass.ds(i * U, U)]).then_inc(d_oi, 1)

                if m == 0:
                    d_round(0)
                with v.Fori(1 if m == 0 else 0, R) as i:
                    d_round(i)

                n0 = m * NT

                def add_up(p, m=m, n0=n0):
                    for k in range(2):
                        v.wait_ge(e_in[k], 48 * (m * NA + p + 1))
                        v.tensor_tensor(eA[:, k, 0, :, 0:AW[m]], eA[:, k, 0, :, 0:AW[m]], eA[:, k, 1, :, 0:AW[m]],
                                        ALU.add).then_inc(e_a, 1)
                    for k in range(2):
                        v.wait_ge(e_a, n0 + 2 * p + k + 1)
                        if not isinstance(p, int):
                            v.wait_ge(e_tp, n0 + 2 * p + k - 1)
                        if m == 0:
                            v.tensor_tensor(eE[:, k, :, :], eA[:, k, 0, :, C:C + EA], self_ea[:, :, :], ALU.add)
                        v.tensor_tensor(eS[:, k, :, :], eA[:, k, 0, :, 0:C], eG[:, k, :, :], ALU.add
                                        ).then_inc(e_s, 1)

                def finish(p, m=m, n0=n0):
                    bias = B2[:, m, :].unsqueeze(1).to_broadcast([P, J, C])
                    for k in range(2):
                        v.wait_ge(e_y, n0 + 2 * p + k + 1)
                        v.wait_ge(e_st[k], 16 * (m * NA + p + 1))
                        v.tensor_tensor(eO[:, k, :, :], ps[6 + k][:, :].rearrange("p (j c) -> p j c", j=J), bias,
                                        ALU.add).then_inc(e_v, 1)
                    if m == M - 1:
                        for k in range(2):
                            v.wait_ge(e_v, n0 + 2 * p + k + 1)
                            v.wait_ge(e_yi[k], 16 * (p + 1))
                            v.tensor_tensor(eO[:, k, :, :], eO[:, k, :, :], eY[:, k, :, :], ALU.add).then_inc(e_o, 1)

                add_up(0)
                with v.Fori(0, NA - 1) as i:
                    add_up(i + 1)
                    finish(i)
                finish(NA - 1)


_INS = ["x", "src", "dst", "edge_attr_16", "L0_gnn_Ws", "L0_gnn_att_src", "L0_gnn_att_dst", "L0_gnn_bias",
        "L1_gnn_enc_w0", "L1_gnn_enc_b0", "L1_gnn_w1_0", "L1_gnn_b1_0", "L1_gnn_g0", "L1_gnn_be0", "L1_gnn_rm0",
        "L1_gnn_rv0", "L1_gnn_w2_0", "L1_gnn_b2_0", "L1_gnn_enc_w", "L1_gnn_enc_b", "L1_gnn_w1", "L1_gnn_b1",
        "L1_gnn_g", "L1_gnn_be", "L1_gnn_rm", "L1_gnn_rv", "L1_gnn_w2", "L1_gnn_b2"]


def kernel(**inputs):
    import numpy as _np
    import concourse.bacc as _bacc
    from concourse import mybir as _mybir
    from concourse.bass_utils import run_bass_kernel_spmd as _run

    nc = _bacc.Bacc("TRN2", target_bir_lowering=False, num_devices=1)
    arrays, args = {}, []
    for name in _INS:
        a = _np.ascontiguousarray(inputs[name])
        arrays[f"in_{name}_dram"] = a
        args.append(nc.dram_tensor(f"in_{name}_dram", a.shape, _mybir.dt.from_np(a.dtype), kind="ExternalInput").ap())
    shape = inputs["x"].shape
    args.append(nc.dram_tensor("out_0_dram", shape, _mybir.dt.float32, kind="ExternalOutput").ap())
    gnn_program(nc, *args)
    r = _run(nc, [arrays], core_ids=[0])
    return r.results[0]["out_0_dram"]
```

```python
from contextlib import ExitStack

import concourse.bass as bass
from concourse import mybir

ALU = mybir.AluOpType
ACT = mybir.ActivationFunctionType
F32 = mybir.dt.float32
I32 = mybir.dt.int32
BF16 = mybir.dt.bfloat16

P = 128
J = 4
TN = P * J
U = 8
M = 3
BIG = 1e30
EPS_LN = 1e-5
EPS_BN = 1e-5
EPS_SM = 1e-16
SLOPE = 0.2
C = 128
H = 256
DE = 16
EA = DE + 1
A_PARTS = (0, 0, 0, 1, 1, 2)
W_PARTS = (0, 1, 2, 0, 1, 0)
KA = EA * len(A_PARTS)
CP = 132


def gnn_program(nc, x, src, dst, attr, Ws, a_src, a_dst, gat_b, enc_w0, enc_b0, w1_0, b1_0, g_0, be_0, rm_0,
                rv_0, w2_0, b2_0, enc_w, enc_b, w1, b1, g, be, rm, rv, w2, b2, out):
    N = x.shape[0]
    E = src.shape[0]
    NT = -(-N // TN)
    NT += -NT % 4
    LAST = N - TN
    R = -(-E // (P * U))
    R += 1 - R % 2
    ET = R * U
    ETP = ET + 2 * U
    NB_ = 4
    EB = ET // NB_
    NR = (NT + 1) * TN
    TRASH = NR - P
    SKIP = 2 * N
    assert EB * NB_ == ET and EB <= P and R >= 7 and NT >= 16

    def dram(name, shape, dt=F32):
        return nc.dram_tensor(name, shape, dt, kind="Internal").ap()

    h0_d = dram("h0_d", (N, C))
    x1_d = dram("x1_d", (N, C))
    xx2_d = dram("xx2_d", (N, 2 * C))
    yg_d = dram("yg_d", (N, 2 * C))
    g1_d = dram("g1_d", (N, C))
    g2_d = dram("g2_d", (N, C))
    AW = [C + EA, C, C]
    agg_d = [[dram(f"agg{m}{b}_d", (NR, AW[m])) for b in range(2)] for m in range(M)]
    eaT_d = dram("eaT_d", (NT, KA, TN), BF16)
    x2_rows = xx2_d.rearrange("n (t c) -> (n t) c", t=2)
    gat_src = [h0_d, x1_d, x2_rows]
    gat_dst = [h0_d, x1_d, xx2_d]
    gat_out = [x1_d, x2_rows, yg_d]
    gin_in = [yg_d.rearrange("n (t c) -> (n t) c", t=2), g1_d, g2_d]

    with ExitStack() as ctx:
        def sb(name, shape, dt=F32):
            return ctx.enter_context(nc.sbuf_tensor(name, shape, dt))

        def sem(name):
            return ctx.enter_context(nc.semaphore(name))

        def sems(name, n):
            return [sem(f"{name}{k}") for k in range(n)]

        ps = [ctx.enter_context(nc.psum_tensor(f"ps{k}", [P, 512], F32)) for k in range(8)]

        ident = sb("ident", [P, P])
        last_row = sb("last_row", [P, P])
        later = sb("later", [P, P])
        ones_row = sb("ones_row", [1, P])
        zeros = sb("zeros", [P, J * (C + EA)])
        mhalf = sb("mhalf", [P, U])
        trash_id = sb("trash_id", [P, 1])
        self_ea = sb("self_ea", [P, J, EA])
        W = sb("W", [P, M, C])
        W1X = sb("W1X", [P, M, H])
        W1B = sb("W1B", [P, M, H])
        W2 = sb("W2", [P, M, 2, C])
        ENC = sb("ENC", [EA, M, C])
        ENCT = sb("ENCT", [P, M, EA])
        EP = sb("EP", [EA, M, H])
        EPP = sb("EPP", [EA, 3, M, H], BF16)
        EPS = sb("EPS", [KA, M, H], BF16)
        BN = sb("BN", [P, 5, M, 2])
        BNS = sb("BNS", [P, M, 2])
        BNT = sb("BNT", [P, M, 2])
        B2 = sb("B2", [P, M, C])
        GBC = sb("GBC", [P, M])
        GBR = sb("GBR", [1, M, C])
        AR = sb("AR", [P, 2, M, C])
        VC = sb("VC", [P, 2 * M])
        VR = sb("VR", [P, 2 * M, C])

        rowI = sb("rowI", [EB, 3, NB_, P], I32)
        keys = sb("keys", [P, 3, ET])
        META = sb("META", [P, 4, ET])
        cnt = sb("cnt", [P, ET])
        tmp = sb("tmp", [P, 2, ET])
        IDX = sb("IDX", [P, 7, ETP], I32)

        s_w = sem("s_w")
        s_idx = sem("s_idx")
        s_pool = sem("s_pool")
        s_rowf, s_keys, s_meta, s_enct, s_vc, s_setup, s_pe, s_dclr = [
            sem(n) for n in ["s_rowf", "s_keys", "s_meta", "s_enct", "s_vc", "s_setup", "s_pe", "s_dclr"]]
        s_v = sem("s_v")
        s_gate = sem("s_gate")
        n_idx = [0]

        weight_loads = [
            (W[:, :, :], Ws.rearrange("m k c -> k m c")),
            (W1X[:, 0, :], w1_0), (W1B[:, 0, :], w1_0),
            (W2[:, 0, :, :], w2_0.rearrange("(h k) c -> k h c", h=2)),
            (ENC[0:DE, 0, :], enc_w0), (ENC[DE:EA, 0, :], enc_b0.rearrange("(o c) -> o c", o=1)),
            (GBC[:, :], gat_b.rearrange("m c -> c m")), (GBR[:, :, :], gat_b.rearrange("(o m) c -> o m c", o=1)),
            (B2[:, 0, :], b2_0.rearrange("(o c) -> o c", o=1).to_broadcast([P, C])),
        ]
        for m in range(1, M):
            weight_loads += [
                (W1X[:, m, :], w1[m - 1, 0:C, :]), (W1B[:, m, :], w1[m - 1, C:2 * C, :]),
                (W2[:, m, :, :], w2[m - 1].rearrange("(h k) c -> k h c", h=2)),
                (ENC[0:DE, m, :], enc_w[m - 1]), (ENC[DE:EA, m, :], enc_b[m - 1:m, :]),
                (B2[:, m, :], b2[m - 1:m, :].to_broadcast([P, C])),
            ]
        for m in range(M):
            weight_loads += [(AR[:, 0, m, :], a_src[m:m + 1, :].to_broadcast([P, C])),
                             (AR[:, 1, m, :], a_dst[m:m + 1, :].to_broadcast([P, C]))]
            for q, (v0, v) in enumerate(((g_0, g), (be_0, be), (rm_0, rm), (rv_0, rv), (b1_0, b1))):
                vec = v0 if m == 0 else v[m - 1]
                weight_loads.append((BN[:, q, m, :], vec.rearrange("(h p) -> p h", p=P)))
        NW = len(weight_loads)

        block = ctx.enter_context(nc.Block())

        aX = sb("aX", [P, 4, J, C])
        aH = sb("aH", [P, 2, J, C])
        aT = sb("aT", [P, 2, 4, TN])
        aS = sb("aS", [P, 2, TN])
        aO = sb("aO", [P, 2, 2, J, C])
        aYG = sb("aYG", [P, 4, J, 2 * C])
        aBS = sb("aBS", [P, 2, 3, J, 6])
        aMV = sb("aMV", [P, 2, 3, J, 2])
        aRS = sb("aRS", [P, 2, 3, J])
        aNM = sb("aNM", [P, 2, 3, J])
        aVE = sb("aVE", [P, 2, 3, J])
        a_x = sems("a_x", 4)
        a_mv, a_rs, a_nm, a_h, a_tp, a_tc, a_mm, a_sg, a_xT, a_bk, a_o, a_y, a_g, a_pv, a_bs = [
            sem(n) for n in ["a_mv", "a_rs", "a_nm", "a_h", "a_tp", "a_tc", "a_mm", "a_sg", "a_xT", "a_bk", "a_o",
                             "a_y", "a_g", "a_pv", "a_bs"]]
        a_sh = sems("a_sh", 2)
        a_s1 = sems("a_s1", 2)
        a_s2 = sems("a_s2", 2)
        a_xc = sems("a_xc", 4)
        a_sy = sems("a_sy", 4)
        NA = NT // 2

        def a_rounds(engine, a_pair, end):
            for p in range(3):
                a_pair(p, p % 2, p // 2, p == 0, False)
            with engine.Fori(1, end // 2) as i:
                a_pair(2 * i + 1, 1, i, False, False)
                a_pair(2 * i + 2, 0, i + 1, False, False)
            for p in range(2 * (end // 2) + 1, NA):
                a_pair(p, p % 2, p // 2, False, p == NA - 1)

        bXs = sb("bXs", [P, 2, U, CP])
        bXd_flat = sb("bXd", [P, 2 * U * (C + CP)])
        bXd = bXd_flat[:, :].rearrange("p (s u c) -> p s u c", s=2, u=U)
        bNE = sb("bNE", [P, U, P])
        bSW = sb("bSW", [P, U, P])
        bTL = sb("bTL", [P, U, CP])
        bTOT = sb("bTOT", [P, U, CP])
        bCB = sb("bCB", [P, U, CP])
        bA = sb("bA", [P, U, C])
        bAT = sb("bAT", [P, U, C])
        bXP = sb("bXP", [P, U, C])
        bTH = sb("bTH", [P, U, C])
        bO = sb("bO", [P, U, 2 * C])
        rowF = bO[0:EB, :, :].rearrange("p u c -> p (u c)")[:, 0:3 * NB_ * P].rearrange("p (k b c) -> p k b c", k=3, b=NB_)
        bFM = sb("bFM", [P, 4, U])
        bGI = sb("bGI", [P, 2, 2, U], I32)
        bOs = [bO, aT[:, :, :, :].rearrange("p k m n -> p (k m n)")[:, 0:2 * U * C].rearrange("p (u c) -> p u c", u=U)]
        bOI = sb("bOI", [P, 2, U], I32)
        bDT = sb("bDT", [P, 3, U])
        bNX = sb("bNX", [P, 2, U])
        bSB = sb("bSB", [P, 4, U])
        bNM = sb("bNM", [P, U])
        bPR = sb("bPR", [P, U])
        bNC = sb("bNC", [P, U + 1])
        bMX = sb("bMX", [P, U])
        bARG = sb("bARG", [P, 4, U])
        bW4 = sb("bW4", [P, 4, U])
        bWS = sb("bWS", [P, U])
        bRL = sb("bRL", [P, 2, U])
        bBS = sb("bBS", [P, U, 6])
        bMV = sb("bMV", [P, U, 2])
        bRS = sb("bRS", [P, 2, U])
        bNR = sb("bNR", [P, U])
        bNG = sb("bNG", [P, U])
        b_g = [sems(f"b_g{s}", U) for s in range(2)]
        RS = [(R + 1) // 2, R // 2]
        b_sc = [sems(f"b_sc{s}", U) for s in range(2)]
        b_names = ["b_fm", "b_gi", "b_d", "b_ne", "b_q", "b_e", "b_eu", "b_pr", "b_bn", "b_arg", "b_wx", "b_sw",
                   "b_acc", "b_tl", "b_bc", "b_cb", "b_tot", "b_rl", "b_a", "b_at", "b_atc", "b_h",
                   "b_th", "b_out", "b_oi", "b_mv", "b_ve", "b_rs", "b_nr", "b_xp"]
        (b_fm, b_gi, b_d, b_ne, b_q, b_e, b_eu, b_pr, b_bn, b_arg, b_wx, b_sw, b_acc, b_tl, b_bc, b_cb,
         b_tot, b_rl, b_a, b_at, b_atc, b_h, b_th, b_out, b_oi, b_mv, b_ve, b_rs, b_nr, b_xp) = [sem(n) for n in b_names]
        s_zero = sem("s_zero")
        s_eps = sem("s_eps")
        b_v = sem("b_v")
        b_per = [7, 7, 10]
        b_base = [0, R * b_per[0], 2 * R * b_per[0]]
        d_ix = sem("d_ix")
        d_c = sem("d_c")
        e_a = sem("e_a")

        dG = bO
        dS = bNE
        dO = sb("dO", [P, U, C + EA])
        dK = sb("dK", [P, U])
        dGI = sb("dGI", [P, U], I32)
        dOI = sb("dOI", [P, U], I32)
        d_g = sems("d_g", U)
        d_a = sems("d_a", 2)
        d_at, d_k, d_gi, d_oi, d_t, d_s, d_acc, d_o = [
            sem(n) for n in ["d_at", "d_k", "d_gi", "d_oi", "d_t", "d_s", "d_acc", "d_o"]]

        eG = aX[:, 0:2, :, :]
        eY = aX[:, 2:4, :, :]
        eA = bXd_flat[:, 0:4 * J * (C + EA)].rearrange("p (k b j c) -> p k b j c", k=2, b=2, j=J)
        eS = aO[:, 0, :, :, :]
        eE = sb("eE", [P, 2, J, KA])
        eQ = sb("eQ", [P, 2, 2 * J, EA])
        eB = sb("eB", [P, 2, 2 * J, EA], BF16)
        eHT = aS
        eET = sb("eET", [KA, 2, TN], BF16)
        eZ = aT[:, 0, :, :].rearrange("p (k h) n -> p k h n", k=2)
        eO = aH
        e_in = sems("e_in", 2)
        e_et = sems("e_et", 2)
        e_st = sems("e_st", 2)
        e_se = sems("e_se", 2)
        e_yi = sems("e_yi", 2)
        e_q = sem("e_q")
        e_s, e_tp, e_tc, e_z, e_zr, e_y, e_o, e_v = [
            sem(n) for n in ["e_s", "e_tp", "e_tc", "e_z", "e_zr", "e_y", "e_o", "e_v"]]

        def node_tile(t, buf):
            return buf[bass.ds(t * TN, TN), :].rearrange("(p j) c -> p j c", j=J)

        def last_tile(buf):
            return buf[LAST:N, :].rearrange("(p j) c -> p j c", j=J)

        def b_rounds(engine, b_round):
            for i in range(3):
                b_round(i, i % 2, i // 2)
            with engine.Fori(1, R // 2 - 1) as i:
                b_round(2 * i + 1, 1, i)
                b_round(2 * i + 2, 0, i + 1)
            b_round(R - 2, 1, R // 2 - 1)
            b_round(R - 1, 0, R // 2)

        @block.sync
        def _(sp):
            sp.wait_ge(s_pool, 1)
            full = E // P
            for k, (vec, off) in enumerate(((src, 0), (dst, 0), (dst, 1))):
                for b in range(NB_):
                    lo = b * EB
                    n = max(0, min(EB, (E - off) // P - lo))
                    if n:
                        sp.dma_start(rowI[0:n, k, b, :], vec[off + lo * P:off + (lo + n) * P]
                                     .rearrange("(t p) -> t p", p=P)).then_inc(s_idx, 16)
                        n_idx[0] += 1
                    rest = E - off - (lo + n) * P
                    if 0 <= n < EB and 0 < rest < P:
                        sp.dma_start(rowI[n:n + 1, k, b, 0:rest],
                                     vec[off + (lo + n) * P:E].rearrange("(t p) -> t p", t=1)).then_inc(s_idx, 16)
                        n_idx[0] += 1

            def tile_of(t):
                if isinstance(t, int) and (t + 1) * TN > N:
                    return last_tile
                return lambda buf: node_tile(t, buf)

            def stores_before(s, p, k):
                if isinstance(p, int) and 2 * p + k >= N // TN:
                    for kk in range(2):
                        sp.wait_ge(s[kk], 16 * (p + 1 + (kk < k)))

            def h0_out(p):
                for k in range(2):
                    stores_before(a_sh, p, k)
                    sp.wait_ge(a_h, 2 * J * p + J * (k + 1))
                    sp.dma_start(tile_of(2 * p + k)(h0_d), aH[:, k, :, :]).then_inc(a_sh[k], 16)

            def set_stores_before(s, p, q, k):
                if isinstance(p, int) and 2 * p + k >= N // TN:
                    for st in range(2):
                        for kk in range(2):
                            before = (p + 1 - st) // 2 + (st == q and kk < k)
                            sp.wait_ge(s[2 * st + kk], 16 * (before + 1))

            def yg_out(p, q):
                for k in range(2):
                    set_stores_before(a_sy, p, q, k)
                    sp.wait_ge(a_g, 2 * J * p + J * (k + 1))
                    sp.dma_start(tile_of(2 * p + k)(yg_d), aYG[:, 2 * q + k, :, :]).then_inc(a_sy[2 * q + k], 16)

            def a_pair(p, q, n, first, last):
                if not first and not last:
                    for k in range(2):
                        sp.wait_ge(a_y, 2 * (p - 1) + k + 1)
                        sp.wait_ge(a_xc[2 * (1 - q) + k], 16 * (n + q + 1))
                        sp.dma_start(aX[:, 2 * (1 - q) + k, :, :], tile_of(2 * p + 2 + k)(x)).then_inc(a_x[2 * (1 - q) + k], 16)
                for k in range(2):
                    sp.wait_ge(a_x[2 * q + k], 16 * (n + 1))
                    set_stores_before(a_xc, p, q, k)
                    sp.dma_start(tile_of(2 * p + k)(xx2_d[:, 0:C]), aX[:, 2 * q + k, :, :]).then_inc(a_xc[2 * q + k], 16)
                for m, (o, s) in enumerate(((x1_d, a_s1), (xx2_d[:, C:2 * C], a_s2))):
                    for k in range(2):
                        stores_before(s, p, k)
                        sp.wait_ge(a_o, 4 * p + 2 * m + k + 1)
                        sp.dma_start(tile_of(2 * p + k)(o), aO[:, k, m, :, :]).then_inc(s[k], 16)
                    if m == 0 and not (isinstance(p, int) and p < 2):
                        yg_out(p - 2, q)
                if not last:
                    h0_out(p + 1)

            for t in range(4):
                sp.dma_start(aX[:, t, :, :], node_tile(t, x)).then_inc(a_x[t], 16)
            sp.wait_ge(s_setup, 1)
            for g, q in enumerate(W_PARTS):
                sp.dma_start(EPS[g * EA:(g + 1) * EA, :, :], EPP[:, q, :, :]).then_inc(s_eps, 16)
            h0_out(0)
            a_rounds(sp, a_pair, NA - 4)
            yg_out(NA - 2, 0)
            yg_out(NA - 1, 1)

            for m in range(M):
                for b in range(2):
                    agg = agg_d[m][b]
                    n = J * AW[m]
                    sp.wait_ge(b_fm, m * R + 1)
                    with sp.Fori(0, NT + 1) as i:
                        sp.dma_start(agg[bass.ds(i * TN, TN), :].rearrange("(p j) c -> p (j c)", j=J),
                                     zeros[:, 0:n]).then_inc(s_zero, 16)

            def attrs(r, t0):
                for u in range(U):
                    left = E - (t0 + u) * P
                    if left > 0:
                        k = min(P, left)
                        sp.dma_start(dG[0:k, u, C:C + DE], attr[(t0 + u) * P:(t0 + u) * P + k, :]).then_inc(d_at, 16)
                    else:
                        sp.sem_inc(d_at, 16)

            def attr_round(r):
                sp.dma_start(dG[:, :, C:C + DE],
                             attr[bass.ds(r * (U * P), U * P), :].rearrange("(u p) c -> p u c", p=P)
                             ).then_inc(d_at, 16 * U)

            sp.wait_ge(s_dclr, 1)
            attr_round(0)
            with sp.Fori(1, R - 1) as i:
                sp.wait_ge(d_acc, U * i)
                attr_round(i)
            sp.wait_ge(d_acc, U * (R - 1))
            sp.wait_ge(d_at, 16 * U * (R - 1))
            attrs(R - 1, (R - 1) * U)

            for m in range(M):
                n0 = m * NT
                into = [g1_d, g2_d, out][m]

                def load_rows(k, t, m=m):
                    pick = tile_of(t)
                    own = pick(yg_d)[:, :, C:2 * C] if m == 0 else pick([None, g1_d, g2_d][m])
                    sp.dma_start(eG[:, k, :, :], own).then_inc(e_in[k], 16)
                    for b in range(2):
                        sp.dma_start(eA[:, k, b, :, 0:AW[m]], pick(agg_d[m][b])).then_inc(e_in[k], 16)

                def load_ea(k, t):
                    sp.dma_start(eET[:, k, :], eaT_d[bass.ds(t, 1), :, :].rearrange("o r n -> (o r) n")
                                 ).then_inc(e_et[k], 16)

                def load_y(k, t):
                    sp.dma_start(eY[:, k, :, :], tile_of(t)(yg_d)[:, :, 0:C]).then_inc(e_yi[k], 16)

                def e_out(p, more, m=m, n0=n0, into=into):
                    for k in range(2):
                        if isinstance(p, int) and 2 * p + k >= N // TN:
                            for kk in range(2):
                                sp.wait_ge(e_st[kk], 16 * (m * NA + p + 1 + (kk < k)))
                        sp.wait_ge(e_o, n0 + 2 * p + k + 1)
                        sp.dma_start(tile_of(2 * p + k)(into), eO[:, k, :, :]).then_inc(e_st[k], 16)
                        if more and m == M - 1:
                            load_y(k, 2 * p + 2 + k)

                def e_pair(p, first, more, m=m, n0=n0):
                    if more:
                        for k in range(2):
                            sp.wait_ge(e_s, n0 + 2 * p + k + 1)
                            load_rows(k, 2 * p + 2 + k)
                    if m == 0:
                        for k in range(2):
                            sp.wait_ge(e_tc, 4 * p + 2 * (k + 1))
                            sp.dma_start(eaT_d[bass.ds(2 * p + k, 1), :, :].rearrange("o r n -> (o r) n"),
                                         eET[:, k, :]).then_inc(e_se[k], 16)
                    if not first:
                        e_out(p - 1, True)
                    if more and m:
                        for k in range(2):
                            sp.wait_ge(e_z, 2 * (n0 + 2 * p + k + 1))
                            load_ea(k, 2 * p + 2 + k)

                for b in range(2):
                    sp.wait_ge(d_a[b], 16 * (U // 2) * R * (m + 1))
                if m == 0:
                    sp.wait_ge(s_zero, 16 * 2 * M * (NT + 1))
                else:
                    for k in range(2):
                        sp.wait_ge(e_st[k], 16 * (NA * m + 1))
                        sp.wait_ge(e_se[k], 16 * (NA + 1))
                for k in range(2):
                    load_rows(k, k)
                    if m:
                        load_ea(k, k)
                    if m == M - 1:
                        load_y(k, k)
                e_pair(0, True, True)
                with sp.Fori(1, NA - 3) as i:
                    e_pair(i, False, True)
                for p in range(NA - 3, NA):
                    e_pair(p, False, p < NA - 1)
                e_out(NA - 1, False)
            for k in range(2):
                sp.wait_ge(e_st[k], 16 * (NA * M + 1))

        @block.gpsimd
        def _(pool):
            pool.memset(rowI[:, 0:2, :, :], -1)
            pool.memset(rowI[:, 2, :, :], -2)
            pool.memset(ident[:, :], 0.0)
            pool.memset(last_row[:, :], 0.0)
            pool.memset(later[:, :], 1.0)
            pool.memset(ones_row[:, :], 1.0)
            pool.memset(zeros[:, :], 0.0)
            pool.memset(mhalf[:, :], -0.5)
            pool.memset(self_ea[:, :, :], 0.0)
            pool.memset(bXs[:, :, :, C:CP], 1.0)
            pool.memset(bXd[:, :, :, 2 * C:C + CP], 1.0)
            pool.memset(bCB[:, :, :], 0.0)
            pool.memset(bNC[:, :], 0.0)
            pool.memset(IDX[:, :, :], 0).then_inc(s_pool, 1)
            for s in a_sh + a_s1 + a_s2 + a_xc + a_sy + e_se + e_st:
                pool.sem_inc(s, 16)
            pool.wait_ge(s_pool, 1)
            pool.memset(self_ea[:, :, 0:1], 1.0)
            pool.memset(self_ea[:, :, DE:EA], 1.0)
            pool.affine_select(out=ident[:, :], in_=ident[:, :], compare_op=ALU.not_equal, fill=1.0, base=0,
                               pattern=[[-1, P]], channel_multiplier=1)
            pool.affine_select(out=last_row[:, :], in_=last_row[:, :], compare_op=ALU.not_equal, fill=1.0,
                               base=-(P - 1), pattern=[[0, P]], channel_multiplier=1)
            pool.affine_select(out=later[:, :], in_=later[:, :], compare_op=ALU.is_gt, fill=0.0, base=0,
                               pattern=[[1, P]], channel_multiplier=-1)
            pool.iota(trash_id[:, :], pattern=[[0, 1]], base=TRASH, channel_multiplier=1,
                      allow_small_or_imprecise_dtypes=True).then_inc(s_pool, 1)

            pool.wait_ge(s_w, 16 * NW)
            pool.tensor_scalar(BNS[:, :, :], BN[:, 3, :, :], EPS_BN, None, ALU.add).then_inc(s_pool, 1)
            pool.wait_ge(s_pool, 3)
            pool.tensor_tensor(BNT[:, :, :], BNS[:, :, :], mhalf[:, 0:2 * M].rearrange("p (m h) -> p m h", h=2),
                               ALU.pow).then_inc(s_pool, 1)

            def a_rstd(n, k, w):
                pool.wait_ge(a_mv, n)
                pool.sem_inc(s_gate, 1)
                pool.tensor_scalar(aVE[:, k, w, :], aMV[:, k, w, :, 1], EPS_LN, None, ALU.add).then_inc(a_pv, 1)
                pool.wait_ge(a_pv, n)
                pool.tensor_tensor(aRS[:, k, w, :], aVE[:, k, w, :], mhalf[:, 0:J], ALU.pow).then_inc(a_rs, 1)

            def a_pair(p, q, n, first, last):
                c = 2 if first else 4 * p
                if not last:
                    for k in range(2):
                        a_rstd(c + k + 1, k, 0)
                if not first:
                    for k in range(2):
                        a_rstd(c + 2 * (not last) + k + 1, k, 2 - q)

            for k in range(2):
                a_rstd(k + 1, k, 0)
            a_rounds(pool, a_pair, NA - 2)
            for k in range(2):
                a_rstd(4 * (NA - 1) + 2 + k + 1, k, 2)

            n_last = pool.to_reg(N - 1)
            lim2 = pool.to_reg(2 * N - 1)
            for s in a_sh + a_s1 + a_s2:
                pool.wait_ge(s, 16 * (NA + 1))
            for s in a_xc + a_sy:
                pool.wait_ge(s, 16 * (NA // 2 + 1))
            for m in range(M):
                r0 = m * R

                def b_rows(to, of, index, limit, signal):
                    pool.indirect_dma_start(to, None, of, bass.IndirectOffsetOnAxis(ap=index, axis=0),
                                            bounds_check=limit, oob_is_err=False).then_inc(signal, 16)

                def b_gather(i, s, m=m):
                    if not isinstance(i, int) or i > 1:
                        pool.wait_ge(b_rl, 2 * (m * R + i - 2) + 2)
                        if m < M - 1:
                            pool.wait_ge(b_xp, m * R + i - 1)
                    pool.wait_ge(b_gi, m * (R + 2) + i + 1)
                    pool.sem_inc(s_gate, 1)
                    two = m == M - 1
                    for u in range(U):
                        b_rows(bXs[:, s, u, 0:C], gat_src[m], bGI[:, s, two, u:u + 1], lim2 if two else n_last, b_g[s][u])
                        b_rows(bXd[:, s, u, (0 if two else C):2 * C], gat_dst[m], bGI[:, s, 1 - two, u:u + 1], n_last,
                               b_g[s][u])

                def b_deviations(i):
                    pool.wait_ge(b_mv, U * (i + 1) + i + 1)
                    pool.sem_inc(s_gate, 1)
                    pool.tensor_scalar(bRS[:, 0, :], bMV[:, :, 1], EPS_LN, None, ALU.add).then_inc(b_ve, 1)
                    pool.wait_ge(b_ve, i + 1)
                    pool.tensor_tensor(bRS[:, 1, :], bRS[:, 0, :], mhalf[:, 0:U], ALU.pow).then_inc(b_rs, 1)
                    pool.wait_ge(b_rs, i + 1)
                    pool.tensor_tensor(bNR[:, :], bRS[:, 1, :], bNG[:, :], ALU.mult).then_inc(b_nr, 1)

                def b_scatter(i, s, m=m):
                    r = m * R + i
                    pool.wait_ge(b_oi, r + 1)
                    for u in range(U):
                        pool.wait_ge(b_out, U * r + u + 1)
                        pool.sem_inc(s_gate, 1)
                        wid = 2 * C if m == M - 1 else C
                        pool.indirect_dma_start(gat_out[m], bass.IndirectOffsetOnAxis(ap=bOI[:, s, u:u + 1], axis=0),
                                                bOs[s][:, u, 0:wid], None, bounds_check=lim2 if m == 1 else n_last,
                                                oob_is_err=False).then_inc(b_sc[s][u], 16)

                def b_step(i, s, m=m):
                    if m == M - 1:
                        b_deviations(i)
                    if not isinstance(i, int) or i < R - 2:
                        b_gather(i + 2, s)
                    b_scatter(i, s)

                b_gather(0, 0)
                b_gather(1, 1)
                b_rounds(pool, lambda i, s, n: b_step(i, s))
                for s in range(2):
                    for u in range(U):
                        pool.wait_ge(b_sc[s][u], 16 * (m + 1) * RS[s])

            agg_last = pool.to_reg(NR - 1)
            pool.wait_ge(s_zero, 16 * 2 * M * (NT + 1))
            for m in range(M):
                r0 = m * R
                if m:
                    for k in range(2):
                        pool.wait_ge(e_st[k], 16 * (NA * m + 1))

                def d_gather(r, u, m=m):
                    if not isinstance(r, int) or r > 0:
                        pool.wait_ge(d_acc, U * (r - 1) + u + 1)
                    pool.wait_ge(d_gi, r + m + 1)
                    pool.sem_inc(s_gate, 1)
                    pool.indirect_dma_start(dG[:, u, 0:C], None, gin_in[m],
                                            bass.IndirectOffsetOnAxis(ap=dGI[:, u:u + 1], axis=0),
                                            bounds_check=lim2 if m == 0 else n_last,
                                            oob_is_err=False).then_inc(d_g[u], 16)

                def d_add(r, u, m=m):
                    pool.wait_ge(d_oi, r + 1)
                    pool.wait_ge(d_o, U * r + u + 1)
                    if not isinstance(r, int) or U * r + u >= 2:
                        pool.wait_ge(d_a[u % 2], 16 * ((U // 2) * r + u // 2))
                    pool.sem_inc(s_gate, 1)
                    pool.indirect_dma_start(agg_d[m][u % 2],
                                            bass.IndirectOffsetOnAxis(ap=dOI[:, u:u + 1], axis=0),
                                            dO[:, u, 0:AW[m]], None, bounds_check=agg_last,
                                            oob_is_err=True, compute_op=ALU.add).then_inc(d_a[u % 2], 16)

                LAG = 3

                def d_step(r):
                    for u in range(U + LAG):
                        if u < U:
                            d_gather(r, u)
                        if u >= LAG:
                            d_add(r - 1, u - LAG)

                for u in range(U):
                    d_gather(r0, u)
                if m == 0:
                    d_step(1)
                with pool.Fori(2 if m == 0 else 1, R) as i:
                    d_step(r0 + i)
                for u in range(U):
                    d_add(r0 + R - 1, u)

        @block.scalar
        def _(act):
            with nc.allow_non_contiguous_dma(reason="a few short vectors as columns"):
                for to, of in weight_loads:
                    act.dma_start(to, of).then_inc(s_w, 16)

            act.wait_ge(s_setup, 1)
            def normed(p, q, c):
                for k in range(2):
                    act.wait_ge(a_nm, c + k + 1)
                    act.wait_ge(a_sh[k], 16 * (p + 1))
                    for j in range(J):
                        act.activation(aH[:, k, j, :], aX[:, 2 * q + k, j, :], ACT.Relu, bias=aNM[:, k, 0, j:j + 1],
                                       scale=aRS[:, k, 0, j:j + 1]).then_inc(a_h, 1)

            def by_channel(p):
                for k in range(2):
                    act.wait_ge(a_tp, 2 * p + k + 1)
                    act.copy(aT[:, k, 0, :], ps[k][:, :]).then_inc(a_tc, 1)

            def normed_y(q, c, k):
                act.wait_ge(a_nm, c + k + 1)
                yg = aYG[:, 2 * q + k, :, :]
                for j in range(J):
                    act.activation(yg[:, j, C:2 * C], yg[:, j, 0:C], ACT.Relu,
                                   bias=aNM[:, k, 1 + q, j:j + 1], scale=aRS[:, k, 1 + q, j:j + 1]).then_inc(a_g, 1)

            def a_pair(p, q, n, first, last):
                c = 2 if first else 4 * p
                for m in range(M):
                    for k in range(2):
                        act.wait_ge(a_mm, 2 * M * p + 2 * m + k + 1)
                        act.activation(aS[:, k, :], ps[2 + k][:, :], ACT.Sigmoid,
                                       bias=GBC[:, m:m + 1]).then_inc(a_sg, 1)
                        if m:
                            act.wait_ge(a_bk, 2 * M * p + 2 * (m - 1) + k + 1)
                            act.wait_ge([a_s1, a_s2][m - 1][k], 16 * (p + 1))
                            act.copy(aO[:, k, m - 1, :, :], ps[4 + k][:, :].rearrange("p (j c) -> p j c", j=J)
                                     ).then_inc(a_o, 1)
                    if m < 2 and not (isinstance(p, int) and p < 2):
                        normed_y(q, 4 * p - 2, m)
                if not last:
                    normed(p + 1, 1 - q, c)
                    by_channel(p + 1)

            normed(0, 0, 0)
            by_channel(0)
            a_rounds(act, a_pair, NA - 2)
            for k in range(4):
                normed_y(k // 2, 4 * (NA - 1) + 2 * (k // 2), k % 2)

            for m in range(M):
                def b_round(i, s, n, m=m):
                    r = m * R + i
                    act.wait_ge(b_arg, r + 1)
                    act.activation(bW4[:, :, :], bARG[:, :, :], ACT.Exp).then_inc(b_wx, 1)
                    for h in range(2):
                        ins = act.activation(bXP[:, 4 * h:4 * h + 4, :], bXd[:, s, 4 * h:4 * h + 4, C:2 * C], ACT.Copy,
                                             bias=0.5)
                    ins.then_inc(b_xp, 1)
                    for h in range(2):
                        act.wait_ge(b_rl, 2 * r + h + 1)
                        for u in range(4 * h, 4 * h + 4):
                            act.activation(bA[:, u, :], bTOT[:, u, 0:C], ACT.Copy,
                                           scale=bRL[:, 1, u:u + 1]).then_inc(b_a, 1)
                        act.wait_ge(b_at, 2 * r + h + 1)
                        act.copy(bAT[:, 4 * h:4 * h + 4, :], ps[h][:, :].rearrange("p (u c) -> p u c", u=4)
                                 ).then_inc(b_atc, 1)
                    for h in range(2):
                        act.wait_ge(b_h, 2 * r + h + 1)
                        act.activation(bTH[:, 4 * h:4 * h + 4, :], ps[6 - 2 * h][:, :].rearrange("p (u c) -> p u c", u=4),
                                       ACT.Tanh, scale=0.5).then_inc(b_th, 1)
                    if m == M - 1:
                        act.wait_ge(b_nr, i + 1)
                        for u in range(U):
                            act.activation(bOs[s][:, u, C:2 * C], bOs[s][:, u, 0:C], ACT.Relu, bias=bNR[:, u:u + 1],
                                           scale=bRS[:, 1, u:u + 1]).then_inc(b_out, 1)

                b_rounds(act, b_round)

            for m in range(M):
                def d_round(r, m=m):
                    for u in range(U):
                        act.wait_ge(d_acc, U * r + u + 1)
                        if not isinstance(r, int) or r > 0:
                            act.wait_ge(d_a[u % 2], 16 * ((U // 2) * (r - 1) + u // 2 + 1))
                        act.copy(dO[:, u, 0:AW[m]], ps[2 + u % 4][:, 0:AW[m]]).then_inc(d_o, 1)

                if m == 0:
                    d_round(0)
                with act.Fori(1 if m == 0 else 0, R) as i:
                    d_round(m * R + i)

                n0 = m * NT

                def turned(p, m=m, n0=n0):
                    for k in range(2):
                        act.wait_ge(e_tp, n0 + 2 * p + k + 1)
                        if m == 0:
                            act.wait_ge(e_se[k], 16 * (p + 1))
                            act.copy(eET[:, k, :], ps[6 + k][0:KA, :]).then_inc(e_tc, 1)
                        act.copy(eHT[:, k, :], ps[k][:, :]).then_inc(e_tc, 1)

                def e_pair(p, more, m=m, n0=n0):
                    for k in range(2):
                        for h in range(2):
                            act.wait_ge(e_z, 2 * (n0 + 2 * p + k) + h + 1)
                            act.activation(eZ[:, k, h, :], ps[2 + 2 * k + h][:, :], ACT.Relu,
                                           bias=BNT[:, m, h:h + 1], scale=BNS[:, m, h:h + 1]).then_inc(e_zr, 1)
                    if more:
                        turned(p + 1)
                    if m < M - 1:
                        for k in range(2):
                            act.wait_ge(e_v, n0 + 2 * p + k + 1)
                            act.activation(eO[:, k, :, :], eO[:, k, :, :], ACT.Relu).then_inc(e_o, 1)

                turned(0)
                with act.Fori(0, NA - 1) as i:
                    e_pair(i, True)
                e_pair(NA - 1, False)

        @block.tensor
        def _(pe):
            def cols(b, u):
                return ps[b][:, u * P:(u + 1) * P]

            pe.wait_ge(s_pool, 2)
            pe.wait_ge(s_rowf, 1)
            for k in range(3):
                for b in range(NB_):
                    mm = pe.transpose(ps[k][:, b * EB:(b + 1) * EB], rowF[:, k, b, :], ident[0:EB, 0:EB])
                mm.then_inc(s_pe, 1)
            pe.wait_ge(s_keys, 1)
            pe.matmul(ps[3][:, 0:ET], last_row[:, :], keys[:, 1, :], start=True, stop=True).then_inc(s_pe, 1)
            pe.wait_ge(s_meta, 1)
            pe.matmul(ps[2][:, 0:ET], last_row[:, :], META[:, 2, :], start=True, stop=True).then_inc(s_pe, 1)
            pe.wait_ge(s_w, 16 * NW)
            for m in range(M):
                mm = pe.transpose(ps[4][:, m * EA:(m + 1) * EA], ENC[:, m, :], ident[0:EA, 0:EA])
            mm.then_inc(s_pe, 1)
            pe.wait_ge(s_enct, 1)
            for m in range(M):
                mm = pe.matmul(ps[5 + m][0:EA, 0:H], ENCT[:, m, :], W1B[:, m, :], start=True, stop=True)
            mm.then_inc(s_pe, 1)
            pe.wait_ge(s_vc, 1)
            for q in range(2 * M):
                mm = pe.transpose(ps[q // 4][:, (q % 4) * P:(q % 4 + 1) * P], VC[:, q:q + 1].to_broadcast([P, P]),
                                  ident[:, :])
            mm.then_inc(s_pe, 1)
            pe.wait_ge(s_setup, 1)
            def a_turn(p):
                for k in range(2):
                    pe.wait_ge(a_h, J * (2 * p + k + 1))
                    for j in range(J):
                        mm = pe.transpose(ps[k][:, j * P:(j + 1) * P], aH[:, k, j, :], ident[:, :])
                    mm.then_inc(a_tp, 1)

            def a_mul(p, m, k):
                if m == 0:
                    pe.wait_ge(a_tc, 2 * p + k + 1)
                else:
                    pe.wait_ge(a_xT, 2 * M * p + 2 * (m - 1) + k + 1)
                pe.matmul(ps[2 + k][:, :], W[:, m, :], aT[:, k, m, :], start=True, stop=True).then_inc(a_mm, 1)

            def a_back(p, m, k):
                pe.wait_ge(a_xT, 2 * M * p + 2 * m + k + 1)
                if m:
                    pe.wait_ge(a_o, 4 * p + 2 * (m - 1) + k + 1)
                for j in range(J):
                    mm = pe.transpose(ps[4 + k][:, j * P:(j + 1) * P], aT[:, k, m + 1, j * P:(j + 1) * P], ident[:, :])
                mm.then_inc(a_bk, 1)

            def a_pair(p, q, n, first, last):
                for k in range(2):
                    a_mul(p, 0, k)
                for m in range(M):
                    for k in range(2):
                        if m < M - 1:
                            a_mul(p, m + 1, k)
                        a_back(p, m, k)
                if not last:
                    a_turn(p + 1)

            a_turn(0)
            a_rounds(pe, a_pair, NA - 2)

            bc_bank = [ps[7], ps[2], ps[3]]

            def b_keys(r):
                pe.wait_ge(b_fm, r + 1)
                for u in range(U):
                    pe.transpose(cols(2 + u // 4, u % 4), bFM[:, 0, u:u + 1].to_broadcast([P, P]), ident[:, :]
                                 ).then_inc(b_d, 1)

            for m in range(M):
                def b_round(i, s, n, m=m):
                    r = m * R + i
                    pe.wait_ge(b_q, r + 1)
                    for u in range(U):
                        pe.transpose(cols(u // 4, u % 4), bSB[:, 0, u:u + 1].to_broadcast([P, P]), ident[:, :]
                                     ).then_inc(b_e, 1)
                    pe.wait_ge(b_pr, r + 1)
                    pe.matmul(ps[7][:, 0:U], last_row[:, :], bPR[:, :], start=True, stop=True).then_inc(b_bn, 1)

                    def spread(u):
                        pe.wait_ge(b_tl, U * r + u + 1)
                        if u >= 3:
                            pe.wait_ge(b_cb, U * r + u - 2)
                        pe.matmul(bc_bank[u % 3][:, 0:C + 1], last_row[:, :], bTL[:, u, 0:C + 1],
                                  start=True, stop=True).then_inc(b_bc, 1)

                    for u in range(U):
                        pe.wait_ge(b_sw, U * r + u + 1)
                        if u >= 3:
                            pe.wait_ge(b_tl, U * r + u - 2)
                        pe.matmul(ps[4 + u % 3][:, 0:C + 1], bSW[:, u, :], bXs[:, s, u, 0:C + 1],
                                  start=True, stop=True).then_inc(b_acc, 1)
                        if u >= 3:
                            spread(u - 3)
                    for u in range(U - 3, U):
                        spread(u)
                        if u > U - 3:
                            pe.wait_ge(b_tl, U * r + u)
                            pe.matmul(ps[6 - 2 * (u - U + 2)][:, :], ones_row[:, :],
                                      GBR[:, m, :].unsqueeze(1).to_broadcast([1, 4, C]), start=True, stop=False)
                    for h in range(2):
                        for u in range(4 * h, 4 * h + 4):
                            pe.wait_ge(b_a, U * r + u + 1)
                            mm = pe.transpose(cols(h, u % 4), bA[:, u, :], ident[:, :])
                        mm.then_inc(b_at, 1)
                        if h == 0 and not (isinstance(i, int) and i == R - 1):
                            b_keys(r + 1)
                        pe.wait_ge(b_atc, 2 * r + h + 1)
                        for u in range(4 * h, 4 * h + 4):
                            to = cols(6 - 2 * h, u % 4)
                            mm = pe.matmul(to, bAT[:, u, :], W[:, m, :], start=False, stop=u % 4 == 3)
                        mm.then_inc(b_h, 1)

                b_keys(m * R)
                b_rounds(pe, b_round)

            for m in range(M):
                def d_round(i, m=m):
                    r = m * R + i
                    pe.wait_ge(d_k, r + 1)
                    for u in range(U):
                        pe.transpose(cols(u // 4, u % 4), dK[:, u:u + 1].to_broadcast([P, P]), ident[:, :]
                                     ).then_inc(d_t, 1)
                    for u in range(U):
                        pe.wait_ge(d_g[u], 16 * (r + 1))
                        if m == 0 and u == 0:
                            pe.wait_ge(d_at, 16 * U * (i + 1))
                        pe.wait_ge(d_s, U * r + u + 1)
                        if not isinstance(r, int) or U * r + u >= 4:
                            pe.wait_ge(d_o, U * r + u - 3)
                        pe.matmul(ps[2 + u % 4][:, 0:AW[m]], dS[:, u, :], dG[:, u, 0:AW[m]], start=True, stop=True
                                  ).then_inc(d_acc, 1)

                if m == 0:
                    d_round(0)
                with pe.Fori(1 if m == 0 else 0, R) as i:
                    d_round(i)
                n0 = m * NT
                tc = 2 if m == 0 else 1
                tc0 = 0 if m == 0 else NT

                def turn(p, m=m, n0=n0):
                    for k in range(2):
                        pe.wait_ge(e_s, n0 + 2 * p + k + 1)
                        if m == 0:
                            for j in range(J):
                                pe.transpose(ps[6 + k][0:KA, j * P:(j + 1) * P], eE[:, k, j, :], ident[:, :])
                        for j in range(J):
                            mm = pe.transpose(ps[k][:, j * P:(j + 1) * P], eS[:, k, j, :], ident[:, :])
                        mm.then_inc(e_tp, 1)

                def e_pair(p, more, m=m, n0=n0, tc=tc, tc0=tc0):
                    for k in range(2):
                        pe.wait_ge(e_tc, tc0 + tc * (n0 + 2 * p + k + 1))
                        if m:
                            pe.wait_ge(e_et[k], 16 * ((m - 1) * NA + p + 1))
                        for h in range(2):
                            z = ps[2 + 2 * k + h][:, :]
                            pe.matmul(z, W1X[:, m, h * P:(h + 1) * P], eHT[:, k, :], start=True, stop=False)
                            pe.matmul(z, EPS[:, m, h * P:(h + 1) * P], eET[:, k, :], start=False, stop=True
                                      ).then_inc(e_z, 1)
                    if more:
                        turn(p + 1)
                    for k in range(2):
                        pe.wait_ge(e_zr, 2 * (n0 + 2 * p + k + 1))
                        if not more:
                            pe.wait_ge(e_v, n0 + 2 * p + k - 1)
                        if m == 0 and more:
                            pe.wait_ge(e_tc, 2 * (2 * p + 2 + k + 1))
                        for j in range(J):
                            for h in range(2):
                                mm = pe.matmul(ps[6 + k][:, j * P:(j + 1) * P], eZ[:, k, h, j * P:(j + 1) * P],
                                               W2[:, m, h, :], start=(h == 0), stop=(h == 1))
                        mm.then_inc(e_y, 1)

                turn(0)
                pe.wait_ge(s_eps, 16 * len(W_PARTS))
                with pe.Fori(0, NA - 1) as i:
                    e_pair(i, 1)
                e_pair(NA - 1, 0)

        @block.vector
        def _(v):
            done = [0]

            def link(ins):
                done[0] += 1
                ins.then_inc(s_v, 1)
                v.wait_ge(s_v, done[0])

            v.wait_ge(s_idx, 16 * n_idx[0])
            v.tensor_copy(rowF[:, :, :, :], rowI[:, :, :, :]).then_inc(s_rowf, 1)
            v.wait_ge(s_pe, 3)
            for k in range(3):
                ins = v.tensor_copy(keys[:, k, :], ps[k][:, 0:ET])
            ins.then_inc(s_keys, 1)
            v.wait_ge(s_keys, 1)
            v.wait_ge(s_pool, 2)
            v.tensor_copy(META[:, 0, :], keys[:, 1, :])
            v.memset(META[:, 1, 0:1], 1.0)
            v.tensor_scalar(IDX[:, 0, 0:ET], keys[:, 0, :], 0.0, None, ALU.max)
            v.tensor_scalar(IDX[:, 1, 0:ET], keys[:, 1, :], 0.0, None, ALU.max)
            v.tensor_scalar(tmp[:, 0, :], keys[:, 1, :], 0.0, 2.0, ALU.max, ALU.mult)
            link(v.tensor_tensor(tmp[:, 1, :], keys[:, 1, :], keys[:, 2, :], ALU.not_equal))
            v.tensor_scalar(IDX[:, 3, 0:ET], tmp[:, 0, :], 1.0, None, ALU.add)
            link(v.scalar_tensor_tensor(out=cnt[:, :], in0=keys[:, 1, :], scalar=0.0, in1=tmp[:, 1, :],
                                        op0=ALU.is_ge, op1=ALU.mult))
            link(v.scalar_tensor_tensor(out=tmp[:, 0, :], in0=keys[:, 1, :], scalar=-float(SKIP), in1=cnt[:, :],
                                        op0=ALU.add, op1=ALU.mult))
            v.tensor_scalar(IDX[:, 4, 0:ET], tmp[:, 0, :], float(SKIP), None, ALU.add)
            link(v.tensor_scalar(tmp[:, 1, :], tmp[:, 0, :], 2.0, float(2 * SKIP + 1), ALU.mult, ALU.add))
            v.tensor_copy(IDX[:, 5, 0:ET], tmp[:, 1, :])
            link(v.tensor_scalar(tmp[:, 0, :], keys[:, 0, :], 0.0, 2.0, ALU.max, ALU.mult))
            link(v.tensor_scalar(IDX[:, 2, 0:ET], tmp[:, 0, :], 1.0, None, ALU.add))
            v.wait_ge(s_pe, 4)
            link(v.tensor_tensor(META[:, 1, 1:ET], keys[:, 1, 1:ET], ps[3][:, 0:ET - 1], ALU.not_equal))
            v.tensor_scalar(META[:, 2, :], META[:, 1, :], BIG, None, ALU.mult).then_inc(s_meta, 1)
            v.wait_ge(s_pe, 5)
            v.tensor_copy(META[:, 3, :], ps[2][:, 0:ET])

            v.wait_ge(s_w, 16 * NW)
            v.wait_ge(s_pe, 6)
            v.tensor_copy(ENCT[:, :, :], ps[4][:, 0:M * EA].rearrange("p (m a) -> p m a", m=M)).then_inc(s_enct, 1)
            for m in range(M):
                for w in range(2):
                    ins = v.tensor_tensor_reduce(bTL[:, 2 * m + w, 0:C], W[:, m, :], AR[:, w, m, :], 1.0, 0.0, ALU.mult, ALU.add,
                                                 VC[:, 2 * m + w:2 * m + w + 1])
            ins.then_inc(s_vc, 1)
            v.wait_ge(s_pe, 7)
            for m in range(M):
                v.tensor_copy(EP[:, m, :], ps[5 + m][0:EA, 0:H])
            v.wait_ge(s_pool, 4)
            link(v.tensor_tensor(BNS[:, :, :], BN[:, 0, :, :], BNT[:, :, :], ALU.mult))
            link(v.tensor_tensor(BN[:, 4, :, :], BN[:, 4, :, :], BN[:, 2, :, :], ALU.subtract))
            link(v.tensor_tensor(BN[:, 4, :, :], BN[:, 4, :, :], BNS[:, :, :], ALU.mult))
            v.tensor_tensor(BNT[:, :, :], BN[:, 4, :, :], BN[:, 1, :, :], ALU.add)
            v.wait_ge(s_pe, 8)
            for b in range(2):
                n = min(4, 2 * M - 4 * b)
                v.tensor_copy(VR[:, 4 * b:4 * b + n, :], ps[b][:, 0:n * P].rearrange("p (q c) -> p q c", q=n))

            for q in range(3):
                link(v.tensor_copy(EPP[:, q, :, :], EP[:, :, :]))
                if q < 2:
                    link(v.tensor_tensor(EP[:, :, :], EP[:, :, :], EPP[:, q, :, :], ALU.subtract))
            v.sem_inc(s_setup, 1)

            def stats(buf, k, w, slot):
                for j in range(J):
                    ins = v.bn_stats(aBS[:, k, w, j, :], buf[:, slot, j, 0:C])
                return ins

            def aggr(k, w):
                for j in range(J):
                    ins = v.bn_aggr(aMV[:, k, w, j, :], aBS[:, k, w, j, :])
                ins.then_inc(a_mv, 1)

            def shift(k, w, n):
                v.wait_ge(a_rs, n)
                v.scalar_tensor_tensor(out=aNM[:, k, w, :], in0=aMV[:, k, w, :, 0], scalar=-1.0, in1=aRS[:, k, w, :],
                                       op0=ALU.mult, op1=ALU.mult).then_inc(a_nm, 1)

            def a_stats(buf, w, q, c, loads=None):
                for k in range(2):
                    if loads is not None:
                        v.wait_ge(a_x[2 * q + k], 16 * (loads + 1))
                    ins = stats(buf, k, w, 2 * q + k)
                ins.then_inc(a_bs, 1)
                v.wait_ge(a_bs, c + 1)
                v.sem_inc(s_gate, 1)
                for k in range(2):
                    aggr(k, w)

            def add(p, m, k):
                v.wait_ge(a_sg, 2 * M * p + 2 * m + k + 1)
                if m:
                    v.wait_ge(a_xT, 2 * M * p + 2 * (m - 1) + k + 1)
                else:
                    v.wait_ge(a_tc, 2 * p + k + 1)
                v.tensor_tensor(aT[:, k, m + 1, :], aT[:, k, m, :], aS[:, k, :], ALU.add).then_inc(a_xT, 1)

            def a_pair(p, q, n, first, last):
                c = 2 if first else 4 * p
                for k in range(2):
                    add(p, 0, k)
                if not last:
                    a_stats(aX, 0, 1 - q, c // 2 if first else 2 * p, n + q)
                for k in range(2):
                    add(p, 1, k)
                if not first:
                    v.wait_ge(a_y, 2 * p)
                    a_stats(aYG, 2 - q, 1 - q, 2 * p + (not last))
                if not last:
                    for k in range(2):
                        shift(k, 0, c + k + 1)
                for k in range(2):
                    add(p, 2, k)
                if not first:
                    for k in range(2):
                        shift(k, 2 - q, c + 2 * (not last) + k + 1)
                for k in range(2):
                    v.wait_ge(a_bk, 2 * M * p + 2 * (M - 1) + k + 1)
                    v.wait_ge(a_sy[2 * q + k], 16 * (n + 1))
                    v.tensor_tensor(aYG[:, 2 * q + k, :, 0:C], ps[4 + k][:, :].rearrange("p (j c) -> p j c", j=J),
                                    aX[:, 2 * q + k, :, :], ALU.add).then_inc(a_y, 1)

            a_stats(aX, 0, 0, 0, 0)
            for k in range(2):
                shift(k, 0, k + 1)
            a_rounds(v, a_pair, NA - 2)
            v.wait_ge(a_y, 2 * NA)
            a_stats(aYG, 2, 1, 2 * (NA - 1) + 1)
            for k in range(2):
                shift(k, 2, 4 * (NA - 1) + 2 + k + 1)

            def steps(s, base, per):
                n = [0]

                def step(ins, wait=True):
                    n[0] += 1
                    ins.then_inc(s, 1)
                    if wait:
                        v.wait_ge(s, base + n[0])
                    return n[0] == per
                return step

            for m in range(M):
                vs, vd = VR[:, 2 * m, :], VR[:, 2 * m + 1, :]

                indices = IDX[:, 1:3, :] if m == M - 1 else IDX[:, 0:2, :]

                def b_begin(i, s, n, m=m, vs=vs, vd=vd, indices=indices):
                    v.tensor_copy(bNC[:, 0:1], bNC[:, U:U + 1])
                    v.tensor_copy(bFM[:, :, :], META[:, :, bass.ds(i * U, U)]).then_inc(b_fm, 1)
                    for u in range(U):
                        v.wait_ge(b_g[s][u], 32 * (m * RS[s] + n + 1))
                        v.tensor_tensor_reduce(bTL[:, u, 0:C], bXs[:, s, u, 0:C], vs, 1.0, 0.0, ALU.mult, ALU.add,
                                               bDT[:, 0, u:u + 1])
                        v.tensor_tensor_reduce(dO[:, u, 0:C], bXd[:, s, u, C:2 * C], vd, 1.0, 0.0, ALU.mult, ALU.add,
                                               bDT[:, 1, u:u + 1])
                        v.tensor_tensor_reduce(bSW[:, u, :], bXd[:, s, u, C:2 * C], vs, 1.0, 0.0, ALU.mult, ALU.add,
                                               bDT[:, 2, u:u + 1])
                    v.tensor_copy(bGI[:, s, :, :], indices[:, :, bass.ds(i * U + 2 * U, U)]).then_inc(b_gi, 1)

                def b_differ(r):
                    for u in range(U):
                        if u % 4 == 0:
                            v.wait_ge(b_d, U * r + u + 4)
                        v.tensor_scalar(bNE[:, u, :], ps[2 + u // 4][:, (u % 4) * P:(u % 4 + 1) * P], bFM[:, 0, u:u + 1], BIG,
                                        ALU.not_equal, ALU.mult).then_inc(b_ne, 1)

                def b_round(i, s, n, m=m, vs=vs, vd=vd):
                    r = m * R + i
                    step = steps(b_v, b_base[m] + i * b_per[m], b_per[m])
                    v.wait_ge(b_ne, U * (r + 1))
                    v.scalar_tensor_tensor(out=bNX[:, 0, :], in0=bDT[:, 0, :], scalar=-1.0, in1=bDT[:, 1, :],
                                           op0=ALU.mult, op1=ALU.subtract)
                    step(v.scalar_tensor_tensor(out=bNX[:, 1, :], in0=bDT[:, 2, :], scalar=-1.0, in1=bDT[:, 1, :],
                                                op0=ALU.mult, op1=ALU.subtract))
                    v.scalar_tensor_tensor(out=bSB[:, 0:2, :], in0=bNX[:, :, :], scalar=SLOPE, in1=bNX[:, :, :],
                                           op0=ALU.mult, op1=ALU.min).then_inc(b_q, 1)
                    for u in range(U):
                        if u % 4 == 0:
                            v.wait_ge(b_e, U * r + u + 4)
                            v.sem_inc(s_gate, 1)
                        v.tensor_tensor_reduce(bTL[:, u, 0:P], bNE[:, u, :], ps[u // 4][:, (u % 4) * P:(u % 4 + 1) * P], 1.0,
                                               BIG, ALU.add, ALU.min, bNM[:, u:u + 1]).then_inc(b_eu, 1)
                    v.wait_ge(b_eu, U * (r + 1))
                    v.tensor_tensor(bPR[:, :], bNM[:, :], bSB[:, 1, :], ALU.min).then_inc(b_pr, 1)
                    v.wait_ge(b_bn, r + 1)
                    step(v.tensor_tensor_scan(out=bNC[:, 1:U + 1], data0=bFM[:, 3, :], data1=ps[7][:, 0:U],
                                              initial=bNC[:, 0:1], op0=ALU.add, op1=ALU.min))
                    step(v.tensor_tensor(bSB[:, 2:4, :], bFM[:, 2:4, :],
                                         bNC[:, 0:U].unsqueeze(1).to_broadcast([P, 2, U]), ALU.add))
                    step(v.tensor_tensor(bMX[:, :], bPR[:, :], bSB[:, 2, :], ALU.min))
                    v.tensor_tensor(bARG[:, 0:3, :], bMX[:, :].unsqueeze(1).to_broadcast([P, 3, U]), bSB[:, 0:3, :],
                                    ALU.subtract)
                    v.tensor_tensor(bARG[:, 3, :], bNC[:, 1:U + 1], bSB[:, 3, :], ALU.subtract).then_inc(b_arg, 1)
                    v.wait_ge(b_wx, r + 1)
                    step(v.tensor_tensor(bWS[:, :], bW4[:, 1, :], bFM[:, 1, :], ALU.mult))

                    def within(u):
                        v.wait_ge(b_acc, U * r + u + 1)
                        v.scalar_tensor_tensor(out=bTL[:, u, 0:C + 1], in0=bXd[:, s, u, C:2 * C + 1], scalar=bWS[:, u:u + 1],
                                               in1=ps[4 + u % 3][:, 0:C + 1], op0=ALU.mult, op1=ALU.add).then_inc(b_tl, 1)

                    def join(u):
                        v.wait_ge(b_bc, U * r + u + 1)
                        v.wait_ge(b_cb, U * r + u)
                        v.scalar_tensor_tensor(out=bTOT[:, u, 0:C + 1], in0=bCB[:, u, 0:C + 1], scalar=bW4[:, 2, u:u + 1],
                                               in1=bTL[:, u, 0:C + 1], op0=ALU.mult, op1=ALU.add).then_inc(b_tot, 1)
                        v.scalar_tensor_tensor(out=bCB[:, (u + 1) % U, 0:C + 1], in0=bCB[:, u, 0:C + 1],
                                               scalar=bW4[:, 3, u:u + 1], in1=[ps[7], ps[2], ps[3]][u % 3][:, 0:C + 1],
                                               op0=ALU.mult, op1=ALU.add).then_inc(b_cb, 1)
                        if u % 4 == 3:
                            v.wait_ge(b_tot, U * r + u + 1)
                            step(v.tensor_scalar(bRL[:, 0, u - 3:u + 1], bTOT[:, u - 3:u + 1, C], EPS_SM, None, ALU.add))
                            v.reciprocal(bRL[:, 1, u - 3:u + 1], bRL[:, 0, u - 3:u + 1]).then_inc(b_rl, 1)

                    for u in range(U + 4):
                        if u < U:
                            v.tensor_scalar(bSW[:, u, :], bNE[:, u, :], 0.0, bW4[:, 0, u:u + 1], ALU.is_equal,
                                            ALU.mult).then_inc(b_sw, 1)
                        if 2 <= u < U + 2:
                            within(u - 2)
                        if u >= 4:
                            join(u - 4)
                    if not (isinstance(i, int) and i == R - 1):
                        b_begin(i + 1, 1 - s, n + s)
                    if not isinstance(n, int) or m * RS[s] + n > 0:
                        for u in range(U):
                            v.wait_ge(b_sc[s][u], 16 * (m * RS[s] + n))
                    v.sem_inc(s_gate, 1)
                    v.tensor_copy(bOI[:, s, :], IDX[:, 5 if m == 1 else 4, bass.ds(i * U, U)]).then_inc(b_oi, 1)
                    for h in range(2):
                        v.wait_ge(b_th, 2 * r + h + 1)
                        ins = v.scalar_tensor_tensor(out=bOs[s][:, 4 * h:4 * h + 4, 0:C], in0=bTH[:, 4 * h:4 * h + 4, :],
                                                     scalar=0.5, in1=bXP[:, 4 * h:4 * h + 4, :], op0=ALU.mult, op1=ALU.add)
                        if m < M - 1:
                            ins.then_inc(b_out, 4)
                        if h == 0 and not (isinstance(i, int) and i == R - 1):
                            b_differ(r + 1)
                    if m < M - 1:
                        v.wait_ge(b_out, U * (r + 1))
                    else:
                        step(ins)
                        step(v.tensor_tensor(bOs[s][:, :, 0:C], bOs[s][:, :, 0:C], bXd[:, s, :, 0:C], ALU.add))
                        for u in range(U):
                            ins = v.bn_stats(bBS[:, u, :], bOs[s][:, u, 0:C])
                        step(ins)
                        v.sem_inc(s_gate, 1)
                        for u in range(U):
                            v.bn_aggr(bMV[:, u, :], bBS[:, u, :]).then_inc(b_mv, 1)
                        v.wait_ge(b_mv, (U + 1) * i + U)
                        v.tensor_scalar(bNG[:, :], bMV[:, :, 0], -1.0, None, ALU.mult).then_inc(b_mv, 1)

                if m:
                    v.wait_ge(b_gi, m * (R + 2))
                for k in range(2):
                    v.tensor_copy(bGI[:, k, :, :], indices[:, :, k * U:(k + 1) * U]).then_inc(b_gi, 1)
                b_begin(0, 0, 0)
                v.wait_ge(b_fm, m * R + 1)
                b_differ(m * R)
                b_rounds(v, b_round)

            for s in range(2):
                for u in range(U):
                    v.wait_ge(b_sc[s][u], 16 * M * RS[s])
            v.wait_ge(b_out, U * M * R)
            v.memset(dG[:, :, C + DE:C + EA], 1.0)
            link(v.memset(dG[:, :, C:C + DE], 0.0))
            v.sem_inc(s_dclr, 1)
            for m in range(M):
                gi = 3 if m == 0 else 1
                v.tensor_copy(dGI[:, :], IDX[:, gi, 0:U]).then_inc(d_gi, 1)

                def d_round(i, m=m, gi=gi):
                    r = m * R + i
                    v.tensor_copy(dK[:, :], keys[:, 0, bass.ds(i * U, U)]).then_inc(d_k, 1)
                    v.wait_ge(d_k, r + 1)
                    for u in range(U):
                        if u % 4 == 0:
                            v.wait_ge(d_t, U * r + u + 4)
                        v.tensor_scalar(dS[:, u, :], ps[u // 4][:, (u % 4) * P:(u % 4 + 1) * P], dK[:, u:u + 1], None,
                                        ALU.is_equal).then_inc(d_s, 1)
                    if m == 0:
                        step = steps(d_c, i * 4, 4)
                        for u in range(U):
                            ins = v.scalar_tensor_tensor(out=bTL[:, u, 0:C], in0=ps[u // 4][:, (u % 4) * P:(u % 4 + 1) * P],
                                                         scalar=dK[:, u:u + 1], in1=later[:, :], op0=ALU.is_equal,
                                                         op1=ALU.mult, accum_out=bNM[:, u:u + 1])
                        step(ins)
                        step(v.tensor_scalar(bPR[:, :], bNM[:, :], 0.0, None, ALU.is_equal))
                        step(v.scalar_tensor_tensor(out=bMX[:, :], in0=dK[:, :], scalar=0.0, in1=bPR[:, :],
                                                    op0=ALU.is_ge, op1=ALU.mult))
                        v.scalar_tensor_tensor(out=bPR[:, :], in0=dK[:, :], scalar=trash_id[:, 0:1],
                                               in1=bMX[:, :], op0=ALU.subtract, op1=ALU.mult).then_inc(d_c, 1)
                        v.wait_ge(d_c, 4 * i + 4)
                        v.tensor_scalar(IDX[:, 6, bass.ds(i * U, U)], bPR[:, :], trash_id[:, 0:1], None, ALU.add
                                        ).then_inc(d_ix, 1)
                        v.wait_ge(d_ix, i + 1)
                    v.wait_ge(d_s, U * (r + 1))
                    for u in range(U):
                        v.wait_ge(d_g[u], 16 * (r + 1))
                    v.sem_inc(s_gate, 1)
                    v.tensor_copy(dGI[:, :], IDX[:, gi, bass.ds(i * U + U, U)]).then_inc(d_gi, 1)
                    if not isinstance(r, int) or r > 0:
                        for b in range(2):
                            v.wait_ge(d_a[b], 16 * (U // 2) * r)
                    v.sem_inc(s_gate, 1)
                    v.tensor_copy(dOI[:, :], IDX[:, 6, bass.ds(i * U, U)]).then_inc(d_oi, 1)

                if m == 0:
                    d_round(0)
                with v.Fori(1 if m == 0 else 0, R) as i:
                    d_round(i)

                n0 = m * NT

                def add_up(p, m=m, n0=n0):
                    for k in range(2):
                        v.wait_ge(e_in[k], 48 * (m * NA + p + 1))
                        v.tensor_tensor(eA[:, k, 0, :, 0:AW[m]], eA[:, k, 0, :, 0:AW[m]], eA[:, k, 1, :, 0:AW[m]],
                                        ALU.add).then_inc(e_a, 1)
                    if m == 0:
                        v.wait_ge(e_a, 2 * p + 2)
                        if not isinstance(p, int):
                            v.wait_ge(e_tp, 2 * p)
                        step = steps(e_q, 7 * p, 7)
                        halves = eE[:, :, :, :].rearrange("p k j c -> p (k j) c")

                        def parts(q):
                            lo, n = A_PARTS.index(q), A_PARTS.count(q)
                            return halves[:, :, lo * EA:(lo + n) * EA].rearrange("p j (g a) -> p j g a", g=n)

                        for k in range(2):
                            ins = v.tensor_tensor(eQ[:, 0, k * J:(k + 1) * J, :], eA[:, k, 0, :, C:C + EA],
                                                  self_ea[:, :, :], ALU.add)
                        step(ins)
                        for q in range(2):
                            step(v.tensor_copy(eB[:, q, :, :], eQ[:, q, :, :]))
                            step(v.tensor_tensor(parts(2)[:, :, 0, :] if q else eQ[:, 1, :, :], eQ[:, q, :, :],
                                                 eB[:, q, :, :], ALU.subtract))
                            step(v.tensor_copy(parts(q), eB[:, q, :, :].unsqueeze(2).to_broadcast(
                                [P, 2 * J, A_PARTS.count(q), EA])))
                    for k in range(2):
                        v.wait_ge(e_a, n0 + 2 * p + k + 1)
                        if not isinstance(p, int):
                            v.wait_ge(e_tp, n0 + 2 * p + k - 1)
                        v.tensor_tensor(eS[:, k, :, :], eA[:, k, 0, :, 0:C], eG[:, k, :, :], ALU.add
                                        ).then_inc(e_s, 1)

                def finish(p, m=m, n0=n0):
                    bias = B2[:, m, :].unsqueeze(1).to_broadcast([P, J, C])
                    for k in range(2):
                        v.wait_ge(e_y, n0 + 2 * p + k + 1)
                        v.wait_ge(e_st[k], 16 * (m * NA + p + 1))
                        v.tensor_tensor(eO[:, k, :, :], ps[6 + k][:, :].rearrange("p (j c) -> p j c", j=J), bias,
                                        ALU.add).then_inc(e_v, 1)
                    if m == M - 1:
                        for k in range(2):
                            v.wait_ge(e_v, n0 + 2 * p + k + 1)
                            v.wait_ge(e_yi[k], 16 * (p + 1))
                            v.tensor_tensor(eO[:, k, :, :], eO[:, k, :, :], eY[:, k, :, :], ALU.add).then_inc(e_o, 1)

                add_up(0)
                with v.Fori(0, NA - 1) as i:
                    add_up(i + 1)
                    finish(i)
                finish(NA - 1)


_INS = ["x", "src", "dst", "edge_attr_16", "L0_gnn_Ws", "L0_gnn_att_src", "L0_gnn_att_dst", "L0_gnn_bias",
        "L1_gnn_enc_w0", "L1_gnn_enc_b0", "L1_gnn_w1_0", "L1_gnn_b1_0", "L1_gnn_g0", "L1_gnn_be0", "L1_gnn_rm0",
        "L1_gnn_rv0", "L1_gnn_w2_0", "L1_gnn_b2_0", "L1_gnn_enc_w", "L1_gnn_enc_b", "L1_gnn_w1", "L1_gnn_b1",
        "L1_gnn_g", "L1_gnn_be", "L1_gnn_rm", "L1_gnn_rv", "L1_gnn_w2", "L1_gnn_b2"]


def kernel(**inputs):
    import numpy as _np
    import concourse.bacc as _bacc
    from concourse import mybir as _mybir
    from concourse.bass_utils import run_bass_kernel_spmd as _run

    nc = _bacc.Bacc("TRN2", target_bir_lowering=False, num_devices=1)
    arrays, args = {}, []
    for name in _INS:
        a = _np.ascontiguousarray(inputs[name])
        arrays[f"in_{name}_dram"] = a
        args.append(nc.dram_tensor(f"in_{name}_dram", a.shape, _mybir.dt.from_np(a.dtype), kind="ExternalInput").ap())
    shape = inputs["x"].shape
    args.append(nc.dram_tensor("out_0_dram", shape, _mybir.dt.float32, kind="ExternalOutput").ap())
    gnn_program(nc, *args)
    r = _run(nc, [arrays], core_ids=[0])
    return r.results[0]["out_0_dram"]
```
